# Optimizing a Trainium2 kernel written in Bass

```python
import numpy as np
import jax
import jax.numpy as jnp

def _softmax(x, axis=-1):
    return jax.nn.softmax(x, axis=axis)

def _gelu(x):
    return jax.nn.gelu(x, approximate=True)

def _silu(x):
    return jax.nn.silu(x)

def _sigmoid(x):
    return jax.nn.sigmoid(x)

def _layernorm(x, axis=-1, eps=1e-05):
    m = jnp.mean(x, axis=axis, keepdims=True)
    v = jnp.var(x, axis=axis, keepdims=True)
    return (x - m) / jnp.sqrt(v + eps)

def _scatter_add(tgt, idx, src, axis=0):
    return tgt.at[idx].add(src)

def _segment_sum(src, seg, n):
    return jax.ops.segment_sum(src, seg, n)
kernel_name = 'mk_adaln_attn_ffn_d1_seqx_r4_5e171e'

def setup_inputs(seed: int=0):
    np.random.seed(seed)
    _w = jnp.asarray

    def _rec_inputs():
        import jax
        import jax.numpy as jnp
        _rk = jax.random.key(seed)
        x = -7.109e-05 + 0.9999 * jax.random.normal(jax.random.fold_in(_rk, 1), (64, 64, 512), jnp.float32)
        _lenS = 64 - jax.random.randint(jax.random.fold_in(_rk, 7), (64,), 0, max(1, 64 // 4) + 1, jnp.int32)
        _lenS2 = 64 - jax.random.randint(jax.random.fold_in(_rk, 8), (64,), 0, max(1, 64 // 4) + 1, jnp.int32)
        itok_B_1_198 = jax.random.randint(jax.random.fold_in(_rk, 11), (64,), 1, 199, jnp.int32)
        itok_Bx257_0_4111 = jax.random.randint(jax.random.fold_in(_rk, 12), (64, 257), 0, 1028, jnp.int32)
        itok_B_37_3939 = jax.random.randint(jax.random.fold_in(_rk, 13), (64,), 37, 985, jnp.int32)
        return (x, itok_B_1_198, itok_Bx257_0_4111, itok_B_37_3939)
    x, itok_B_1_198, itok_Bx257_0_4111, itok_B_37_3939 = _rec_inputs()

    def _L0_cond_setup():
        import jax, jax.numpy as jnp
        import numpy as np
        B, C, T = (128, 64, 512)
        S, D = (200, 64)
        key = jax.random.key(seed)
        k1, k2, k3 = jax.random.split(key, 3)
        x = jax.random.normal(k1, (B, C, T), dtype=jnp.float32)
        conditions = jax.random.randint(k2, (B,), 0, S, dtype=jnp.int64)
        weights = jax.random.normal(k3, (S, C, D), dtype=jnp.float32) / jnp.sqrt(jnp.float32(C))
        return {'x': x, 'conditions': conditions, 'weights': weights}
    _L0_cond_all = _L0_cond_setup()
    _L0_cond_in = {k: v for k, v in _L0_cond_all.items() if k in ('weights',)}
    del _L0_cond_all

    def _L0_attn_setup():
        import jax, jax.numpy as jnp
        import numpy as np
        D_INNER, D_STATE, DT_RANK = (512, 16, 128)
        BATCH, SEQ = (2, 512)

        def _selective_scan(u, delta, A, B, C, D):
            dA = jnp.exp(delta[..., None] * A[None, None])
            dBu = (delta * u)[..., None] * B[:, :, None, :]

            def step(h, inp):
                dA_t, dBu_t, C_t = inp
                h = dA_t * h + dBu_t
                y_t = jnp.einsum('bdn,bn->bd', h, C_t)
                return (h, y_t)
            h0 = jnp.zeros((u.shape[0], u.shape[2], A.shape[1]), dtype=u.dtype)
            xs = (jnp.moveaxis(dA, 1, 0), jnp.moveaxis(dBu, 1, 0), jnp.moveaxis(C, 1, 0))
            _, ys = jax.lax.scan(step, h0, xs)
            y = jnp.moveaxis(ys, 0, 1)
            return y + u * D[None, None, :]
        key = jax.random.key(seed)
        ks = jax.random.split(key, 6)
        x = jax.random.normal(ks[0], (BATCH, SEQ, D_INNER), dtype=jnp.float32)
        A_log = jax.random.uniform(ks[1], (D_INNER, D_STATE), minval=-4.0, maxval=-1.0, dtype=jnp.float32)
        D = jnp.ones((D_INNER,), dtype=jnp.float32)
        x_proj_w = jax.random.normal(ks[2], (DT_RANK + 2 * D_STATE, D_INNER), dtype=jnp.float32) / np.sqrt(D_INNER)
        dt_proj_w = jax.random.normal(ks[3], (D_INNER, DT_RANK), dtype=jnp.float32) / np.sqrt(DT_RANK)
        dt_std = DT_RANK ** (-0.5)
        dt_proj_b = jax.random.uniform(ks[4], (D_INNER,), minval=-dt_std, maxval=dt_std, dtype=jnp.float32)
        return {'x': x, 'A_log': A_log, 'D': D, 'x_proj_w': x_proj_w, 'dt_proj_w': dt_proj_w, 'dt_proj_b': dt_proj_b}
    _L0_attn_all = _L0_attn_setup()
    _L0_attn_in = {k: v for k, v in _L0_attn_all.items() if k in ('A_log', 'D', 'x_proj_w', 'dt_proj_w', 'dt_proj_b')}
    del _L0_attn_all

    def _L0_cond2_setup():
        import jax, jax.numpy as jnp
        import numpy as np
        H, G, HD = (8, 4, 64)
        GSZ = H // G
        BLOCK = 16
        WINDOW = 256
        SCALE = 256.0 ** (-0.5)
        EPS = 1e-06
        THETA = 10000.0
        B, T, D = (16, 4, 512)
        NBLK = 257

        def _rms(x, scale):
            var = jnp.mean(x * x, axis=-1, keepdims=True)
            return x * jax.lax.rsqrt(var + EPS) * (1.0 + scale)

        def _rope(x, pos):
            half = HD // 2
            inv = 1.0 / THETA ** (jnp.arange(half, dtype=jnp.float32) / half)
            ang = pos[:, :, None].astype(jnp.float32) * inv
            cos = jnp.cos(ang)[:, None, :, :]
            sin = jnp.sin(ang)[:, None, :, :]
            x1, x2 = (x[..., :half], x[..., half:])
            return jnp.concatenate([x1 * cos - x2 * sin, x2 * cos + x1 * sin], axis=-1)
        key = jax.random.key(seed)
        ks = jax.random.split(key, 10)
        inv_d = 1.0 / np.sqrt(D)
        return {'x': jax.random.normal(ks[0], (B, T, D), jnp.float32), 'Wq': jax.random.normal(ks[1], (H * HD, D), jnp.float32) * inv_d, 'Wk': jax.random.normal(ks[2], (G * HD, D), jnp.float32) * inv_d, 'Wv': jax.random.normal(ks[3], (G * HD, D), jnp.float32) * inv_d, 'Wo': jax.random.normal(ks[4], (D, H * HD), jnp.float32) * inv_d, 'q_norm_scale': jax.random.normal(ks[5], (HD,), jnp.float32) * 0.02, 'k_norm_scale': jax.random.normal(ks[6], (HD,), jnp.float32) * 0.02, 'k_blocks': jax.random.normal(ks[7], (B * NBLK, G, BLOCK, HD), jnp.float32), 'v_blocks': jax.random.normal(ks[8], (B * NBLK, G, BLOCK, HD), jnp.float32), 'block_tables': jnp.arange(B * NBLK, dtype=jnp.int32).reshape(B, NBLK), 'kv_lens': jax.random.randint(ks[9], (B,), 0, 1024, dtype=jnp.int32)}
    _L0_cond2_all = _L0_cond2_setup()
    _L0_cond2_in = {k: v for k, v in _L0_cond2_all.items() if k in ('Wq', 'Wk', 'Wv', 'Wo', 'q_norm_scale', 'k_norm_scale', 'k_blocks', 'v_blocks')}
    del _L0_cond2_all

    def _L0_ffn_setup():
        import jax, jax.numpy as jnp
        import numpy as np
        B, L, D = (4, 1024, 512)
        DF = 4 * D
        CAPACITY_RATIO = 0.5
        key = jax.random.key(seed)
        ks = jax.random.split(key, 4)
        s = 0.02
        return {'x': jax.random.normal(ks[0], (B, L, D), dtype=jnp.float32), 'w_r': jax.random.normal(ks[1], (D,), dtype=jnp.float32) * s, 'b_r': jnp.zeros((), dtype=jnp.float32), 'w1': jax.random.normal(ks[2], (D, DF), dtype=jnp.float32) * s, 'b1': jnp.zeros((DF,), dtype=jnp.float32), 'w2': jax.random.normal(ks[3], (DF, D), dtype=jnp.float32) * s, 'b2': jnp.zeros((D,), dtype=jnp.float32)}
    _L0_ffn_all = _L0_ffn_setup()
    _L0_ffn_in = {k: v for k, v in _L0_ffn_all.items() if k in ('w_r', 'b_r', 'w1', 'b1', 'w2', 'b2')}
    del _L0_ffn_all
    return {'x': x, 'itok_B_1_198': itok_B_1_198, 'itok_Bx257_0_4111': itok_Bx257_0_4111, 'itok_B_37_3939': itok_B_37_3939, 'L0_cond_weights': _L0_cond_in['weights'], 'L0_attn_A_log': _L0_attn_in['A_log'], 'L0_attn_D': _L0_attn_in['D'], 'L0_attn_x_proj_w': _L0_attn_in['x_proj_w'], 'L0_attn_dt_proj_w': _L0_attn_in['dt_proj_w'], 'L0_attn_dt_proj_b': _L0_attn_in['dt_proj_b'], 'L0_cond2_Wq': _L0_cond2_in['Wq'], 'L0_cond2_Wk': _L0_cond2_in['Wk'], 'L0_cond2_Wv': _L0_cond2_in['Wv'], 'L0_cond2_Wo': _L0_cond2_in['Wo'], 'L0_cond2_q_norm_scale': _L0_cond2_in['q_norm_scale'], 'L0_cond2_k_norm_scale': _L0_cond2_in['k_norm_scale'], 'L0_cond2_k_blocks': _L0_cond2_in['k_blocks'], 'L0_cond2_v_blocks': _L0_cond2_in['v_blocks'], 'L0_ffn_w_r': _L0_ffn_in['w_r'], 'L0_ffn_b_r': _L0_ffn_in['b_r'], 'L0_ffn_w1': _L0_ffn_in['w1'], 'L0_ffn_b1': _L0_ffn_in['b1'], 'L0_ffn_w2': _L0_ffn_in['w2'], 'L0_ffn_b2': _L0_ffn_in['b2']}

def reference(x, itok_B_1_198, itok_Bx257_0_4111, itok_B_37_3939, L0_cond_weights, L0_attn_A_log, L0_attn_D, L0_attn_x_proj_w, L0_attn_dt_proj_w, L0_attn_dt_proj_b, L0_cond2_Wq, L0_cond2_Wk, L0_cond2_Wv, L0_cond2_Wo, L0_cond2_q_norm_scale, L0_cond2_k_norm_scale, L0_cond2_k_blocks, L0_cond2_v_blocks, L0_ffn_w_r, L0_ffn_b_r, L0_ffn_w1, L0_ffn_b1, L0_ffn_w2, L0_ffn_b2):
    import jax
    import jax.numpy as jnp

    def _L0_cond_ref(x, conditions, weights):
        import jax, jax.numpy as jnp
        import numpy as np
        B, C, T = (128, 64, 512)
        S, D = (200, 64)
        w = weights[conditions]
        return jnp.einsum('bct,bcd->bdt', x, w)

    def _L0_attn_ref(x, A_log, D, x_proj_w, dt_proj_w, dt_proj_b):
        import jax, jax.numpy as jnp
        import numpy as np
        D_INNER, D_STATE, DT_RANK = (512, 16, 128)
        BATCH, SEQ = (2, 512)

        def _selective_scan(u, delta, A, B, C, D):
            dA = jnp.exp(delta[..., None] * A[None, None])
            dBu = (delta * u)[..., None] * B[:, :, None, :]

            def step(h, inp):
                dA_t, dBu_t, C_t = inp
                h = dA_t * h + dBu_t
                y_t = jnp.einsum('bdn,bn->bd', h, C_t)
                return (h, y_t)
            h0 = jnp.zeros((u.shape[0], u.shape[2], A.shape[1]), dtype=u.dtype)
            xs = (jnp.moveaxis(dA, 1, 0), jnp.moveaxis(dBu, 1, 0), jnp.moveaxis(C, 1, 0))
            _, ys = jax.lax.scan(step, h0, xs)
            y = jnp.moveaxis(ys, 0, 1)
            return y + u * D[None, None, :]
        x_dbl = jnp.einsum('bld,ed->ble', x, x_proj_w)
        delta_r = x_dbl[..., :DT_RANK]
        B = x_dbl[..., DT_RANK:DT_RANK + D_STATE]
        C = x_dbl[..., DT_RANK + D_STATE:]
        delta = jnp.einsum('blr,dr->bld', delta_r, dt_proj_w) + dt_proj_b
        delta = jax.nn.softplus(delta)
        A = -jnp.exp(A_log)
        return _selective_scan(x, delta, A, B, C, D)

    def _L0_cond2_ref(x, Wq, Wk, Wv, Wo, q_norm_scale, k_norm_scale, k_blocks, v_blocks, block_tables, kv_lens):
        import jax, jax.numpy as jnp
        import numpy as np
        H, G, HD = (8, 4, 64)
        GSZ = H // G
        BLOCK = 16
        WINDOW = 256
        SCALE = 256.0 ** (-0.5)
        EPS = 1e-06
        THETA = 10000.0
        B, T, D = (16, 4, 512)
        NBLK = 257

        def _rms(x, scale):
            var = jnp.mean(x * x, axis=-1, keepdims=True)
            return x * jax.lax.rsqrt(var + EPS) * (1.0 + scale)

        def _rope(x, pos):
            half = HD // 2
            inv = 1.0 / THETA ** (jnp.arange(half, dtype=jnp.float32) / half)
            ang = pos[:, :, None].astype(jnp.float32) * inv
            cos = jnp.cos(ang)[:, None, :, :]
            sin = jnp.sin(ang)[:, None, :, :]
            x1, x2 = (x[..., :half], x[..., half:])
            return jnp.concatenate([x1 * cos - x2 * sin, x2 * cos + x1 * sin], axis=-1)
        Bx, Tx, _ = x.shape
        q = jnp.einsum('btd,od->bto', x, Wq).reshape(Bx, Tx, H, HD).transpose(0, 2, 1, 3)
        k = jnp.einsum('btd,od->bto', x, Wk).reshape(Bx, Tx, G, HD).transpose(0, 2, 1, 3)
        v = jnp.einsum('btd,od->bto', x, Wv).reshape(Bx, Tx, G, HD).transpose(0, 2, 1, 3)
        q = _rms(q, q_norm_scale)
        k = _rms(k, k_norm_scale)
        pos = kv_lens[:, None] + jnp.arange(Tx, dtype=jnp.int32)
        q = _rope(q, pos)
        k = _rope(k, pos)
        slot = pos // BLOCK
        off = pos % BLOCK
        blk = jnp.take_along_axis(block_tables, slot, axis=1)
        k_blocks = k_blocks.at[blk, :, off, :].set(k.transpose(0, 2, 1, 3))
        v_blocks = v_blocks.at[blk, :, off, :].set(v.transpose(0, 2, 1, 3))
        k_all = k_blocks[block_tables].transpose(0, 2, 1, 3, 4).reshape(Bx, G, -1, HD)
        v_all = v_blocks[block_tables].transpose(0, 2, 1, 3, 4).reshape(Bx, G, -1, HD)
        S = k_all.shape[2]
        qg = q.reshape(Bx, G, GSZ, Tx, HD)
        scores = jnp.einsum('bghtd,bgsd->bghts', qg, k_all) * SCALE
        kpos = jnp.arange(S, dtype=jnp.int32)
        allowed = (kpos[None, None, :] <= pos[:, :, None]) & (kpos[None, None, :] > pos[:, :, None] - WINDOW)
        scores = jnp.where(allowed[:, None, None, :, :], scores, -jnp.inf)
        p = jax.nn.softmax(scores, axis=-1)
        o = jnp.einsum('bghts,bgsd->bghtd', p, v_all).reshape(Bx, H, Tx, HD)
        o = o.transpose(0, 2, 1, 3).reshape(Bx, Tx, H * HD)
        return jnp.einsum('bto,do->btd', o, Wo)

    def _L0_ffn_ref(x, w_r, b_r, w1, b1, w2, b2):
        import jax, jax.numpy as jnp
        import numpy as np
        B, L, D = (4, 1024, 512)
        DF = 4 * D
        CAPACITY_RATIO = 0.5
        b, l, d = x.shape
        k = int(l * CAPACITY_RATIO)
        scores = jnp.einsum('bld,d->bl', x, w_r) + b_r
        _, idx = jax.lax.top_k(scores, k)
        x_sel = jnp.take_along_axis(x, idx[:, :, None], axis=1)
        h = jax.nn.gelu(jnp.einsum('bkd,df->bkf', x_sel, w1) + b1)
        out_sel = jnp.einsum('bkf,fd->bkd', h, w2) + b2
        batch_ix = jnp.arange(b)[:, None]
        out = jnp.zeros_like(x).at[batch_ix, idx].set(out_sel)
        return out
    x = x + _L0_attn_ref(_L0_cond_ref(x, itok_B_1_198, L0_cond_weights), L0_attn_A_log, L0_attn_D, L0_attn_x_proj_w, L0_attn_dt_proj_w, L0_attn_dt_proj_b)
    x = x + _L0_ffn_ref(_L0_cond2_ref(x, L0_cond2_Wq, L0_cond2_Wk, L0_cond2_Wv, L0_cond2_Wo, L0_cond2_q_norm_scale, L0_cond2_k_norm_scale, L0_cond2_k_blocks, L0_cond2_v_blocks, itok_Bx257_0_4111, itok_B_37_3939), L0_ffn_w_r, L0_ffn_b_r, L0_ffn_w1, L0_ffn_b1, L0_ffn_w2, L0_ffn_b2)
    return x

_drawn_inputs = setup_inputs


def setup_inputs(seed=0):
    import zlib

    import numpy as np

    out = dict(_drawn_inputs(seed))
    spreads = {'L0_attn_D': (1.0, 0.6), 'L0_ffn_b1': (0.0, 2.0), 'L0_ffn_b2': (0.0, 2.0)}
    factors = {'L0_attn_dt_proj_b': 2.828,
     'L0_cond2_Wq': 8.0,
     'L0_cond2_Wk': 8.0,
     'L0_cond2_Wv': 7.085,
     'L0_cond2_Wo': 7.017,
     'L0_cond2_q_norm_scale': 8.0,
     'L0_cond2_k_norm_scale': 22.923,
     'L0_cond2_k_blocks': 8.0,
     'L0_cond2_v_blocks': 8.0,
     'L0_ffn_w_r': 8.0,
     'L0_ffn_w1': 8.0,
     'L0_ffn_w2': 7.576}
    for name, (base, spread) in spreads.items():
        noise = np.random.default_rng([zlib.crc32(name.encode()), seed]).standard_normal(out[name].shape)
        drawn = base * np.exp(spread * noise) if base else spread * noise
        out[name] = jnp.asarray(drawn.astype(out[name].dtype))
    for name, factor in factors.items():
        out[name] = (out[name] * factor).astype(out[name].dtype)
    return out
```

```python
from contextlib import ExitStack

import numpy as np

import concourse.bass as bass
from concourse import mybir

F32 = mybir.dt.float32
I32 = mybir.dt.int32
ALU = mybir.AluOpType
ACT = mybir.ActivationFunctionType
AX = mybir.AxisListType

P = 128
B, T, D = 64, 64, 512
NTOK = B * T
NCH = D // P
NST = 16
TILE = 512
NT = NTOK // TILE
BT = TILE // T
GRP = 128
NG = NTOK // GRP
H, G, HD = 8, 4, 64
HALF = HD // 2
BLOCK, WINDOW, NBLK = 16, 256, 257
NROW = B // 4 * NBLK * BLOCK
KV = 2 * G * HD
SCALE = 256.0 ** -0.5
EPS = 1e-6
NSLOT = 21
SC = 7
KC = SC * BLOCK
NKC = NSLOT // SC
NKEY = NSLOT * BLOCK
NWS = 6
NWC = NWS // 2
SEL = T // 2
DF = 4 * D
NF = DF // P
NEG = -1.0e30
FAR = 1.0e6
MAGIC = 12582912.0
TWO_PI = (6.28125, 1.9340515136718750e-03, 1.2556659146e-06)


def wait(eng, sem, value, mark=None):
    if isinstance(value, int) and value <= 0:
        return
    eng.wait_ge(sem, value)
    if mark and not isinstance(value, int):
        eng.sem_inc(mark, 1)


def scan_block(nc, A, S):
    with ExitStack() as ctx:
        def sb(name, shape, dt=F32):
            return ctx.enter_context(nc.sbuf_tensor(name, shape, dt))

        def sem(name):
            return ctx.enter_context(nc.semaphore(name))

        psum = ctx.enter_context(nc.psum_tensor("scan_psum", [P, 8, 512], F32))
        decay = [psum[:, i, :] for i in range(2)]
        du = psum[:, 2, :]
        y = [psum[:, 3 + i, :] for i in range(2)]
        pro = psum[:, 5, :]
        qk = [psum[:, 6 + i, :] for i in range(2)]

        ident = sb("ident", [P, P])
        neg_a = sb("neg_a", [P, NCH * NST])
        a_log = sb("a_log", [P, NCH * NST])
        skip_d = sb("skip_d", [P, NCH])
        dt_bias = sb("dt_bias", [P, NCH])
        w_x = sb("w_x", [P, NCH, 160])
        w_dt = sb("w_dt", [P, D])
        w_qkv = sb("w_qkv", [P, NCH, 1024])
        bc = sb("bc", [P, NST, 2, TILE])
        u_in = [sb(f"u_in{i}", [P, TILE]) for i in range(2)]
        dl_in = [sb(f"dl_in{i}", [P, TILE]) for i in range(2)]
        xt_in = [sb(f"xt_in{i}", [P, TILE]) for i in range(2)]
        resid = [sb(f"resid{i}", [P, TILE]) for i in range(2)]
        x1_out = [sb(f"x1_out{i}", [P, TILE]) for i in range(2)]
        dbu = [sb(f"dbu{i}", [P, TILE]) for i in range(4)]
        hid = [sb(f"hid{i}", [P, TILE]) for i in range(4)]
        hc = [sb(f"hc{i}", [P, TILE]) for i in range(4)]

        x_pair = [sb(f"x_pair{i}", [P, D]) for i in range(2)]
        w_rows = [sb(f"w_rows{i}", [P, HD]) for i in range(2)]
        w_pair = [sb(f"w_pair{i}", [P, 2 * HD]) for i in range(2)]
        ug = [sb(f"ug{i}", [P, NCH, GRP]) for i in range(2)]
        drg = sb("drg", [P, GRP])
        bcg = [sb(f"bcg{i}", [32, GRP]) for i in range(2)]
        zg = sb("zg", [P, NCH, GRP])
        sp_a = sb("sp_a", [P, NCH, GRP])
        sp_l = sb("sp_l", [P, NCH, GRP])
        dlg = [sb(f"dlg{i}", [P, NCH, GRP]) for i in range(2)]

        x1g = [sb(f"x1g{i}", [P, NCH, GRP]) for i in range(2)]
        qg = [sb(f"qg{i}", [P, H * HD]) for i in range(2)]
        kvg = [sb(f"kvg{i}", [P, KV]) for i in range(2)]
        k_raw = sb("k_raw", [P, G, HD])
        k_sq = sb("k_sq", [P, G, HD])
        k_n = sb("k_n", [P, G, HD])
        k_rot = sb("k_rot", [P, G, HD])
        k_ss = sb("k_ss", [P, G])
        k_ln = sb("k_ln", [P, G])
        k_r0 = sb("k_r0", [P, G])
        k_r2 = sb("k_r2", [P, G])
        k_rs = sb("k_rs", [P, G])
        k_cos = sb("k_cos", [P, HD])
        k_sin = sb("k_sin", [P, HD])
        k_scale = sb("k_scale", [P, 2, HD])
        one_ks = sb("one_ks", [P, 2, HD])

        cond_i = sb("cond_i", [P, NG], I32)
        len_i = sb("len_i", [P, NG], I32)
        cond_f = sb("cond_f", [P, NG])
        pos_f = sb("pos_f", [P, NG])
        part = sb("part", [P, 2])
        inv = sb("inv", [P, HALF])
        w_idx = sb("w_idx", [P, NG + 1], I32)
        w_now = [sb(f"w_now{i}", [P, 1], I32) for i in range(2)]
        ang = bc[:, 0, :, :].rearrange("p a b -> p (a b)")
        turns = bc[:, 1, :, :].rearrange("p a b -> p (a b)")
        rem = bc[:, 2, :, :].rearrange("p a b -> p (a b)")
        cos = sb("cos", [P, NG * HALF])
        sin = sb("sin", [P, NG * HALF])

        s_const = sem("s_const")
        s_qkvw = sem("s_qkvw")
        c_a = sem("c_a")
        c_dve = sem("c_dve")
        c_sin = sem("c_sin")
        widx_ok = sem("widx_ok")
        wnow_ok = sem("wnow_ok")
        wpair_ok = sem("wpair_ok")
        rope_ok = sem("rope_ok")
        zero_ok = sem("zero_ok")
        zpair_ok = sem("zpair_ok")
        ld_xp = [sem(f"ld_xp{i}") for i in range(2)]
        ld_w = [sem(f"ld_w{i}") for i in range(2)]
        ld_u = [sem(f"ld_u{i}") for i in range(2)]
        ld_dl = [sem(f"ld_dl{i}") for i in range(2)]
        ld_xt = [sem(f"ld_xt{i}") for i in range(2)]
        ld_bc = [sem(f"ld_bc{i}") for i in range(4)]
        ld_x1 = [sem(f"ld_x1{i}") for i in range(2)]
        st_u = [sem(f"st_u{i}") for i in range(4)]
        st_bc = [sem(f"st_bc{i}") for i in range(4)]
        st_dl = [sem(f"st_dl{i}") for i in range(4)]
        st_x1 = [sem(f"st_x1{i}") for i in range(2)]
        st_q = [sem(f"st_q{i}") for i in range(2)]
        st_kv = [sem(f"st_kv{i}") for i in range(2)]
        st_rope = sem("st_rope")
        pe_u, pe_x, pe_z = sem("pe_u"), sem("pe_x"), sem("pe_z")
        pe_hc, pe_y, pe_kv, pe_q = sem("pe_hc"), sem("pe_y"), sem("pe_kv"), sem("pe_q")
        act_u, act_dr, act_sp = sem("act_u"), sem("act_dr"), sem("act_sp")
        act_exp, act_y, act_kv, act_q = sem("act_exp"), sem("act_y"), sem("act_kv"), sem("act_q")
        dve_du, dve_res, dve_dbu, dve_h = sem("dve_du"), sem("dve_res"), sem("dve_dbu"), sem("dve_h")
        dve_z, dve_dl, dve_ks, dve_kt = sem("dve_z"), sem("dve_dl"), sem("dve_ks"), sem("dve_kt")
        dve_ms, act_rs = sem("dve_ms"), sem("act_rs")
        pool_hc, pool_k = sem("pool_hc"), sem("pool_k")

        sp_mark, pool_mark = sem("sp_mark"), sem("pool_mark")

        block = ctx.enter_context(nc.Block())

        def tiles(eng, step):
            for c in range(4):
                step(-1, c, True, False, False)
            for c in range(4):
                step(0, c, True, True, False)
            for c in range(4):
                step(1, c, True, True, True)
            with eng.Fori(2, NT - 1) as t:
                for c in range(4):
                    step(t, c, True, True, True)
            for c in range(4):
                step(NT - 1, c, False, True, True)
            for c in range(4):
                step(NT, c, False, False, True)

        @block.sync
        def _(sp):
            for dst, src in ((a_log, A["a_log"]), (skip_d, A["skip_d"]), (dt_bias, A["dt_bias"]),
                             (ident, A["ident"]), (w_x, A["w_x"]), (w_dt, A["w_dt"]), (part, A["part"])):
                sp.dma_start(dst[:], src).then_inc(s_const, 16)
            sp.dma_start(inv[:], A["inv_freq"].partition_broadcast(P)).then_inc(s_const, 16)
            for half in range(2):
                rows = slice(64 * half, 64 * half + 64)
                sp.dma_start(cond_i[rows, :], A["cond"][half].partition_broadcast(64)).then_inc(s_const, 16)
                sp.dma_start(len_i[rows, :], A["lens_pair"][half].partition_broadcast(64)).then_inc(s_const, 16)
            for s in range(2):
                sp.dma_start(k_scale[:, s, :], A["k_scale2"][s].partition_broadcast(P)).then_inc(s_const, 16)
            sp.dma_start(w_qkv[:], A["w_qkv"]).then_inc(s_qkvw, 16)

            def scan_loads(t, c):
                s, p = 4 * t + c, c % 2
                if c == 0:
                    for g in range(4):
                        wait(sp, st_u[g], 16 * (t + 1), sp_mark)
                        wait(sp, st_dl[g], 16 * (t + 1), sp_mark)
                wait(sp, dve_res, s - 1, sp_mark)
                wait(sp, act_exp, NST * (s - 1), sp_mark)
                cols = bass.ds(t * TILE, TILE)
                sp.dma_start(dl_in[p][:], S["delta"][c][:, cols]).then_inc(ld_dl[p], 16)
                sp.dma_start(u_in[p][:], S["u"][c][:, cols]).then_inc(ld_u[p], 16)
                sp.dma_start(xt_in[p][:], A["x_t"][c][:, cols]).then_inc(ld_xt[p], 16)

            def load_bc(t, g):
                if g == 0:
                    for c in range(4):
                        wait(sp, st_bc[c], 16 * (t + 1), sp_mark)
                wait(sp, pool_hc, NST * 4 * t - NST + 4 * g + 4, sp_mark)
                sp.dma_start(bc[:, 4 * g:4 * g + 4, :, :].rearrange("p a b c -> p (a b) c"),
                             S["bc"][8 * g:8 * g + 8, bass.ds(t * TILE, TILE)].partition_broadcast(P)
                             ).then_inc(ld_bc[g], 16)

            def step(t, c, ahead, scan, behind):
                s, p = 4 * t + c, c % 2
                g, q = s + 4, s - 4
                if ahead:
                    wait(sp, pe_u, g - 1, sp_mark)
                    sp.dma_start(x_pair[p][:], A["x_pairs"][g]).then_inc(ld_xp[p], 16)
                if (scan and not (isinstance(t, int) and s == 0)) or (behind and c == 0 and not scan):
                    wait(sp, act_y, s, sp_mark)
                    t1, c1 = (t, c - 1) if c else (t - 1, 3)
                    sp.dma_start(S["x1"][c1][:, bass.ds(t1 * TILE, TILE)], x1_out[1 - p][:]
                                 ).then_inc(st_x1[1 - p], 16)
                if behind:
                    if c == 0:
                        for i in range(2):
                            wait(sp, st_x1[i], 32 * t, sp_mark)
                    wait(sp, pe_q, q - 1, sp_mark)
                    sp.dma_start(x1g[p][:], S["x1p"][:, :, bass.ds(q * GRP, GRP)]).then_inc(ld_x1[p], 16)
                if ahead:
                    wait(sp, act_u, g + 1, sp_mark)
                    sp.dma_start(S["up"][:, :, bass.ds(g * GRP, GRP)], ug[p][:]).then_inc(st_u[c], 16)
                    wait(sp, act_dr, 2 * (g + 1), sp_mark)
                    sp.dma_start(S["bc"][:, bass.ds(g * GRP, GRP)], bcg[p][:]).then_inc(st_bc[c], 16)
                    if c == 3:
                        if isinstance(t, int) and t == -1:
                            sp.wait_ge(rope_ok, 1)
                        load_bc(t + 1, 0)
                        load_bc(t + 1, 1)
                    wait(sp, dve_dl, g + 1, sp_mark)
                    sp.dma_start(S["deltap"][:, :, bass.ds(g * GRP, GRP)], dlg[p][:]).then_inc(st_dl[c], 16)
                    if c == 3:
                        load_bc(t + 1, 2)
                if c == 3 and ahead:
                    scan_loads(t + 1, 0)
                if scan and c < 3:
                    scan_loads(t, c + 1)
                if behind:
                    wait(sp, act_q, q + 1, sp_mark)
                    sp.dma_start(S["q"][bass.ds(q * GRP, GRP), :], qg[p][:]).then_inc(st_q[p], 16)
                    wait(sp, pool_k, 6 * (q + 1), sp_mark)
                    sp.dma_start(S["kv_new"][bass.ds(q * GRP, GRP), :], kvg[p][:]).then_inc(st_kv[p], 16)
                if c == 3 and ahead:
                    load_bc(t + 1, 3)

            sp.wait_ge(rope_ok, 1)
            sp.dma_start(S["cos"], cos[:]).then_inc(st_rope, 16)
            sp.dma_start(S["sin"], sin[:]).then_inc(st_rope, 16)
            tiles(sp, step)
            sp.wait_ge(st_rope, 32)
            for i in range(2):
                sp.wait_ge(st_x1[i], 16 * 4 * NT // 2)
                sp.wait_ge(st_q[i], 16 * NG // 2)
                sp.wait_ge(st_kv[i], 16 * NG // 2)

        @block.gpsimd
        def _(pool):
            def weights(g, p):
                wait(pool, wpair_ok, 2 * g - 2, pool_mark)
                pool.tensor_copy(w_now[p][:], w_idx[:, bass.ds(g, 1)]).then_inc(wnow_ok, 1)
                wait(pool, wnow_ok, g + 1, pool_mark)
                pool.indirect_dma_start(w_rows[p][:], None, A["w_cond"],
                                        bass.IndirectOffsetOnAxis(ap=w_now[p][:, :], axis=0)
                                        ).then_inc(ld_w[p], 16)

            def key_squares(q):
                pool.wait_ge(act_kv, 2 * (q + 1))
                pool.tensor_tensor(k_sq[:], k_raw[:], k_raw[:], ALU.mult).then_inc(pool_k, 1)

            def keys(q, c):
                p = c % 2
                k = 6 * q
                pool.wait_ge(dve_ks, q + 1)
                pool.tensor_tensor(k_n[:], k_raw[:], k_rs[:].unsqueeze(2).to_broadcast([P, G, HD]),
                                   ALU.mult).then_inc(pool_k, 1)
                pool.wait_ge(pool_k, k + 2)
                for half in range(2):
                    pool.tensor_tensor(k_rot[:, :, HALF * half:HALF * half + HALF],
                                       k_n[:, :, HALF * (1 - half):HALF * (1 - half) + HALF],
                                       k_sin[:, HALF * half:HALF * half + HALF].unsqueeze(1)
                                       .to_broadcast([P, G, HALF]), ALU.mult).then_inc(pool_k, 1)
                pool.tensor_tensor(k_sq[:], k_n[:], k_cos[:].unsqueeze(1).to_broadcast([P, G, HD]),
                                   ALU.mult).then_inc(pool_k, 1)
                pool.wait_ge(pool_k, k + 5)
                pool.tensor_tensor(kvg[p][:, 0:G * HD].rearrange("p (g d) -> p g d", g=G), k_sq[:], k_rot[:],
                                   ALU.add).then_inc(pool_k, 1)

            def step(t, c, ahead, scan, behind):
                s = 4 * t + c
                if ahead:
                    weights(s + 5, (c + 1) % 2)
                if scan:
                    for n in range(NST):
                        if n % 4 == 0:
                            pool.wait_ge(ld_bc[n // 4], 16 * (t + 1))
                        wait(pool, pe_hc, NST * s + n + 1 - 4)
                        pool.wait_ge(dve_h, NST * s + n + 1)
                        pool.tensor_tensor(hc[n % 4][:], hid[n % 4][:], bc[:, n, 1, :],
                                           ALU.mult).then_inc(pool_hc, 1)
                        if n == 8 and behind:
                            key_squares(s - 4)
                    if behind:
                        keys(s - 4, c)
                elif behind:
                    key_squares(s - 4)
                    keys(s - 4, c)

            for i in range(2):
                pool.memset(w_pair[i][:], 0.0).then_inc(zpair_ok, 1)
            pool.wait_ge(widx_ok, 1)
            weights(0, 0)
            tiles(pool, step)
            pool.wait_ge(ld_w[0], 16 * (NG // 2 + 1))

        @block.scalar
        def _(act):
            act.wait_ge(s_const, 16 * 14)
            nc.scalar.activation(neg_a[:], a_log[:], ACT.Exp).then_inc(c_a, 1)
            act.wait_ge(c_sin, 1)
            nc.scalar.activation(sin[:], rem, ACT.Sin).then_inc(c_a, 1)
            act.wait_ge(c_sin, 2)
            nc.scalar.activation(cos[:], rem, ACT.Sin).then_inc(c_a, 1)

            def step(t, c, ahead, scan, behind):
                s, p = 4 * t + c, c % 2
                g, q = s + 4, s - 4

                def weight_blocks():
                    act.wait_ge(ld_w[p], 16 * (2 * t + c // 2 + 3))
                    wait(act, pe_u, g - 1)
                    for b in range(2):
                        rows = slice(64 * b, 64 * b + 64)
                        nc.scalar.copy(w_pair[p][rows, HD * b:HD * b + HD], w_rows[p][rows, :]).then_inc(wpair_ok, 1)

                def sums():
                    wait(act, pe_y, s)
                    if not (isinstance(s, int) and s < 3):
                        act.wait_ge(st_x1[1 - p], 16 * (2 * t + (c - 1) // 2))
                    nc.scalar.copy(x1_out[1 - p][:], y[1 - p]).then_inc(act_y, 1)

                def take_u():
                    act.wait_ge(pe_u, g + 1)
                    wait(act, st_u[(c + 2) % 4], 16 * (t + 1) if c < 2 else 16 * (t + 2))
                    nc.scalar.copy(ug[p][:].rearrange("p a b -> p (a b)"), pro).then_inc(act_u, 1)

                def take_x():
                    act.wait_ge(pe_x, g + 1)
                    wait(act, st_bc[(c + 2) % 4], 16 * (t + 1) if c < 2 else 16 * (t + 2))
                    nc.scalar.copy(drg[:], pro[:, 0:GRP]).then_inc(act_dr, 1)
                    nc.scalar.copy(bcg[p][:], pro[0:32, GRP:2 * GRP]).then_inc(act_dr, 1)

                def softplus():
                    act.wait_ge(dve_z, g + 1)
                    wait(act, dve_dl, g)
                    nc.scalar.activation(sp_a[:], zg[:], ACT.Abs).then_inc(act_sp, 1)
                    act.wait_ge(act_sp, 3 * g + 1)
                    nc.scalar.activation(sp_a[:], sp_a[:], ACT.Exp, scale=-1.0).then_inc(act_sp, 1)
                    act.wait_ge(act_sp, 3 * g + 2)
                    nc.scalar.activation(sp_l[:], sp_a[:], ACT.Ln, bias=1.0).then_inc(act_sp, 1)

                def take_kv():
                    act.wait_ge(pe_kv, q + 1)
                    wait(act, st_kv[p], 16 * (2 * t + c // 2 - 2))
                    nc.scalar.copy(kvg[p][:, G * HD:KV], qk[0][:, G * HD:KV]).then_inc(act_kv, 1)
                    wait(act, pool_k, 6 * q)
                    nc.scalar.copy(k_raw[:].rearrange("p g d -> p (g d)"), qk[0][:, 0:G * HD]).then_inc(act_kv, 1)

                def key_rms():
                    act.wait_ge(dve_ms, q + 1)
                    wait(act, dve_ks, q)
                    nc.scalar.activation(k_ln[:], k_ss[:], ACT.Ln).then_inc(act_rs, 1)
                    act.wait_ge(act_rs, 2 * q + 1)
                    nc.scalar.activation(k_r0[:], k_ln[:], ACT.Exp, scale=-0.5).then_inc(act_rs, 1)

                def take_q():
                    act.wait_ge(pe_q, q + 1)
                    wait(act, st_q[p], 16 * (2 * t + c // 2 - 2))
                    nc.scalar.copy(qg[p][:], qk[1]).then_inc(act_q, 1)

                if scan:
                    act.wait_ge(ld_dl[p], 16 * (2 * t + c // 2 + 1))
                    for n in range(NST):
                        wait(act, dve_h, NST * s + n + 1 - 2)
                        nc.scalar.activation(
                            decay[n % 2].rearrange("p (b t) -> p b t", t=T)[:, :, 1:T],
                            dl_in[p][:].rearrange("p (b t) -> p b t", t=T)[:, :, 1:T],
                            ACT.Exp, scale=neg_a[:, NST * c + n:NST * c + n + 1]).then_inc(act_exp, 1)
                        if n == 2 and not (isinstance(s, int) and s == 0):
                            sums()
                        if ahead:
                            if n == 1:
                                weight_blocks()
                            if n == 4:
                                take_u()
                            if n == 6:
                                take_x()
                            if n == 10:
                                softplus()
                        if behind:
                            if n == 7:
                                take_kv()
                            if n == 12:
                                key_rms()
                            if n == 14:
                                take_q()
                else:
                    if behind and c == 0:
                        sums()
                    if ahead:
                        weight_blocks()
                        take_u()
                        take_x()
                        softplus()
                    if behind:
                        take_kv()
                        key_rms()
                        take_q()

            act.wait_ge(zpair_ok, 2)
            act.wait_ge(zero_ok, 3)
            tiles(act, step)

        @block.vector
        def _(dve):
            done = [0]

            def link(ins):
                done[0] += 1
                ins.then_inc(c_dve, 1)
                dve.wait_ge(c_dve, done[0])

            for i in range(2):
                nc.vector.memset(decay[i].rearrange("p (b t) -> p b t", t=T)[:, :, 0:1], 0.0).then_inc(zero_ok, 1)
            dve.wait_ge(s_const, 16 * 14)
            link(nc.vector.tensor_copy(cond_f[:], cond_i[:]))
            link(nc.vector.tensor_scalar(cond_f[:], cond_f[:], 64.0, part[:, 0:1], ALU.mult, ALU.add))
            nc.vector.tensor_copy(w_idx[:, 0:NG], cond_f[:])
            link(nc.vector.tensor_copy(w_idx[:, NG:NG + 1], cond_f[:, NG - 1:NG]))
            nc.vector.tensor_copy(pos_f[:], len_i[:]).then_inc(widx_ok, 1)
            dve.wait_ge(c_a, 1)
            nc.vector.tensor_scalar(neg_a[:], neg_a[:], -1.0, None, ALU.mult).then_inc(zero_ok, 1)
            dve.wait_ge(widx_ok, 1)
            link(nc.vector.tensor_scalar(pos_f[:], pos_f[:], part[:, 0:1], None, ALU.add))
            link(nc.vector.tensor_tensor(ang.rearrange("p (g f) -> p g f", f=HALF),
                                         pos_f[:].unsqueeze(2).to_broadcast([P, NG, HALF]),
                                         inv[:].unsqueeze(1).to_broadcast([P, NG, HALF]), ALU.mult))
            for which, (quarter, shift) in enumerate(((0.0, 0.0), (0.25, float(np.float32(np.pi / 2))))):
                link(nc.vector.tensor_scalar(turns, ang, float(1 / (2 * np.pi)), quarter, ALU.mult, ALU.add))
                link(nc.vector.tensor_scalar(turns, turns, MAGIC, None, ALU.add))
                link(nc.vector.tensor_scalar(turns, turns, MAGIC, None, ALU.subtract))
                if which:
                    dve.wait_ge(c_a, 2)
                link(nc.vector.scalar_tensor_tensor(rem, turns, -TWO_PI[0], ang, ALU.mult, ALU.add))
                link(nc.vector.scalar_tensor_tensor(rem, turns, -TWO_PI[1], rem, ALU.mult, ALU.add))
                link(nc.vector.scalar_tensor_tensor(rem, turns, -TWO_PI[2], rem, ALU.mult, ALU.add))
                link(nc.vector.tensor_scalar(rem, rem, shift, 3.1415925, ALU.add, ALU.min))
                nc.vector.tensor_scalar(rem, rem, -3.1415925, None, ALU.max).then_inc(c_sin, 1)
            nc.vector.tensor_scalar(one_ks[:, 0, :], k_scale[:, 0, :], 1.0, None, ALU.add)
            nc.vector.tensor_scalar(one_ks[:, 1, 0:HALF], k_scale[:, 1, 0:HALF], -1.0, -1.0, ALU.mult, ALU.add)
            link(nc.vector.tensor_scalar(one_ks[:, 1, HALF:HD], k_scale[:, 1, HALF:HD], 1.0, None, ALU.add))
            dve.wait_ge(c_a, 3)
            nc.vector.memset(k_ss[:], 0.0).then_inc(rope_ok, 1)

            def step(t, c, ahead, scan, behind):
                s, p = 4 * t + c, c % 2
                g, q = s + 4, s - 4

                def times_b(n):
                    if n == 0:
                        dve.wait_ge(dve_du, s + 1)
                    if n % 4 == 0:
                        dve.wait_ge(ld_bc[n // 4], 16 * (t + 1))
                    nc.vector.tensor_tensor(dbu[n % 4][:], du, bc[:, n, 0, :], ALU.mult).then_inc(dve_dbu, 1)

                def add_bias():
                    dve.wait_ge(pe_z, g + 1)
                    wait(dve, act_sp, 3 * g)
                    nc.vector.tensor_tensor(zg[:], pro.rearrange("p (c t) -> p c t", c=NCH),
                                            dt_bias[:].unsqueeze(2).to_broadcast([P, NCH, GRP]),
                                            ALU.add).then_inc(dve_z, 1)

                def delta():
                    dve.wait_ge(act_sp, 3 * (g + 1))
                    wait(dve, st_dl[(c + 2) % 4], 16 * (t + 1) if c < 2 else 16 * (t + 2))
                    nc.vector.scalar_tensor_tensor(dlg[p][:].rearrange("p a b -> p (a b)"),
                                                   zg[:].rearrange("p a b -> p (a b)"), 0.0,
                                                   sp_l[:].rearrange("p a b -> p (a b)"),
                                                   ALU.max, ALU.add).then_inc(dve_dl, 1)

                def key_squares():
                    wait(dve, pool_k, 6 * q)
                    for out, table, i in ((k_cos, cos, 0), (k_sin, sin, 1)):
                        nc.vector.tensor_tensor(
                            out[:].rearrange("p (a f) -> p a f", a=2),
                            table[:, bass.ds(q * HALF, HALF)].unsqueeze(1).to_broadcast([P, 2, HALF]),
                            one_ks[:, i, :].rearrange("p (a f) -> p a f", a=2), ALU.mult)
                    dve.wait_ge(pool_k, 6 * q + 1)
                    wait(dve, act_rs, 2 * q)
                    nc.vector.tensor_reduce(k_ss[:], k_sq[:], AX.X, ALU.add).then_inc(dve_kt, 1)
                    dve.wait_ge(dve_kt, 3 * q + 1)
                    nc.vector.tensor_scalar(k_ss[:], k_ss[:], 1.0 / HD, EPS, ALU.mult, ALU.add).then_inc(dve_ms, 1)

                def key_rms():
                    dve.wait_ge(act_rs, 2 * q + 2)
                    nc.vector.tensor_tensor(k_r2[:], k_r0[:], k_r0[:], ALU.mult).then_inc(dve_kt, 1)
                    dve.wait_ge(dve_kt, 3 * q + 2)
                    nc.vector.scalar_tensor_tensor(k_r2[:], k_r2[:], -0.5, k_ss[:], ALU.mult, ALU.mult
                                                   ).then_inc(dve_kt, 1)
                    dve.wait_ge(dve_kt, 3 * q + 3)
                    nc.vector.scalar_tensor_tensor(k_rs[:], k_r2[:], 1.5, k_r0[:], ALU.add, ALU.mult
                                                   ).then_inc(dve_ks, 1)

                if scan:
                    uses = 16 * (2 * t + c // 2 + 1)
                    dve.wait_ge(ld_u[p], uses)
                    dve.wait_ge(ld_dl[p], uses)
                    nc.vector.tensor_tensor(du, dl_in[p][:], u_in[p][:], ALU.mult).then_inc(dve_du, 1)
                    dve.wait_ge(ld_xt[p], uses)
                    wait(dve, pe_y, s - 1)
                    nc.vector.scalar_tensor_tensor(resid[p][:], u_in[p][:], skip_d[:, c:c + 1], xt_in[p][:],
                                                   ALU.mult, ALU.add).then_inc(dve_res, 1)
                    times_b(0)
                    for n in range(NST):
                        if ahead and n == 9:
                            add_bias()
                        if ahead and n == 13:
                            delta()
                        if behind and n == 10:
                            key_squares()
                        if behind and n == 14:
                            key_rms()
                        if n < NST - 1:
                            times_b(n + 1)
                        dve.wait_ge(act_exp, NST * s + n + 1)
                        dve.wait_ge(dve_dbu, NST * s + n + 1)
                        wait(dve, pool_hc, NST * s + n + 1 - 4)
                        nc.vector.tensor_tensor_scan(hid[n % 4][:], decay[n % 2], dbu[n % 4][:], 0.0,
                                                     ALU.mult, ALU.add).then_inc(dve_h, 1)
                else:
                    if ahead:
                        add_bias()
                        delta()
                    if behind:
                        key_squares()
                        key_rms()

            tiles(dve, step)

        @block.tensor
        def _(pe):
            pe.wait_ge(s_const, 16 * 14)
            pe.wait_ge(s_qkvw, 16)

            def step(t, c, ahead, scan, behind):
                s, p = 4 * t + c, c % 2
                g, q = s + 4, s - 4

                def project_u():
                    uses = 16 * (2 * t + c // 2 + 3)
                    pe.wait_ge(ld_xp[p], uses)
                    pe.wait_ge(wpair_ok, 2 * (g + 1))
                    wait(pe, dve_z, g)
                    for j in range(NCH):
                        mm = nc.tensor.matmul(pro[:, GRP * j:GRP * j + GRP], x_pair[p][:, P * j:P * j + P],
                                              w_pair[p][:], start=True, stop=True)
                    mm.then_inc(pe_u, 1)

                def project_x():
                    pe.wait_ge(act_u, g + 1)
                    for lo, n, m in ((0, 0, P), (P, 1, 32)):
                        for j in range(NCH):
                            mm = nc.tensor.matmul(pro[0:m, GRP * n:GRP * n + GRP], w_x[:, j, lo:lo + m],
                                                  ug[p][:, j, :], start=(j == 0), stop=(j == NCH - 1))
                    mm.then_inc(pe_x, 1)

                def project_dt():
                    pe.wait_ge(act_dr, 2 * (g + 1))
                    for j in range(NCH):
                        mm = nc.tensor.matmul(pro[:, GRP * j:GRP * j + GRP], w_dt[:, P * j:P * j + P], drg[:],
                                              start=True, stop=True)
                    mm.then_inc(pe_z, 1)

                def project_qkv(i):
                    if i == 0:
                        pe.wait_ge(ld_x1[p], 16 * (2 * t + c // 2 - 1))
                        wait(pe, act_kv, 2 * q)
                    else:
                        wait(pe, act_q, q)
                    lo = D * (1 - i)
                    for j in range(NCH):
                        mm = nc.tensor.matmul(qk[i], x1g[p][:, j, :], w_qkv[:, j, lo:lo + D],
                                              start=(j == 0), stop=(j == NCH - 1))
                    mm.then_inc((pe_kv, pe_q)[i], 1)

                if scan:
                    for n in range(NST):
                        if ahead:
                            if n == 3:
                                project_u()
                            if n == 5:
                                project_x()
                            if n == 8:
                                project_dt()
                        if behind:
                            if n == 6:
                                project_qkv(0)
                            if n == 12:
                                project_qkv(1)
                        if n == 0:
                            wait(pe, act_y, s - 1)
                        pe.wait_ge(pool_hc, NST * s + n + 1)
                        nc.tensor.matmul(y[p], ident[:], hc[n % 4][:], start=(n == 0), stop=False
                                         ).then_inc(pe_hc, 1)
                    pe.wait_ge(dve_res, s + 1)
                    nc.tensor.matmul(y[p], ident[:], resid[p][:], start=False, stop=True).then_inc(pe_y, 1)
                else:
                    if ahead:
                        project_u()
                        project_x()
                        project_dt()
                    if behind:
                        project_qkv(0)
                        project_qkv(1)

            tiles(pe, step)


def attention_block(nc, A, S):
    with ExitStack() as ctx:
        def sb(name, shape, dt=F32):
            return ctx.enter_context(nc.sbuf_tensor(name, shape, dt))

        def sem(name):
            return ctx.enter_context(nc.semaphore(name))

        psum = ctx.enter_context(nc.psum_tensor("attn_psum", [P, 8, 512], F32))
        q_bank = psum[:, 0, :]
        k_bank = [psum[:, 1 + i, 0:NKEY] for i in range(2)]
        score = [psum[:, 3 + i, 0:NKEY] for i in range(2)]
        p_bank = psum[0:KC, 5, 0:NKC * P]
        o_bank = psum[:, 6, :].rearrange("p (c t) -> p c t", c=4)
        a_bank = psum[:, 7, :]

        ident = sb("ident2", [P, P])
        ones = sb("ones", [P, P])
        w_o = sb("w_o", [P, 4, D])
        w_r = sb("w_r", [P, D])
        b_r = sb("b_r", [P, 1])
        q_scale = sb("q_scale", [P, 2, HD])
        one_qs = sb("one_qs", [P, 2, HD])
        cos = sb("cos2", [P, NG * HALF])
        sin = sb("sin2", [P, NG * HALF])
        dist = sb("dist", [P, NKEY])
        own = sb("own", [P, P])
        before = sb("before", [P, P])
        slot_no = sb("slot_no", [P, SEL * 2])

        ids = sb("ids", [P, NBLK])
        table_i = sb("table_i", [P, NBLK], I32)
        table = sb("table", [P, NBLK])
        len_i = sb("len2_i", [P, 1 + B], I32)
        len_f = sb("len_f", [P, 1 + B])
        sh_i = sb("sh_i", [P, 1 + B], I32)
        q_blk = sb("q_blk", [P, 1 + B])
        rest = sb("rest", [P, 1 + B])
        first = sb("first", [P, 1 + B])
        mask_at = sb("mask_at", [P, 1 + B])
        slots = sb("slots", [P, NSLOT])
        w_slots = sb("w_slots", [P, NWC])
        w_slot0 = sb("w_slot0", [P, NWC])
        junk = sb("junk", [P, NBLK])
        win = sb("win", [P, NSLOT])
        wid = sb("wid", [P, NWC])
        win_t = sb("win_t", [NSLOT, B])
        wid_t = sb("wid_t", [NWC, P])
        row_blk = sb("row_blk", [KC, NKC, B])
        all_blk = sb("all_blk", [P, NSLOT * B])
        all_wid = sb("all_wid", [P, NWC * P])
        later = sb("later", [P, NWC, NWC * P])
        beats = sb("beats", [P, NWC, NWC * P])
        off_in = sb("off_in", [P, 1])
        tau0 = sb("tau0", [P, NWC, BLOCK])
        tau = sb("tau", [P, NWC, BLOCK])
        cover = sb("cover", [P, NWC, BLOCK])
        alive = sb("alive", [P, NWC, BLOCK])
        tok0 = sb("tok0", [P, 1])
        token = sb("token", [P, NWC, BLOCK])
        placed = sb("placed", [P, NWC, SC, KC])
        match = sb("match", [P, NWC, NSLOT * B])
        far = sb("far", [KC, NKC * B])
        idx_old = sb("idx_old", [KC, NKC, B], I32)
        idx_new = sb("idx_new", [KC, NKC, B], I32)

        old_now = [sb(f"old_now{i}", [KC, NKC], I32) for i in range(4)]
        new_now = [sb(f"new_now{i}", [KC, NKC], I32) for i in range(4)]
        kv = [sb(f"kv{i}", [KC, NKC, KV]) for i in range(4)]
        q_in = [sb(f"q_in{i}", [P, H, HD]) for i in range(2)]
        q_sq = sb("q_sq", [P, H, HD])
        q_n = sb("q_n", [P, H, HD])
        q_rot = sb("q_rot", [P, H, HD])
        q_ss, q_ln, q_r0, q_r2, q_rs = (sb(n, [P, H]) for n in ("q_ss", "q_ln", "q_r0", "q_r2", "q_rs"))
        q_cos = sb("q_cos", [P, HD])
        q_sin = sb("q_sin", [P, HD])
        q_t = [sb(f"q_t{i}", [P, 2, 2, 2, T]) for i in range(2)]
        k_t = [sb(f"k_t{i}", [P, 2, NKEY]) for i in range(2)]
        far2 = sb("far2", [P, NKEY])
        mask = [sb(f"mask{i}", [P, NKEY]) for i in range(2)]
        sm = [sb(f"sm{i}", [P, NKEY]) for i in range(2)]
        prob = [sb(f"prob{i}", [P, NKEY]) for i in range(2)]
        p_t = [sb(f"p_t{i}", [KC, NKC, P]) for i in range(2)]
        top = [sb(f"top{i}", [P, 1]) for i in range(2)]
        ntop = [sb(f"ntop{i}", [P, 1]) for i in range(2)]
        total = [sb(f"total{i}", [P, 1]) for i in range(2)]
        share = [sb(f"share{i}", [P, 1]) for i in range(2)]
        o_t = [sb(f"o_t{i}", [P, 4, P]) for i in range(2)]
        a_sb = [sb(f"a_sb{i}", [P, D]) for i in range(2)]
        r_junk = sb("r_junk", [P, D])
        r_s = sb("r_s", [P, 1])
        r_diag = sb("r_diag", [P, P])
        r_own, r_gt, r_eq, r_rank = (sb(n, [P, 1]) for n in ("r_own", "r_gt", "r_eq", "r_rank"))
        keep = [sb(f"keep{i}", [P, 2 * SEL]) for i in range(2)]
        keep_t = [sb(f"keep_t{i}", [P, P]) for i in range(2)]
        xs = [sb(f"xs{i}", [P, NCH, 2 * SEL]) for i in range(2)]

        s_c = sem("a_const")
        c_dve, c_pe = sem("c2_dve"), sem("c2_pe")
        st_blk, ld_blk = sem("st_blk"), sem("ld_blk")
        idx_ok, now_ok, pool_mark = sem("idx_ok"), sem("now_ok"), sem("pool_mark2")
        sp_mark, dve_mark = sem("sp_mark2"), sem("dve_mark2")
        filled = sem("filled")
        ld_old = [sem(f"ld_old{i}") for i in range(4)]
        ld_kv = [sem(f"ld_kv{i}") for i in range(4)]
        ld_q = [sem(f"ld_q{i}") for i in range(2)]
        st_keep = [sem(f"st_keep{i}") for i in range(2)]
        st_xs = [sem(f"st_xs{i}") for i in range(2)]
        pe_q, pe_k, pe_sc, pe_pt, pe_pv = sem("pe2_q"), sem("pe_k"), sem("pe_sc"), sem("pe_pt"), sem("pe_pv")
        pe_a, pe_row, pe_xs = sem("pe_a"), sem("pe_row"), sem("pe_xs")
        act_sq, act_qr, act_qt, act_kt = sem("act_sq"), sem("act_qr"), sem("act_qt"), sem("act_kt")
        act_far, act_e, act_pt = sem("act_far"), sem("act_e"), sem("act_pt")
        act_o, act_a, act_xs = sem("act_o"), sem("act_a"), sem("act_xs")
        dve_qc, dve_ms, dve_q, dve_mask = sem("dve_qc"), sem("dve_qms"), sem("dve_q"), sem("dve_mask")
        dve_sm, dve_nt, dve_sh, dve_p = sem("dve_sm"), sem("dve_nt"), sem("dve_sh"), sem("dve_p")
        dve_rc, dve_diag, dve_keep = sem("dve_rc"), sem("dve_diag"), sem("dve_keep")

        NC = 23

        block = ctx.enter_context(nc.Block())

        def pairs(eng, pair):
            pair(0, 0, 0, False, True)
            pair(1, 0, 1, True, True)
            pair(2, 1, 0, True, True)
            pair(3, 1, 1, True, True)
            with eng.Fori(2, NG // 2 - 1) as i:
                pair(2 * i, i, 0, True, True)
                pair(2 * i + 1, i, 1, True, True)
            pair(NG - 2, NG // 2 - 1, 0, True, True)
            pair(NG - 1, NG // 2 - 1, 1, True, False)

        def unit(u):
            return u // 4, u // 2 % 2, u % 2

        @block.sync
        def _(sp):
            for dst, src in ((ident, A["ident"]), (ids, A["ids"]), (w_slot0, A["w_slot0"]), (tau0, A["tau0"]),
                             (tok0, A["tok0"]), (off_in, A["off_in"]), (later, A["later"]), (dist, A["dist"]),
                             (own, A["own"]), (before, A["before"]), (slot_no, A["slot_no"]), (w_o, A["w_o"]),
                             (cos, S["cos"]), (sin, S["sin"])):
                sp.dma_start(dst[:], src).then_inc(s_c, 16)
            for half in range(2):
                rows = slice(64 * half, 64 * half + 64)
                sp.dma_start(table_i[rows, :], A["table"]).then_inc(s_c, 16)
                sp.dma_start(len_i[rows, 0:1], A["lens"]).then_inc(s_c, 16)
            sp.dma_start(len_i[:, 1:1 + B], A["lens_row"].partition_broadcast(P)).then_inc(s_c, 16)
            sp.dma_start(w_r[:], A["w_r"].partition_broadcast(P)).then_inc(s_c, 16)
            sp.dma_start(b_r[:], A["b_r"].partition_broadcast(P)).then_inc(s_c, 16)
            for s in range(2):
                sp.dma_start(q_scale[:, s, :], A["q_scale2"][s].partition_broadcast(P)).then_inc(s_c, 16)
            sp.wait_ge(c_dve, C_TURNED)
            sp.dma_start(S["win"], win_t[:]).then_inc(st_blk, 16)
            sp.dma_start(S["wid"], wid_t[:]).then_inc(st_blk, 16)
            sp.wait_ge(st_blk, 32)
            by_slot = S["win"].rearrange("(c j) b -> j c b", j=SC)
            for j in range(SC):
                sp.dma_start(row_blk[BLOCK * j:BLOCK * j + BLOCK, :, :], by_slot[j].partition_broadcast(BLOCK)
                             ).then_inc(ld_blk, 16)
            sp.dma_start(all_blk[:], S["win"].rearrange("s b -> (s b)").partition_broadcast(P)).then_inc(ld_blk, 16)
            sp.dma_start(all_wid[:], S["wid"].rearrange("s b -> (s b)").partition_broadcast(P)).then_inc(ld_blk, 16)

            def load_q(m, h):
                wait(sp, dve_q, 6 * (m - 1), sp_mark)
                sp.dma_start(q_in[h][:].rearrange("p h d -> p (h d)"), S["q"][bass.ds(m * GRP, GRP), :]
                             ).then_inc(ld_q[h], 16)

            def pair(m, i, h, last, nxt):
                if nxt:
                    load_q(m + 1, 1 - h)
                if last:
                    store(m - 1, i if h else i - 1, 1 - h)

            def store(m, i, h):
                wait(sp, act_xs, 2 * (m + 1), sp_mark)
                sp.dma_start(S["keep"][bass.ds(2 * i + h, 1)].rearrange("o s t -> (o s) t"),
                             keep_t[h][64 * h:64 * h + 64, :]).then_inc(st_keep[h], 16)
                sp.dma_start(S["xsp"][:, :, bass.ds(m * 2 * SEL, 2 * SEL)], xs[h][:]).then_inc(st_xs[h], 16)

            load_q(0, 0)
            pairs(sp, pair)
            store(NG - 1, NG // 2 - 1, 1)
            for h in range(2):
                sp.wait_ge(st_keep[h], 16 * NG // 2)
                sp.wait_ge(st_xs[h], 16 * NG // 2)

        @block.gpsimd
        def _(pool):
            nc.gpsimd.memset(placed[:], 0.0).then_inc(filled, 1)
            nc.gpsimd.memset(ones[:], 1.0).then_inc(filled, 1)
            pool.wait_ge(idx_ok, 2)

            def gather_old(b, s):
                wait(pool, pe_pv, 4 * (b - 3), pool_mark)
                pool.tensor_copy(old_now[s][:], idx_old[:, :, bass.ds(b, 1)].rearrange("p c o -> p (c o)")
                                 ).then_inc(now_ok, 1)
                pool.tensor_copy(new_now[s][:], idx_new[:, :, bass.ds(b, 1)].rearrange("p c o -> p (c o)")
                                 ).then_inc(now_ok, 1)
                wait(pool, now_ok, 2 * (b + 1), pool_mark)
                for c in range(NKC):
                    pool.indirect_dma_start(kv[s][:, c, :], None, A["kv_rows"],
                                            bass.IndirectOffsetOnAxis(ap=old_now[s][:, c:c + 1], axis=0)
                                            ).then_inc(ld_old[s], 16)

            def gather_new(i, s):
                wait(pool, ld_old[s], 16 * NKC * (i + 1), pool_mark)
                for c in range(NKC):
                    pool.indirect_dma_start(kv[s][:, c, :], None, S["kv_new"],
                                            bass.IndirectOffsetOnAxis(ap=new_now[s][:, c:c + 1], axis=0),
                                            bounds_check=NTOK - 1, oob_is_err=False).then_inc(ld_kv[s], 16)

            gather_old(0, 0)
            for s in range(4):
                gather_old(s + 1, (s + 1) % 4)
                gather_new(0, s)
            with pool.Fori(1, B // 4 - 1) as i:
                for s in range(4):
                    gather_old(4 * i + s + 1, (s + 1) % 4)
                    gather_new(i, s)
            for s in range(4):
                if s < 3:
                    gather_old(B - 4 + s + 1, s + 1)
                gather_new(B // 4 - 1, s)

        @block.scalar
        def _(act):
            def query_squares(m, h):
                act.wait_ge(ld_q[h], 16 * (m // 2 + 1) if isinstance(m, int) else 16 * (half_of[0] + 1))
                wait(act, dve_q, 6 * m)
                nc.scalar.activation(q_sq[:], q_in[h][:], ACT.Square).then_inc(act_sq, 1)

            def query_rms(m):
                act.wait_ge(dve_ms, m + 1)
                nc.scalar.activation(q_ln[:], q_ss[:], ACT.Ln).then_inc(act_qr, 1)
                act.wait_ge(act_qr, 2 * m + 1)
                nc.scalar.activation(q_r0[:], q_ln[:], ACT.Exp, scale=-0.5).then_inc(act_qr, 1)

            def take_q(m, h):
                act.wait_ge(pe_q, m + 1)
                wait(act, pe_sc, 8 * (m - 1))
                for gp in range(2):
                    nc.scalar.copy(q_t[h][:, gp, :, :, :].rearrange("p b j t -> p j b t"),
                                   q_bank[:, 2 * P * gp:2 * P * gp + 2 * P].rearrange("p (j b t) -> p j b t", j=2, b=2)
                                   ).then_inc(act_qt, 1)

            def take_k(m, b):
                act.wait_ge(pe_k, 2 * m + b + 1)
                wait(act, pe_sc, 8 * m - 4 + 4 * b)
                for gp in range(2):
                    nc.scalar.copy(k_t[b][:, gp, :], k_bank[gp]).then_inc(act_kt, 1)

            def distance(m, b):
                wait(act, dve_mask, 2 * m + b)
                nc.scalar.activation(far2[:], dist[:], ACT.Square, bias=mask_at[:, bass.ds(2 * m + b + 1, 1)]
                                     ).then_inc(act_far, 1)

            def exps(m, u):
                act.wait_ge(dve_nt, 8 * m + u + 1)
                wait(act, pe_pt, 8 * m + u - 1)
                nc.scalar.activation(prob[u % 2][:], sm[u % 2][:], ACT.Exp, bias=ntop[u % 2][:], scale=SCALE,
                                     accum_out=total[u % 2][:]).then_inc(act_e, 1)

            def take_p(m, u):
                act.wait_ge(pe_pt, 8 * m + u + 1)
                wait(act, pe_pv, 8 * m + u - 1)
                nc.scalar.copy(p_t[u % 2][:].rearrange("p c t -> p (c t)"), p_bank).then_inc(act_pt, 1)

            def take_rows(m, h):
                act.wait_ge(pe_xs, m + 1)
                if not (isinstance(m, int) and m < 2):
                    act.wait_ge(st_keep[h], 16 * half_of[1])
                    act.wait_ge(st_xs[h], 16 * half_of[1])
                rows = slice(64 * h, 64 * h + 64)
                nc.scalar.copy(keep_t[h][rows, :], a_bank[rows, P:2 * P]).then_inc(act_xs, 1)
                nc.scalar.copy(xs[h][:].rearrange("p c s -> p (c s)"), a_bank[:, 2 * P:]).then_inc(act_xs, 1)

            half_of = [0, 0]

            def pair(m, i, h, last, nxt):
                half_of[0] = i if h == 0 else i + 1
                half_of[1] = i - 1 if h == 0 else i
                for u in range(8):
                    if u < 7:
                        exps(m, u + 1)
                    elif nxt:
                        exps(m + 1, 0)
                    if u == 0:
                        distance(m, 1)
                        if nxt:
                            query_squares(m + 1, 1 - h)
                    if u == 1 and nxt:
                        query_rms(m + 1)
                    if u == 2:
                        take_k(m, 1)
                    if u == 4 and nxt:
                        distance(m + 1, 0)
                        take_q(m + 1, 1 - h)
                    if u == 5 and last:
                        take_rows(m - 1, 1 - h)
                    if u == 6 and nxt:
                        take_k(m + 1, 0)
                    take_p(m, u)
                take_o(m, h)
                act.wait_ge(pe_a, m + 1)
                wait(act, pe_xs, m - 1)
                nc.scalar.copy(a_sb[h][:], a_bank).then_inc(act_a, 1)

            def take_o(m, h):
                act.wait_ge(pe_pv, 8 * m + 8)
                wait(act, pe_a, m - 1)
                nc.scalar.copy(o_t[h][:], o_bank).then_inc(act_o, 1)

            act.wait_ge(s_c, 16 * NC)
            query_squares(0, 0)
            query_rms(0)
            act.wait_ge(c_dve, C_MASK)
            distance(0, 0)
            take_q(0, 0)
            take_k(0, 0)
            exps(0, 0)
            pairs(act, pair)
            half_of[1] = NG // 2 - 1
            take_rows(NG - 1, 1)

        @block.vector
        def _(dve):
            done = [0]

            def mark(ins):
                done[0] += 1
                ins.then_inc(c_dve, 1)
                return ins

            def link(ins):
                mark(ins)
                dve.wait_ge(c_dve, done[0])

            dve.wait_ge(s_c, 16 * NC)
            v = nc.vector
            mark(v.tensor_scalar(one_qs[:, 0, :], q_scale[:, 0, :], 1.0, None, ALU.add))
            mark(v.tensor_scalar(one_qs[:, 1, 0:HALF], q_scale[:, 1, 0:HALF], -1.0, -1.0, ALU.mult, ALU.add))
            mark(v.tensor_scalar(one_qs[:, 1, HALF:HD], q_scale[:, 1, HALF:HD], 1.0, None, ALU.add))
            mark(v.tensor_copy(table[:], table_i[:]))
            mark(v.tensor_copy(len_f[:], len_i[:]))
            link(v.tensor_scalar(sh_i[:], len_i[:], 4, None, ALU.arith_shift_right))
            link(v.tensor_copy(q_blk[:], sh_i[:]))
            link(v.scalar_tensor_tensor(rest[:], q_blk[:], -float(BLOCK), len_f[:], ALU.mult, ALU.add))
            link(v.tensor_scalar(first[:], len_f[:], -float(WINDOW - 1), 0.0, ALU.add, ALU.max))
            link(v.tensor_copy(sh_i[:], first[:]))
            link(v.tensor_scalar(sh_i[:], sh_i[:], 4, None, ALU.arith_shift_right))
            link(v.tensor_copy(first[:], sh_i[:]))
            link(v.tensor_scalar(first[:], first[:], float(NBLK - NSLOT), None, ALU.min))
            link(v.scalar_tensor_tensor(mask_at[:], first[:], float(BLOCK), len_f[:], ALU.mult, ALU.subtract))
            link(v.tensor_scalar(mask_at[:], mask_at[:], WINDOW / 2 - 0.5, None, ALU.add))
            assert done[0] == C_MASK
            mark(v.tensor_scalar(slots[:], ids[:, 0:NSLOT], first[:, 0:1], None, ALU.add))
            link(v.tensor_scalar(w_slots[:], w_slot0[:], q_blk[:, 0:1], None, ALU.add))
            for n in range(NSLOT + NWC):
                at, to = (slots[:, n:n + 1], win[:, n:n + 1]) if n < NSLOT else \
                    (w_slots[:, n - NSLOT:n - NSLOT + 1], wid[:, n - NSLOT:n - NSLOT + 1])
                link(v.scalar_tensor_tensor(junk[:], ids[:], at, table[:], ALU.is_equal, ALU.mult, accum_out=to))
            assert done[0] == C_IDS
            link(v.tensor_scalar(tau[:], tau0[:], rest[:, 0:1], None, ALU.subtract))
            link(v.tensor_scalar(cover[:], tau[:], 0.0, None, ALU.is_ge))
            link(v.scalar_tensor_tensor(cover[:].rearrange("p c o -> p (c o)"), tau[:].rearrange("p c o -> p (c o)"),
                                        float(T), cover[:].rearrange("p c o -> p (c o)"), ALU.is_lt, ALU.mult))
            link(v.tensor_scalar(token[:], tau[:], tok0[:, 0:1], None, ALU.add))
            dve.wait_ge(c_pe, 1)
            mark(v.tensor_copy(win_t[:], q_bank[0:NSLOT, 0:B]))
            mark(v.tensor_copy(wid_t[:], q_bank[0:NWC, P:2 * P]))
            assert done[0] == C_TURNED
            dve.wait_ge(ld_blk, 16 * 9)
            for c in range(NWC):
                mark(v.scalar_tensor_tensor(beats[:, c, :], all_wid[:], wid[:, c:c + 1], later[:, c, :],
                                            ALU.is_equal, ALU.mult))
                mark(v.tensor_scalar(match[:, c, :], all_blk[:], wid[:, c:c + 1], None, ALU.is_equal))
            assert done[0] == C_BEATS
            v.tensor_scalar(idx_old[:], row_blk[:], float(BLOCK), off_in[0:KC, 0:1], ALU.mult, ALU.add
                            ).then_inc(idx_ok, 1)
            dve.wait_ge(c_pe, 2)
            link(v.scalar_tensor_tensor(alive[:].rearrange("p c o -> p (c o)"), q_bank[:, 0:NWC * BLOCK], 0.5,
                                        cover[:].rearrange("p c o -> p (c o)"), ALU.is_lt, ALU.mult))
            dve.wait_ge(filled, 2)
            for j in range(SC):
                mark(v.tensor_tensor(placed[:, :, j, BLOCK * j:BLOCK * j + BLOCK], alive[:], token[:], ALU.mult))
            assert done[0] == C_PLACED
            dve.wait_ge(c_pe, 3)
            winner = k_bank[0][0:KC, 0:NKC * B]
            link(v.tensor_scalar(far[:], winner, 0.5, FAR, ALU.is_lt, ALU.mult))
            v.scalar_tensor_tensor(idx_new[:].rearrange("p c b -> p (c b)"), winner, -1.0, far[:], ALU.add, ALU.add
                                   ).then_inc(idx_ok, 1)

            def query_squares(m):
                for out, table_, i in ((q_cos, cos, 0), (q_sin, sin, 1)):
                    v.tensor_tensor(out[:].rearrange("p (a f) -> p a f", a=2),
                                    table_[:, bass.ds(m * HALF, HALF)].unsqueeze(1).to_broadcast([P, 2, HALF]),
                                    one_qs[:, i, :].rearrange("p (a f) -> p a f", a=2), ALU.mult)
                dve.wait_ge(act_sq, m + 1)
                v.tensor_reduce(q_ss[:], q_sq[:], AX.X, ALU.add).then_inc(dve_qc, 1)
                dve.wait_ge(dve_qc, 3 * m + 1)
                v.tensor_scalar(q_ss[:], q_ss[:], 1.0 / HD, EPS, ALU.mult, ALU.add).then_inc(dve_ms, 1)

            def queries(m, h):
                dve.wait_ge(act_qr, 2 * m + 2)
                v.tensor_tensor(q_r2[:], q_r0[:], q_r0[:], ALU.mult).then_inc(dve_q, 1)
                dve.wait_ge(dve_q, 6 * m + 1)
                v.scalar_tensor_tensor(q_r2[:], q_r2[:], -0.5, q_ss[:], ALU.mult, ALU.mult).then_inc(dve_q, 1)
                dve.wait_ge(dve_q, 6 * m + 2)
                v.scalar_tensor_tensor(q_rs[:], q_r2[:], 1.5, q_r0[:], ALU.add, ALU.mult).then_inc(dve_q, 1)
                dve.wait_ge(dve_q, 6 * m + 3)
                v.tensor_tensor(q_n[:], q_in[h][:], q_rs[:].unsqueeze(2).to_broadcast([P, H, HD]), ALU.mult
                                ).then_inc(dve_q, 1)
                dve.wait_ge(dve_q, 6 * m + 4)
                wait(dve, pe_q, m)
                for half in range(2):
                    v.tensor_tensor(q_rot[:, :, HALF * half:HALF * half + HALF],
                                    q_n[:, :, HALF * (1 - half):HALF * (1 - half) + HALF],
                                    q_sin[:, HALF * half:HALF * half + HALF].unsqueeze(1)
                                    .to_broadcast([P, H, HALF]), ALU.mult).then_inc(dve_qc, 1)
                v.tensor_tensor(q_sq[:], q_n[:], q_cos[:].unsqueeze(1).to_broadcast([P, H, HD]), ALU.mult
                                ).then_inc(dve_q, 1)
                dve.wait_ge(dve_q, 6 * m + 5)
                dve.wait_ge(dve_qc, 3 * m + 3)
                v.tensor_tensor(q_rot[:], q_rot[:], q_sq[:], ALU.add).then_inc(dve_q, 1)

            def masks(m, b):
                dve.wait_ge(act_far, 2 * m + b + 1)
                v.tensor_scalar(mask[b][:], far2[:], float(WINDOW // 2) ** 2, NEG, ALU.is_gt, ALU.mult
                                ).then_inc(dve_mask, 1)

            def maxima(m, u):
                b = u // 4
                wait(dve, act_e, 8 * m + u - 1)
                dve.wait_ge(dve_mask, 2 * m + b + 1)
                wait(dve, pe_sc, 8 * m + u + 1, dve_mark)
                v.tensor_tensor_reduce(sm[u % 2][:], score[u % 2], mask[b][:], 1.0, NEG * 4, ALU.add, ALU.max,
                                       top[u % 2][:]).then_inc(dve_sm, 1)
                dve.wait_ge(dve_sm, 8 * m + u + 1)
                v.tensor_scalar(ntop[u % 2][:], top[u % 2][:], -SCALE, None, ALU.mult).then_inc(dve_nt, 1)

            def norms(m, u):
                dve.wait_ge(act_e, 8 * m + u + 1)
                v.reciprocal(share[u % 2][:], total[u % 2][:]).then_inc(dve_sh, 1)
                dve.wait_ge(dve_sh, 8 * m + u + 1)
                v.tensor_scalar(prob[u % 2][:], prob[u % 2][:], share[u % 2][:], None, ALU.mult).then_inc(dve_p, 1)

            def router_score(m, h):
                dve.wait_ge(act_a, m + 1)
                v.tensor_tensor_reduce(r_junk[:], a_sb[h][:], w_r[:], 1.0, 0.0, ALU.mult, ALU.add, r_s[:]
                                       ).then_inc(dve_rc, 1)
                dve.wait_ge(dve_rc, 6 * m + 1)
                v.tensor_tensor(r_s[:], r_s[:], b_r[:], ALU.add).then_inc(dve_rc, 1)
                dve.wait_ge(dve_rc, 6 * m + 2)
                v.tensor_scalar(r_diag[:], ident[:], r_s[:], None, ALU.mult).then_inc(dve_diag, 1)

            def router_keep(m, h):
                row = a_bank[:, 0:P]
                dve.wait_ge(pe_row, m + 1)
                v.tensor_tensor_reduce(r_junk[:, 0:P], row, ident[:], 1.0, 0.0, ALU.mult, ALU.add, r_own[:]
                                       ).then_inc(dve_rc, 1)
                dve.wait_ge(dve_rc, 6 * m + 3)
                v.scalar_tensor_tensor(r_junk[:, P:2 * P], row, r_own[:], own[:], ALU.is_gt, ALU.mult,
                                       accum_out=r_gt[:]).then_inc(dve_rc, 1)
                v.scalar_tensor_tensor(r_junk[:, 2 * P:3 * P], row, r_own[:], before[:], ALU.is_equal, ALU.mult,
                                       accum_out=r_eq[:]).then_inc(dve_rc, 1)
                dve.wait_ge(dve_rc, 6 * m + 5)
                v.tensor_tensor(r_rank[:], r_gt[:], r_eq[:], ALU.add).then_inc(dve_rc, 1)
                dve.wait_ge(dve_rc, 6 * m + 6)
                v.tensor_scalar(keep[h][:], slot_no[:], r_rank[:], None, ALU.is_equal).then_inc(dve_keep, 1)

            def pair(m, i, h, last, nxt):
                for u in range(8):
                    if u < 7:
                        maxima(m, u + 1)
                    elif nxt:
                        maxima(m + 1, 0)
                    norms(m, u)
                    if u == 0:
                        masks(m, 1)
                        if nxt:
                            query_squares(m + 1)
                    if u == 1 and last:
                        router_score(m - 1, 1 - h)
                    if u == 2 and nxt:
                        queries(m + 1, 1 - h)
                    if u == 3 and last:
                        router_keep(m - 1, 1 - h)
                    if u == 4 and nxt:
                        masks(m + 1, 0)

            query_squares(0)
            queries(0, 0)
            masks(0, 0)
            maxima(0, 0)
            pairs(dve, pair)
            router_score(NG - 1, 1)
            router_keep(NG - 1, 1)

        @block.tensor
        def _(pe):
            pe.wait_ge(s_c, 16 * NC)
            pe.wait_ge(c_dve, C_IDS)
            nc.tensor.matmul(q_bank[0:NSLOT, 0:B], win[0:B, :], ident[0:B, 0:B], start=True, stop=True)
            nc.tensor.matmul(q_bank[0:NWC, P:2 * P], wid[:], ident[:], start=True, stop=True).then_inc(c_pe, 1)
            pe.wait_ge(c_dve, C_BEATS)
            for c in range(NWC):
                for c2 in range(NWC):
                    mm = nc.tensor.matmul(q_bank[:, BLOCK * c:BLOCK * c + BLOCK], beats[:, c2, P * c:P * c + P],
                                          cover[:, c2, :], start=(c2 == 0), stop=(c2 == NWC - 1))
            mm.then_inc(c_pe, 1)
            pe.wait_ge(c_dve, C_PLACED)
            for n in range(SC * NWC):
                j, c = n // NWC, n % NWC
                mm = nc.tensor.matmul(k_bank[0][0:KC, 0:NKC * B], placed[:, c, j, :],
                                      match[:, c, :].rearrange("p (c j b) -> p j c b", c=NKC, j=SC)[:, j, :, :],
                                      start=(n == 0), stop=(n == SC * NWC - 1))
            mm.then_inc(c_pe, 1)

            def turn_q(m, h):
                pe.wait_ge(dve_q, 6 * (m + 1))
                wait(pe, act_qt, 2 * m)
                qv = q_rot[:].rearrange("p h d -> p (h d)")
                for c in range(4):
                    mm = nc.tensor.transpose(q_bank[:, P * c:P * c + P], qv[:, P * c:P * c + P], ident[:])
                mm.then_inc(pe_q, 1)

            def turn_k(m, i, h, b):
                s = 2 * h + b
                pe.wait_ge(ld_kv[s], 16 * NKC * (i + 1))
                wait(pe, act_kt, 2 * (2 * m + b))
                for gp in range(2):
                    for c in range(NKC):
                        mm = nc.tensor.transpose(k_bank[gp][:, KC * c:KC * c + KC],
                                                 kv[s][:, c, P * gp:P * gp + P], ident[0:KC, 0:KC])
                mm.then_inc(pe_k, 1)

            def scores(m, h, u):
                b, gp, gq = unit(u)
                rows = slice(64 * gq, 64 * gq + 64)
                if u == 0:
                    pe.wait_ge(act_qt, 2 * (m + 1))
                if u % 4 == 0:
                    pe.wait_ge(act_kt, 2 * (2 * m + b + 1))
                wait(pe, dve_sm, 8 * m + u - 1)
                nc.tensor.matmul(score[u % 2], q_t[h][rows, gp, b, :, :].rearrange("p j t -> p (j t)"),
                                 k_t[b][rows, gp, :], start=True, stop=True).then_inc(pe_sc, 1)

            def turn_p(m, u):
                pe.wait_ge(dve_p, 8 * m + u + 1)
                wait(pe, act_pt, 8 * m + u)
                for c in range(NKC):
                    mm = nc.tensor.transpose(p_bank[:, P * c:P * c + P], prob[u % 2][:, KC * c:KC * c + KC], ident[:])
                mm.then_inc(pe_pt, 1)

            def values(m, h, u):
                b, gp, gq = unit(u)
                g = 2 * gp + gq
                pe.wait_ge(act_pt, 8 * m + u + 1)
                if u == 0:
                    wait(pe, act_o, m)
                for c in range(NKC):
                    mm = nc.tensor.matmul(o_bank[64 * gq:64 * gq + 64, 2 * gp:2 * gp + 2, T * b:T * b + T],
                                          kv[2 * h + b][:, c, G * HD + HD * g:G * HD + HD * g + HD],
                                          p_t[u % 2][:, c, :].rearrange("p (j t) -> p j t", j=2),
                                          start=(c == 0), stop=(c == NKC - 1))
                mm.then_inc(pe_pv, 1)

            def project(m, h):
                pe.wait_ge(act_o, m + 1)
                wait(pe, act_xs, 2 * m)
                for c in range(4):
                    mm = nc.tensor.matmul(a_bank, o_t[h][:, c, :], w_o[:, c, :], start=(c == 0), stop=(c == 3))
                mm.then_inc(pe_a, 1)

            def router_row(m):
                pe.wait_ge(act_a, m + 1)
                pe.wait_ge(dve_diag, m + 1)
                nc.tensor.matmul(a_bank[:, 0:P], ones[:], r_diag[:], start=True, stop=True).then_inc(pe_row, 1)

            def router_take(m, h):
                pe.wait_ge(dve_keep, m + 1)
                nc.tensor.matmul(a_bank[64 * h:64 * h + 64, P:2 * P], keep[h][:], ident[:], start=True, stop=True)
                for c in range(NCH):
                    mm = nc.tensor.matmul(a_bank[:, 2 * P + 2 * SEL * c:2 * P + 2 * SEL * c + 2 * SEL],
                                          a_sb[h][:, P * c:P * c + P], keep[h][:], start=True, stop=True)
                mm.then_inc(pe_xs, 1)

            def pair(m, i, h, last, nxt):
                i1 = i if h == 0 else i + 1
                for u in range(8):
                    if u < 7:
                        scores(m, h, u + 1)
                    elif nxt:
                        scores(m + 1, 1 - h, 0)
                    if u == 1:
                        turn_k(m, i, h, 1)
                    if u == 2 and last:
                        router_row(m - 1)
                    if u == 3 and nxt:
                        turn_q(m + 1, 1 - h)
                    if u == 4 and last:
                        router_take(m - 1, 1 - h)
                    if u == 5 and nxt:
                        turn_k(m + 1, i1, 1 - h, 0)
                    if u > 0:
                        values(m, h, u - 1)
                    turn_p(m, u)
                values(m, h, 7)
                project(m, h)

            pe.wait_ge(filled, 2)
            pe.wait_ge(idx_ok, 2)
            turn_q(0, 0)
            turn_k(0, 0, 0, 0)
            scores(0, 0, 0)
            pairs(pe, pair)
            router_row(NG - 1)
            router_take(NG - 1, 1)


C_MASK = 15
C_IDS = C_MASK + 2 + NSLOT + NWC
C_TURNED = C_IDS + 4 + 2
C_BEATS = C_TURNED + 2 * NWC
C_PLACED = C_BEATS + 1 + SC


def ffn_block(nc, A, S, out):
    NS = NG * 2 * SEL // TILE
    NTT = TILE // P
    with ExitStack() as ctx:
        def sb(name, shape, dt=F32):
            return ctx.enter_context(nc.sbuf_tensor(name, shape, dt))

        def sem(name):
            return ctx.enter_context(nc.semaphore(name))

        psum = ctx.enter_context(nc.psum_tensor("ffn_psum", [P, 8, 512], F32))
        h_bank = [psum[:, i, :] for i in range(3)]
        y_bank = [psum[:, 3 + i, :] for i in range(2)]
        s_bank = [psum[:, 5 + i, :] for i in range(3)]

        w1 = sb("w1", [P, NCH, DF])
        w2 = sb("w2", [P, NF, D])
        b1 = sb("b1", [P, NF])
        b2 = sb("b2", [P, D])
        xs = sb("xs_in", [P, NCH, TILE])
        hid = sb("ffn_hid", [P, NF, TILE])
        y_sb = [sb(f"y_sb{i}", [P, D]) for i in range(2)]
        keep_t = [sb(f"keep_in{i}", [P, P]) for i in range(2)]
        x1 = [sb(f"x1_in{i}", [P, NCH, P]) for i in range(2)]
        res = [sb(f"res{i}", [P, NCH, P]) for i in range(2)]

        s_w = [sem(f"s_w{i}") for i in range(3)]
        ld_xs = sem("ld_xs")
        ld_keep = [sem(f"ld_keep{i}") for i in range(2)]
        ld_x1 = [sem(f"ld2_x1{i}") for i in range(2)]
        st_res = [sem(f"st_res{i}") for i in range(2)]
        pe_h, pe_y, pe_s = sem("pe_h"), sem("pe2_y"), sem("pe_s")
        act_h, dve_y, dve_r, sp_mark = sem("act_h"), sem("dve_y"), sem("dve_r"), sem("sp_mark3")

        block = ctx.enter_context(nc.Block())

        @block.sync
        def _(sp):
            sp.dma_start(w1[:], A["w1"]).then_inc(s_w[0], 16)
            sp.dma_start(b1[:], A["b1"]).then_inc(s_w[0], 16)
            sp.dma_start(xs[:], S["xsp"][:, :, 0:TILE]).then_inc(ld_xs, 16)
            sp.dma_start(w2[:], A["w2"]).then_inc(s_w[1], 16)
            sp.dma_start(b2[:], A["b2"].partition_broadcast(P)).then_inc(s_w[1], 16)

            def loads(n, p):
                wait(sp, pe_s, 2 * (n - 1), sp_mark)
                sp.dma_start(keep_t[p][:], S["keep"][bass.ds(2 * n, 2)].rearrange("j s t -> (j s) t")
                             ).then_inc(ld_keep[p], 16)

            def tile(s, tt, more):
                n, p = NTT * s + tt, tt % 2
                loads(n, p)
                if more and tt == 0:
                    wait(sp, pe_h, NF * (s + 1), sp_mark)
                    sp.dma_start(xs[:], S["xsp"][:, :, bass.ds((s + 1) * TILE, TILE)]).then_inc(ld_xs, 16)
                for j in range(2):
                    wait(sp, dve_r, 2 * n + j - 1, sp_mark)
                    sp.dma_start(x1[j][:], S["x1p"][:, :, bass.ds((2 * n + j) * GRP, GRP)]).then_inc(ld_x1[j], 16)
                for j in range(2):
                    wait(sp, dve_r, 2 * n + j + 1, sp_mark)
                    sp.dma_start(out.rearrange("c p t -> p c t")[:, :, bass.ds((2 * n + j) * GRP, GRP)],
                                 res[j][:]).then_inc(st_res[j], 16)

            for tt in range(NTT):
                tile(0, tt, True)
            with sp.Fori(1, NS - 1) as s:
                for tt in range(NTT):
                    tile(s, tt, True)
            for tt in range(NTT):
                tile(NS - 1, tt, False)
            for j in range(2):
                sp.wait_ge(st_res[j], 16 * NG // 2)

        @block.scalar
        def _(act):
            act.wait_ge(s_w[0], 32)

            def tile(s):
                for f in range(NF):
                    k = NF * s + f
                    act.wait_ge(pe_h, k + 1)
                    if f == 0:
                        wait(act, pe_y, NTT * s)
                    nc.scalar.activation(hid[:, f, :], h_bank[f % 2], ACT.Gelu_apprx_tanh, bias=b1[:, f:f + 1]
                                         ).then_inc(act_h, 1)

            tile(0)
            with act.Fori(1, NS) as s:
                tile(s)

        @block.vector
        def _(dve):
            dve.wait_ge(s_w[1], 32)

            def tile(s, tt):
                n, p = NTT * s + tt, tt % 2
                dve.wait_ge(pe_y, n + 1)
                wait(dve, pe_s, 2 * (n - 1))
                nc.vector.tensor_tensor(y_sb[p][:], y_bank[p], b2[:], ALU.add).then_inc(dve_y, 1)
                for j in range(2):
                    dve.wait_ge(pe_s, 2 * n + j + 1)
                    dve.wait_ge(ld_x1[j], 16 * (n + 1))
                    wait(dve, st_res[j], 16 * n)
                    nc.vector.tensor_tensor(res[j][:].rearrange("p c t -> p (c t)"), s_bank[j],
                                            x1[j][:].rearrange("p c t -> p (c t)"), ALU.add).then_inc(dve_r, 1)

            for tt in range(NTT):
                tile(0, tt)
            with dve.Fori(1, NS) as s:
                for tt in range(NTT):
                    tile(s, tt)

        @block.tensor
        def _(pe):
            pe.wait_ge(s_w[0], 32)

            def tile(s):
                pe.wait_ge(ld_xs, 16 * (s + 1))
                for f in range(NF):
                    k = NF * s + f
                    wait(pe, act_h, k - 1)
                    for c in range(NCH):
                        mm = nc.tensor.matmul(h_bank[f % 2], w1[:, c, P * f:P * f + P], xs[:, c, :],
                                              start=(c == 0), stop=(c == NCH - 1))
                    mm.then_inc(pe_h, 1)
                pe.wait_ge(s_w[1], 32)
                for tt in range(NTT + 1):
                    if tt < NTT:
                        n, p = NTT * s + tt, tt % 2
                        wait(pe, dve_y, n - 1)
                        for f in range(NF):
                            if tt == 0:
                                pe.wait_ge(act_h, NF * s + f + 1)
                            mm = nc.tensor.matmul(y_bank[p], hid[:, f, P * tt:P * tt + P], w2[:, f, :],
                                                  start=(f == 0), stop=(f == NF - 1))
                        mm.then_inc(pe_y, 1)
                    if tt > 0:
                        scatter(NTT * s + tt - 1, (tt - 1) % 2, 2 * s + (tt - 1) // 2)

            def scatter(n, p, uses):
                pe.wait_ge(dve_y, n + 1)
                pe.wait_ge(ld_keep[p], 16 * (uses + 1))
                for j in range(2):
                    rows = slice(64 * j, 64 * j + 64)
                    wait(pe, dve_r, 2 * n + j - 1)
                    for c in range(NCH):
                        mm = nc.tensor.matmul(s_bank[j][:, P * c:P * c + P], y_sb[p][rows, P * c:P * c + P],
                                              keep_t[p][rows, :], start=True, stop=True)
                    mm.then_inc(pe_s, 1)

            tile(0)
            with pe.Fori(1, NS) as s:
                tile(s)


def program(nc, A, out):
    S = {}
    S["u"] = nc.dram_tensor("u_scratch", [NCH, P, NTOK], F32).ap()
    S["delta"] = nc.dram_tensor("delta_scratch", [NCH, P, NTOK], F32).ap()
    S["x1"] = nc.dram_tensor("x1_scratch", [NCH, P, NTOK], F32).ap()
    for name in ("u", "delta", "x1"):
        S[name + "p"] = S[name].rearrange("c p t -> p c t")
    S["bc"] = nc.dram_tensor("bc_scratch", [2 * NST, NTOK], F32).ap()
    S["q"] = nc.dram_tensor("q_scratch", [NTOK, H * HD], F32).ap()
    S["kv_new"] = nc.dram_tensor("kv_scratch", [NTOK, KV], F32).ap()
    S["cos"] = nc.dram_tensor("cos_scratch", [P, NG * HALF], F32).ap()
    S["sin"] = nc.dram_tensor("sin_scratch", [P, NG * HALF], F32).ap()
    S["win"] = nc.dram_tensor("win_scratch", [NSLOT, B], F32).ap()
    S["wid"] = nc.dram_tensor("wid_scratch", [NWC, P], F32).ap()
    S["keep"] = nc.dram_tensor("keep_scratch", [NG, 2 * SEL, P], F32).ap()
    S["xs"] = nc.dram_tensor("xs_scratch", [NCH, P, NG * 2 * SEL], F32).ap()
    S["xsp"] = S["xs"].rearrange("c p t -> p c t")
    scan_block(nc, A, S)
    attention_block(nc, A, S)
    ffn_block(nc, A, S, out)


def layouts(inp):
    f = np.ascontiguousarray
    a = {}
    x = inp["x"]
    a["x_pairs"] = f(x.reshape(NG, P, D))
    a["x_t"] = f(x.reshape(NTOK, NCH, P).transpose(1, 2, 0))
    a["w_cond"] = f(inp["L0_cond_weights"].reshape(-1, HD))
    a["cond"] = f(inp["itok_B_1_198"].reshape(NG, 2).T)
    a["lens_pair"] = f(inp["itok_B_37_3939"].reshape(NG, 2).T)
    a["a_log"] = f(inp["L0_attn_A_log"].reshape(NCH, P, NST).transpose(1, 0, 2).reshape(P, -1))
    a["skip_d"] = f(inp["L0_attn_D"].reshape(NCH, P).T)
    a["dt_bias"] = f(inp["L0_attn_dt_proj_b"].reshape(NCH, P).T)
    wx = inp["L0_attn_x_proj_w"]
    wx = np.concatenate([wx[:P], wx[P:].reshape(2, NST, D).transpose(1, 0, 2).reshape(2 * NST, D)])
    a["w_x"] = f(wx.T.reshape(NCH, P, 160).transpose(1, 0, 2))
    a["w_dt"] = f(inp["L0_attn_dt_proj_w"].T)
    wq = inp["L0_cond2_Wq"].reshape(2, 2, 2, HD, D).transpose(0, 2, 1, 3, 4).reshape(D, D)
    w = np.concatenate([wq, inp["L0_cond2_Wk"], inp["L0_cond2_Wv"]])
    a["w_qkv"] = f(w.T.reshape(NCH, P, 1024).transpose(1, 0, 2))
    ks = inp["L0_cond2_k_norm_scale"]
    a["k_scale2"] = f(np.stack([ks, np.concatenate([ks[HALF:], ks[:HALF]])]))
    a["ident"] = np.eye(P, dtype=np.float32)
    a["part"] = f(np.stack([np.arange(P) % T, np.zeros(P)], 1).astype(np.float32))
    qs = inp["L0_cond2_q_norm_scale"]
    a["q_scale2"] = f(np.stack([qs, np.concatenate([qs[HALF:], qs[:HALF]])]))
    wo = inp["L0_cond2_Wo"].T.reshape(2, 2, 2, HD, D).transpose(0, 2, 1, 3, 4).reshape(NCH, P, D)
    a["w_o"] = f(wo.transpose(1, 0, 2))
    kb = inp["L0_cond2_k_blocks"].transpose(0, 2, 1, 3).reshape(NROW, G * HD)
    vb = inp["L0_cond2_v_blocks"].transpose(0, 2, 1, 3).reshape(NROW, G * HD)
    a["kv_rows"] = f(np.concatenate([kb, vb], axis=1))
    a["table"] = f(inp["itok_Bx257_0_4111"])
    a["lens"] = f(inp["itok_B_37_3939"].reshape(B, 1))
    a["lens_row"] = f(inp["itok_B_37_3939"])
    a["w_r"] = f(inp["L0_ffn_w_r"])
    a["b_r"] = f(inp["L0_ffn_b_r"].reshape(1))
    a["w1"] = f(inp["L0_ffn_w1"].reshape(NCH, P, DF).transpose(1, 0, 2))
    a["w2"] = f(inp["L0_ffn_w2"].reshape(NF, P, D).transpose(1, 0, 2))
    a["b1"] = f(inp["L0_ffn_b1"].reshape(NF, P).T)
    a["b2"] = f(inp["L0_ffn_b2"])

    p = np.arange(P)
    half, seq = p // T, p % T
    slot = 2 * np.arange(NWC) + half[:, None]
    a["ids"] = f(np.broadcast_to(np.arange(NBLK, dtype=np.float32), (P, NBLK)))
    a["w_slot0"] = f(slot.astype(np.float32))
    a["tau0"] = f((BLOCK * slot[:, :, None] + np.arange(BLOCK)).astype(np.float32))
    a["tok0"] = f((T * seq + 1).astype(np.float32)[:, None])
    a["off_in"] = f((p % BLOCK).astype(np.float32)[:, None])
    order = seq[:, None] * 8 + slot
    a["later"] = f((order[:, :, None] > order.T.reshape(-1)).astype(np.float32))
    a["dist"] = f((np.arange(NKEY) - seq[:, None]).astype(np.float32))
    same = half[:, None] == half
    a["own"] = f(same.astype(np.float32))
    a["before"] = f((same & (p < p[:, None])).astype(np.float32))
    at = np.arange(2 * SEL)
    a["slot_no"] = f(np.where(at // SEL == half[:, None], at % SEL, -1).astype(np.float32))
    a["inv_freq"] = (1.0 / np.float32(10000.0) ** (np.arange(HALF, dtype=np.float32) / HALF)).astype(np.float32)
    return a


def kernel(**inputs):
    import concourse.bacc as _bacc
    from concourse.bass_utils import run_bass_kernel_spmd as _run

    nc = _bacc.Bacc("TRN2", target_bir_lowering=False, num_devices=1)
    arrays = layouts({k: np.asarray(v) for k, v in inputs.items()})
    aps = {n: nc.dram_tensor(f"in_{n}", v.shape, mybir.dt.from_np(v.dtype), kind="ExternalInput").ap()
           for n, v in arrays.items()}
    out = nc.dram_tensor("out_t", (NCH, P, NTOK), F32, kind="ExternalOutput").ap()
    program(nc, aps, out)
    r = _run(nc, [{f"in_{n}": v for n, v in arrays.items()}], core_ids=[0])
    return np.ascontiguousarray(r.results[0]["out_t"].transpose(2, 0, 1).reshape(B, T, D))
```

```python
from contextlib import ExitStack

import numpy as np

import concourse.bass as bass
from concourse import mybir

F32 = mybir.dt.float32
I32 = mybir.dt.int32
ALU = mybir.AluOpType
ACT = mybir.ActivationFunctionType
AX = mybir.AxisListType

P = 128
B, T, D = 64, 64, 512
NTOK = B * T
NCH = D // P
NST = 16
TILE = 512
NT = NTOK // TILE
BT = TILE // T
GRP = 128
NG = NTOK // GRP
H, G, HD = 8, 4, 64
HALF = HD // 2
BLOCK, WINDOW, NBLK = 16, 256, 257
NROW = B // 4 * NBLK * BLOCK
KV = 2 * G * HD
SCALE = 256.0 ** -0.5
EPS = 1e-6
NBUF = 8
NCONST = 11
NSLOT = 21
SC = 7
KC = SC * BLOCK
NKC = NSLOT // SC
NKEY = NSLOT * BLOCK
NWS = 6
NWC = NWS // 2
SEL = T // 2
DF = 4 * D
NF = DF // P
NEG = -1.0e30
FAR = 1.0e6
MAGIC = 12582912.0
TWO_PI = (6.28125, 1.9340515136718750e-03, 1.2556659146e-06)


def wait(eng, sem, value, mark=None):
    if isinstance(value, int) and value <= 0:
        return
    eng.wait_ge(sem, value)
    if mark and not isinstance(value, int):
        eng.sem_inc(mark, 1)


def half(t, k):
    return 2 * t + k // 2


def scan_block(nc, A, S):
    with ExitStack() as ctx:
        def sb(name, shape, dt=F32):
            return ctx.enter_context(nc.sbuf_tensor(name, shape, dt))

        def sem(name):
            return ctx.enter_context(nc.semaphore(name))

        psum = ctx.enter_context(nc.psum_tensor("scan_psum", [P, 8, 512], F32))
        y = [psum[:, c, :] for c in range(NCH)]
        pro = [psum[:, 4 + i, :] for i in range(2)]
        qk = [psum[:, 6 + i, :] for i in range(2)]

        ident = sb("ident", [P, P])
        neg_a = sb("neg_a", [P, NCH * NST])
        a_log = sb("a_log", [P, NCH * NST])
        skip_d = sb("skip_d", [P, NCH])
        dt_bias = sb("dt_bias", [P, NCH])
        w_x = sb("w_x", [P, NCH, 160])
        w_dt = sb("w_dt", [P, D])
        w_qkv = sb("w_qkv", [P, NCH, 1024])
        bc = [sb(f"bc{i}", [P, 4, 2, TILE]) for i in range(2)]
        u = [sb(f"u{i}", [P, NCH, TILE]) for i in range(2)]
        delta = [sb(f"delta{i}", [P, NCH, TILE]) for i in range(2)]
        du = [sb(f"du{c}", [P, TILE]) for c in range(NCH)]
        xt_in = [sb(f"xt_in{i}", [P, TILE]) for i in range(2)]
        resid = [sb(f"resid{i}", [P, TILE]) for i in range(2)]
        x1 = [sb(f"x1_{c}", [P, TILE]) for c in range(NCH)]
        decay = [sb(f"decay{i}", [P, TILE]) for i in range(NBUF)]
        dbu = sb("dbu", [P, 4, TILE])
        hid = sb("hid", [P, NBUF, TILE])
        hc = [sb(f"hc{i}", [P, TILE]) for i in range(NBUF)]

        x_pair = [sb(f"x_pair{i}", [P, D]) for i in range(2)]
        w_rows = [sb(f"w_rows{i}", [P, HD]) for i in range(2)]
        w_pair = [sb(f"w_pair{i}", [P, 2 * HD]) for i in range(2)]
        drg = sb("drg", [P, GRP])
        bcg = [sb(f"bcg{i}", [32, GRP]) for i in range(2)]
        zg = sb("zg", [P, NCH, GRP])
        sp_a = sb("sp_a", [P, NCH, GRP])
        sp_l = sb("sp_l", [P, NCH, GRP])

        qg = [sb(f"qg{i}", [P, H * HD]) for i in range(2)]
        kvg = [sb(f"kvg{i}", [P, KV]) for i in range(2)]
        k_raw = sb("k_raw", [P, G, HD])
        k_sq = sb("k_sq", [P, G, HD])
        k_n = sb("k_n", [P, G, HD])
        k_rot = sb("k_rot", [P, G, HD])
        k_par = sb("k_par", [P, G, HD])
        k_ss = sb("k_ss", [P, G])
        k_ms = sb("k_ms", [P, G])
        k_ln = sb("k_ln", [P, G])
        k_r0 = sb("k_r0", [P, G])
        k_r2 = sb("k_r2", [P, G])
        k_r3 = sb("k_r3", [P, G])
        k_rs = sb("k_rs", [P, G])
        k_cos = sb("k_cos", [P, HD])
        k_sin = sb("k_sin", [P, HD])
        k_scale = sb("k_scale", [P, 2, HD])
        one_ks = sb("one_ks", [P, 2, HD])

        cond_i = sb("cond_i", [P, NG], I32)
        len_i = sb("len_i", [P, NG], I32)
        cond_f = sb("cond_f", [P, NG])
        pos_f = sb("pos_f", [P, NG])
        part = sb("part", [P, 2])
        inv = sb("inv", [P, HALF])
        w_idx = sb("w_idx", [P, NG], I32)
        w_now = [sb(f"w_now{i}", [P, 1], I32) for i in range(2)]
        ang, turns, rem = (hid[:, 2 * i:2 * i + 2, :].rearrange("p a b -> p (a b)") for i in range(3))
        cos = sb("cos", [P, NG * HALF])
        sin = sb("sin", [P, NG * HALF])

        s_cond, s_const, s_qkvw = sem("s_cond"), sem("s_const"), sem("s_qkvw")
        c_a, c_neg, c_dve, c_sin = sem("c_a"), sem("c_neg"), sem("c_dve"), sem("c_sin")
        widx_ok, wnow_ok, wpair_ok = sem("widx_ok"), sem("wnow_ok"), sem("wpair_ok")
        rope_ok, zero_ok, zpair_ok = sem("rope_ok"), sem("zero_ok"), sem("zpair_ok")
        ld_xp = [sem(f"ld_xp{i}") for i in range(2)]
        ld_w = [sem(f"ld_w{i}") for i in range(2)]
        ld_xt = [sem(f"ld_xt{i}") for i in range(2)]
        ld_bc = [sem(f"ld_bc{i}") for i in range(2)]
        st_bc = [sem(f"st_bc{i}") for i in range(4)]
        st_x1 = [sem(f"st_x1{i}") for i in range(NCH)]
        st_q = [sem(f"st_q{i}") for i in range(2)]
        st_kv = [sem(f"st_kv{i}") for i in range(2)]
        st_rope = sem("st_rope")
        pe_u, pe_x, pe_z, pe_res = sem("pe_u"), sem("pe_x"), sem("pe_z"), sem("pe_res")
        pe_hc, pe_kv, pe_q = sem("pe_hc"), sem("pe_kv"), sem("pe_q")
        act_u, act_dr, act_sp = sem("act_u"), sem("act_dr"), sem("act_sp")
        act_exp, act_y, act_kv, act_q = sem("act_exp"), sem("act_y"), sem("act_kv"), sem("act_q")
        dve_du, dve_res, dve_dbu, dve_h = sem("dve_du"), sem("dve_res"), sem("dve_dbu"), sem("dve_h")
        dve_z, dve_dl, dve_ks, dve_kt = sem("dve_z"), sem("dve_dl"), sem("dve_ks"), sem("dve_kt")
        dve_ms, act_rs = sem("dve_ms"), sem("act_rs")
        pool_hc, pool_k = sem("pool_hc"), sem("pool_k")
        sp_mark, pool_mark = sem("sp_mark"), sem("pool_mark")

        block = ctx.enter_context(nc.Block())

        class Parts:

            def __init__(self, t, q):
                s = 4 * t + q if isinstance(t, int) else None

                def within(lo, hi):
                    return s is None or lo <= s <= hi

                self.scan = within(0, 4 * NT - 1)
                self.next_scan = within(-1, 4 * NT - 2)
                self.gather = within(-6, NG - 7)
                self.first = within(-5, NG - 6)
                self.second = within(-4, NG - 5)
                self.third = within(4, NG + 3)
                self.fourth = within(5, NG + 4)

        def quarters(eng, quarter):
            def run(t, h, some=range(4)):
                for q in some:
                    quarter(t, h, q, Parts(t, q))

            run(-2, 0, [3])
            run(-1, 1)
            run(0, 0)
            run(1, 1)
            with eng.Fori(1, NT // 2 - 1) as i:
                run(2 * i, 0)
                run(2 * i + 1, 1)
            run(NT - 2, 0)
            run(NT - 1, 1)
            run(NT, 0)
            run(NT + 1, 1, [0])

        @block.sync
        def _(sp):
            def load_x(g, p):
                wait(sp, pe_u, g - 1, sp_mark)
                sp.dma_start(x_pair[p][:], A["x_pairs"][g]).then_inc(ld_xp[p], 16)

            for h in range(2):
                rows = slice(64 * h, 64 * h + 64)
                sp.dma_start(cond_i[rows, :], A["cond"][h].partition_broadcast(64)).then_inc(s_cond, 16)
            sp.dma_start(part[:], A["part"]).then_inc(s_cond, 16)
            load_x(0, 0)
            for dst, src in ((w_x, A["w_x"]), (w_dt, A["w_dt"]), (dt_bias, A["dt_bias"]), (a_log, A["a_log"]),
                             (skip_d, A["skip_d"]), (ident, A["ident"])):
                sp.dma_start(dst[:], src).then_inc(s_const, 16)
            sp.dma_start(inv[:], A["inv_freq"].partition_broadcast(P)).then_inc(s_const, 16)
            for h in range(2):
                rows = slice(64 * h, 64 * h + 64)
                sp.dma_start(len_i[rows, :], A["lens_pair"][h].partition_broadcast(64)).then_inc(s_const, 16)
            for i in range(2):
                sp.dma_start(k_scale[:, i, :], A["k_scale2"][i].partition_broadcast(P)).then_inc(s_const, 16)

            def load_bc(t, q):
                if q == 0:
                    for i in range(4):
                        wait(sp, st_bc[i], 16 * (t + 1), sp_mark)
                wait(sp, pool_hc, 16 * (4 * t + q - 1), sp_mark)
                sp.dma_start(bc[q % 2][:].rearrange("p a b c -> p (a b) c"),
                             S["bc"][8 * q:8 * q + 8, bass.ds(t * TILE, TILE)].partition_broadcast(P)
                             ).then_inc(ld_bc[q % 2], 16)

            def load_xt(t, c):
                wait(sp, dve_res, 4 * t + c - 1, sp_mark)
                sp.dma_start(xt_in[c % 2][:], A["x_t"][c][:, bass.ds(t * TILE, TILE)]).then_inc(ld_xt[c % 2], 16)

            def store_x1(t, c):
                wait(sp, act_y, 4 * t + c + 1, sp_mark)
                sp.dma_start(S["x1"][c][:, bass.ds(t * TILE, TILE)], x1[c][:]).then_inc(st_x1[c], 16)

            def quarter(t, h, q, parts):
                s = 4 * t + q
                if parts.gather:
                    load_x(s + 6, q % 2)
                if parts.next_scan:
                    load_bc(t if q < 3 else t + 1, (q + 1) % 4)
                if q == 3 and parts.next_scan:
                    load_xt(t + 1, 0)
                    load_xt(t + 1, 1)
                if q == 0 and parts.third:
                    store_x1(t - 1, 3)
                if parts.fourth:
                    g, p = s - 5, (q + 1) % 2
                    wait(sp, act_q, g + 1, sp_mark)
                    sp.dma_start(S["q"][bass.ds(g * GRP, GRP), :], qg[p][:]).then_inc(st_q[p], 16)
                if q == 0 and parts.scan:
                    load_xt(t, 2)
                    load_xt(t, 3)
                if parts.first:
                    g = s + 5
                    wait(sp, act_dr, 2 * (g + 1), sp_mark)
                    sp.dma_start(S["bc"][:, bass.ds(g * GRP, GRP)], bcg[(q + 1) % 2][:]
                                 ).then_inc(st_bc[(q + 1) % 4], 16)
                if isinstance(t, int) and t == -1 and q == 0:
                    sp.dma_start(w_qkv[:], A["w_qkv"]).then_inc(s_qkvw, 16)
                if parts.fourth:
                    wait(sp, pool_k, 5 * (g_kv(t, q) + 1), sp_mark)
                    sp.dma_start(S["kv_new"][bass.ds(g_kv(t, q) * GRP, GRP), :], kvg[(q + 1) % 2][:]
                                 ).then_inc(st_kv[(q + 1) % 2], 16)
                if q == 3 and parts.scan:
                    for c in range(3):
                        store_x1(t, c)

            def g_kv(t, q):
                return 4 * t + q - 5

            quarters(sp, quarter)
            sp.wait_ge(rope_ok, 1)
            sp.dma_start(S["cos"], cos[:]).then_inc(st_rope, 16)
            sp.dma_start(S["sin"], sin[:]).then_inc(st_rope, 16)
            sp.wait_ge(st_rope, 32)
            for c in range(NCH):
                sp.wait_ge(st_x1[c], 16 * NT)
            for i in range(2):
                sp.wait_ge(st_q[i], 16 * NG // 2)
                sp.wait_ge(st_kv[i], 16 * NG // 2)

        @block.gpsimd
        def _(pool):
            def weights(g, p):
                wait(pool, wpair_ok, 2 * g - 2, pool_mark)
                pool.tensor_copy(w_now[p][:], w_idx[:, bass.ds(g, 1)]).then_inc(wnow_ok, 1)
                wait(pool, wnow_ok, g + 1, pool_mark)
                pool.indirect_dma_start(w_rows[p][:], None, A["w_cond"],
                                        bass.IndirectOffsetOnAxis(ap=w_now[p][:, :], axis=0)
                                        ).then_inc(ld_w[p], 16)

            def keys(g, p):
                k = 5 * g
                pool.wait_ge(dve_ks, g + 1)
                pool.tensor_tensor(k_n[:], k_raw[:], k_rs[:].unsqueeze(2).to_broadcast([P, G, HD]),
                                   ALU.mult).then_inc(pool_k, 1)
                pool.wait_ge(pool_k, k + 1)
                for i in range(2):
                    pool.tensor_tensor(k_rot[:, :, HALF * i:HALF * i + HALF],
                                       k_n[:, :, HALF * (1 - i):HALF * (1 - i) + HALF],
                                       k_sin[:, HALF * i:HALF * i + HALF].unsqueeze(1)
                                       .to_broadcast([P, G, HALF]), ALU.mult).then_inc(pool_k, 1)
                pool.tensor_tensor(k_par[:], k_n[:], k_cos[:].unsqueeze(1).to_broadcast([P, G, HD]),
                                   ALU.mult).then_inc(pool_k, 1)
                pool.wait_ge(pool_k, k + 4)
                pool.tensor_tensor(kvg[p][:, 0:G * HD].rearrange("p (g d) -> p g d", g=G), k_par[:], k_rot[:],
                                   ALU.add).then_inc(pool_k, 1)

            def quarter(t, h, q, parts):
                s = 4 * t + q
                for n in range(16):
                    if parts.scan:
                        i, e = n % 4, 16 * s + n
                        if n == 0:
                            pool.wait_ge(ld_bc[q % 2], 16 * (half(t, q) + 1))
                        wait(pool, pe_hc, e + 1 - NBUF)
                        pool.wait_ge(dve_h, e + 1)
                        pool.tensor_tensor(hc[n % NBUF][:], hid[:, n % NBUF, :], bc[q % 2][:, i, 1, :],
                                           ALU.mult).then_inc(pool_hc, 1)
                    if n == 3 and parts.gather:
                        weights(s + 6, q % 2)
                    if n == 8 and parts.fourth:
                        keys(s - 5, (q + 1) % 2)

            for i in range(2):
                pool.memset(w_pair[i][:], 0.0).then_inc(zpair_ok, 1)
            pool.wait_ge(widx_ok, 1)
            weights(0, 0)
            quarters(pool, quarter)
            for i in range(2):
                pool.wait_ge(ld_w[i], 16 * NG // 2)

        @block.scalar
        def _(act):
            def quarter(t, h, q, parts):
                s = 4 * t + q

                def weight_blocks():
                    g, p = s + 5, (q + 1) % 2
                    act.wait_ge(ld_w[p], 16 * (half(t, q + 5) + 1))
                    wait(act, pe_u, g - 1)
                    for b in range(2):
                        rows = slice(64 * b, 64 * b + 64)
                        nc.scalar.copy(w_pair[p][rows, HD * b:HD * b + HD], w_rows[p][rows, :]).then_inc(wpair_ok, 1)

                def sums(t, c):
                    act.wait_ge(pe_hc, 64 * t + 48 + 4 * c + 4)
                    wait(act, pe_q, 4 * (4 * t - 1) + c + 1)
                    wait(act, st_x1[c], 16 * t)
                    nc.scalar.copy(x1[c][:], y[c]).then_inc(act_y, 1)

                def take_u():
                    g = s + 5
                    act.wait_ge(pe_u, g + 1)
                    wait(act, dve_res, 4 * (t if q == 3 else t - 1) + 4)
                    k = (q + 1) % 4
                    nc.scalar.copy(u[h if q == 3 else 1 - h][:, :, GRP * k:GRP * k + GRP],
                                   pro[0].rearrange("p (c t) -> p c t", c=NCH)).then_inc(act_u, 1)

                def take_x():
                    g, p = s + 5, (q + 1) % 2
                    act.wait_ge(pe_x, g + 1)
                    wait(act, st_bc[(q + 3) % 4], 16 * (t + (q + 3) // 4))
                    nc.scalar.copy(drg[:], pro[1][:, 0:GRP]).then_inc(act_dr, 1)
                    nc.scalar.copy(bcg[p][:], pro[1][0:32, GRP:2 * GRP]).then_inc(act_dr, 1)

                def softplus_exp():
                    g = s + 4
                    act.wait_ge(dve_z, g + 1)
                    wait(act, act_sp, 3 * g)
                    nc.scalar.activation(sp_a[:], zg[:], ACT.Abs).then_inc(act_sp, 1)
                    act.wait_ge(act_sp, 3 * g + 1)
                    nc.scalar.activation(sp_a[:], sp_a[:], ACT.Exp, scale=-1.0).then_inc(act_sp, 1)

                def softplus_ln():
                    g = s + 4
                    act.wait_ge(act_sp, 3 * g + 2)
                    wait(act, dve_dl, g)
                    nc.scalar.activation(sp_l[:], sp_a[:], ACT.Ln, bias=1.0).then_inc(act_sp, 1)

                def take_kv():
                    g, p = s - 5, (q + 1) % 2
                    act.wait_ge(pe_kv, g + 1)
                    wait(act, st_kv[p], 16 * half(t, q - 5))
                    nc.scalar.copy(kvg[p][:, G * HD:KV], qk[0][:, G * HD:KV]).then_inc(act_kv, 1)
                    wait(act, pool_k, 5 * g)
                    nc.scalar.copy(k_raw[:].rearrange("p g d -> p (g d)"), qk[0][:, 0:G * HD]).then_inc(act_kv, 1)
                    wait(act, dve_ms, g)
                    for j in range(G):
                        nc.scalar.activation(k_sq[:, j, :], qk[0][:, HD * j:HD * j + HD], ACT.Square,
                                             accum_out=k_ss[:, j:j + 1]).then_inc(act_kv, 1)

                def key_rms():
                    g = s - 5
                    act.wait_ge(dve_ms, g + 1)
                    wait(act, dve_ks, g)
                    nc.scalar.activation(k_ln[:], k_ms[:], ACT.Ln).then_inc(act_rs, 1)
                    act.wait_ge(act_rs, 2 * g + 1)
                    nc.scalar.activation(k_r0[:], k_ln[:], ACT.Exp, scale=-0.5).then_inc(act_rs, 1)

                def take_q():
                    g, p = s - 5, (q + 1) % 2
                    act.wait_ge(pe_q, 4 * (g + 1))
                    wait(act, st_q[p], 16 * half(t, q - 5))
                    nc.scalar.copy(qg[p][:], qk[1]).then_inc(act_q, 1)

                if parts.scan and q == 0:
                    act.wait_ge(dve_dl, 4 * (t + 1))
                for n in range(16):
                    if parts.scan:
                        c, i, e = n // 4, n % 4, 16 * s + n
                        wait(act, dve_h, e + 1 - NBUF)
                        nc.scalar.activation(
                            decay[n % NBUF].rearrange("p (b t) -> p b t", t=T)[:, :, 1:T],
                            delta[h][:, c, :].rearrange("p (b t) -> p b t", t=T)[:, :, 1:T],
                            ACT.Exp, scale=neg_a[:, NST * c + 4 * q + i:NST * c + 4 * q + i + 1]).then_inc(act_exp, 1)
                    if n == 0:
                        if parts.first:
                            weight_blocks()
                        if parts.fourth:
                            take_kv()
                    if n == 1 and parts.fourth:
                        take_q()
                    if n == 2 and parts.second:
                        softplus_exp()
                    if n == 4 and q == 0 and parts.third:
                        sums(t - 1, 3)
                    if n == 5 and parts.first:
                        take_u()
                    if n == 6:
                        if parts.second:
                            softplus_ln()
                        if parts.fourth:
                            key_rms()
                    if n == 9 and parts.first:
                        take_x()
                    if n in (11, 13, 15) and q == 3 and parts.scan:
                        sums(t, (n - 11) // 2)

                if isinstance(t, int) and t == -1:
                    if q == 0:
                        act.wait_ge(s_const, 16 * NCONST)
                        nc.scalar.activation(neg_a[:], a_log[:], ACT.Exp).then_inc(c_neg, 1)
                    if q == 1:
                        act.wait_ge(c_sin, 1)
                        nc.scalar.activation(sin[:], rem, ACT.Sin).then_inc(c_a, 1)
                    if q == 2:
                        act.wait_ge(c_sin, 2)
                        nc.scalar.activation(cos[:], rem, ACT.Sin).then_inc(c_a, 1)
                        act.wait_ge(zero_ok, NBUF + 1)

            act.wait_ge(zpair_ok, 2)
            quarters(act, quarter)

        @block.vector
        def _(dve):
            done = [0]

            def link(ins):
                done[0] += 1
                ins.then_inc(c_dve, 1)
                dve.wait_ge(c_dve, done[0])

            dve.wait_ge(s_cond, 16 * 3)
            link(nc.vector.tensor_copy(cond_f[:], cond_i[:]))
            link(nc.vector.tensor_scalar(cond_f[:], cond_f[:], 64.0, part[:, 0:1], ALU.mult, ALU.add))
            nc.vector.tensor_copy(w_idx[:], cond_f[:]).then_inc(widx_ok, 1)
            for i in range(NBUF):
                nc.vector.memset(decay[i].rearrange("p (b t) -> p b t", t=T)[:, :, 0:1], 0.0).then_inc(zero_ok, 1)
            dve.wait_ge(s_const, 16 * NCONST)

            def tables(which):
                if which == 0:
                    link(nc.vector.tensor_copy(pos_f[:], len_i[:]))
                    link(nc.vector.tensor_scalar(pos_f[:], pos_f[:], part[:, 0:1], None, ALU.add))
                    link(nc.vector.tensor_tensor(ang.rearrange("p (g f) -> p g f", f=HALF),
                                                 pos_f[:].unsqueeze(2).to_broadcast([P, NG, HALF]),
                                                 inv[:].unsqueeze(1).to_broadcast([P, NG, HALF]), ALU.mult))
                quart, shift = ((0.0, 0.0), (0.25, float(np.float32(np.pi / 2))))[which]
                link(nc.vector.tensor_scalar(turns, ang, float(1 / (2 * np.pi)), quart, ALU.mult, ALU.add))
                link(nc.vector.tensor_scalar(turns, turns, MAGIC, None, ALU.add))
                link(nc.vector.tensor_scalar(turns, turns, MAGIC, None, ALU.subtract))
                if which:
                    dve.wait_ge(c_a, 1)
                link(nc.vector.scalar_tensor_tensor(rem, turns, -TWO_PI[0], ang, ALU.mult, ALU.add))
                link(nc.vector.scalar_tensor_tensor(rem, turns, -TWO_PI[1], rem, ALU.mult, ALU.add))
                link(nc.vector.scalar_tensor_tensor(rem, turns, -TWO_PI[2], rem, ALU.mult, ALU.add))
                link(nc.vector.tensor_scalar(rem, rem, shift, 3.1415925, ALU.add, ALU.min))
                nc.vector.tensor_scalar(rem, rem, -3.1415925, None, ALU.max).then_inc(c_sin, 1)

            def scales():
                nc.vector.tensor_scalar(one_ks[:, 0, :], k_scale[:, 0, :], 1.0, None, ALU.add)
                nc.vector.tensor_scalar(one_ks[:, 1, 0:HALF], k_scale[:, 1, 0:HALF], -1.0, -1.0, ALU.mult, ALU.add)
                link(nc.vector.tensor_scalar(one_ks[:, 1, HALF:HD], k_scale[:, 1, HALF:HD], 1.0, None, ALU.add))
                dve.wait_ge(c_neg, 1)
                nc.vector.tensor_scalar(neg_a[:], neg_a[:], -1.0, None, ALU.mult).then_inc(zero_ok, 1)
                dve.wait_ge(c_a, 2)
                nc.vector.memset(k_ms[:], 0.0).then_inc(rope_ok, 1)

            def quarter(t, h, q, parts):
                s = 4 * t + q

                def times_b(n):
                    if n == 0:
                        dve.wait_ge(ld_bc[q % 2], 16 * (half(t, q) + 1))
                    if n % 4 == 0 and q == 0:
                        dve.wait_ge(dve_du, 4 * t + n // 4 + 1)
                    wait(dve, dve_h, 16 * s + n + 1 - 4)
                    nc.vector.tensor_tensor(dbu[:, n % 4, :], du[n // 4][:], bc[q % 2][:, n % 4, 0, :], ALU.mult
                                            ).then_inc(dve_dbu, 1)

                def prepare(t, c, h):
                    dve.wait_ge(dve_dl, 4 * (t + 1))
                    wait(dve, dve_dbu, 64 * t - 16 + 4 * c + 4)
                    nc.vector.tensor_tensor(du[c][:], delta[h][:, c, :], u[h][:, c, :], ALU.mult).then_inc(dve_du, 1)
                    dve.wait_ge(ld_xt[c % 2], 16 * (2 * t + c // 2 + 1))
                    wait(dve, pe_res, 4 * t + c - 1)
                    nc.vector.scalar_tensor_tensor(resid[c % 2][:], u[h][:, c, :], skip_d[:, c:c + 1], xt_in[c % 2][:],
                                                   ALU.mult, ALU.add).then_inc(dve_res, 1)

                def add_bias():
                    g = s + 5
                    dve.wait_ge(pe_z, g + 1)
                    wait(dve, act_sp, 3 * g)
                    wait(dve, dve_dl, g)
                    nc.vector.tensor_tensor(zg[:], pro[0].rearrange("p (c t) -> p c t", c=NCH),
                                            dt_bias[:].unsqueeze(2).to_broadcast([P, NCH, GRP]),
                                            ALU.add).then_inc(dve_z, 1)

                def softplus():
                    g = s + 4
                    dve.wait_ge(act_sp, 3 * (g + 1))
                    wait(dve, act_exp, 64 * t)
                    nc.vector.scalar_tensor_tensor(delta[1 - h][:, :, GRP * q:GRP * q + GRP], zg[:], 0.0, sp_l[:],
                                                   ALU.max, ALU.add).then_inc(dve_dl, 1)

                def key_squares():
                    g = s - 5
                    wait(dve, pool_k, 5 * g)
                    for out, table, i in ((k_cos, cos, 0), (k_sin, sin, 1)):
                        nc.vector.tensor_tensor(
                            out[:].rearrange("p (a f) -> p a f", a=2),
                            table[:, bass.ds(g * HALF, HALF)].unsqueeze(1).to_broadcast([P, 2, HALF]),
                            one_ks[:, i, :].rearrange("p (a f) -> p a f", a=2), ALU.mult)
                    dve.wait_ge(act_kv, 6 * (g + 1))
                    wait(dve, dve_ks, g)
                    nc.vector.tensor_scalar(k_ms[:], k_ss[:], 1.0 / HD, EPS, ALU.mult, ALU.add).then_inc(dve_ms, 1)

                def key_rms():
                    g = s - 5
                    dve.wait_ge(act_rs, 2 * g + 2)
                    nc.vector.tensor_tensor(k_r2[:], k_r0[:], k_r0[:], ALU.mult).then_inc(dve_kt, 1)
                    dve.wait_ge(dve_kt, 2 * g + 1)
                    nc.vector.scalar_tensor_tensor(k_r3[:], k_r2[:], -0.5, k_ms[:], ALU.mult, ALU.mult
                                                   ).then_inc(dve_kt, 1)
                    dve.wait_ge(dve_kt, 2 * g + 2)
                    nc.vector.scalar_tensor_tensor(k_rs[:], k_r3[:], 1.5, k_r0[:], ALU.add, ALU.mult
                                                   ).then_inc(dve_ks, 1)

                if parts.scan:
                    times_b(0)
                for n in range(16):
                    if n == 2 and parts.fourth:
                        key_squares()
                    if n == 6:
                        if parts.second:
                            softplus()
                        if parts.fourth:
                            key_rms()
                    if n == 12 and parts.first:
                        add_bias()
                    if n in (2, 6, 10) and q == 0 and parts.scan:
                        prepare(t, n // 4 + 1, h)
                    if n == 14 and q == 3 and parts.next_scan:
                        prepare(t + 1, 0, 1 - h)
                    if parts.scan:
                        e = 16 * s + n
                        if n < 15:
                            times_b(n + 1)
                        dve.wait_ge(act_exp, e + 1)
                        dve.wait_ge(dve_dbu, e + 1)
                        wait(dve, pool_hc, e + 1 - NBUF)
                        nc.vector.tensor_tensor_scan(hid[:, n % NBUF, :], decay[n % NBUF][:], dbu[:, n % 4, :], 0.0,
                                                     ALU.mult, ALU.add).then_inc(dve_h, 1)
                if isinstance(t, int) and t == -1:
                    if q < 2:
                        tables(q)
                    if q == 2:
                        scales()

            quarters(dve, quarter)

        @block.tensor
        def _(pe):
            pe.wait_ge(s_const, 16 * NCONST)

            def quarter(t, h, q, parts):
                s = 4 * t + q

                def project_u():
                    g, p = s + 5, (q + 1) % 2
                    pe.wait_ge(ld_xp[p], 16 * (half(t, q + 5) + 1))
                    pe.wait_ge(wpair_ok, 2 * (g + 1))
                    wait(pe, dve_z, g)
                    for j in range(NCH):
                        mm = nc.tensor.matmul(pro[0][:, GRP * j:GRP * j + GRP], x_pair[p][:, P * j:P * j + P],
                                              w_pair[p][:], start=True, stop=True)
                    mm.then_inc(pe_u, 1)

                def project_x():
                    g, k = s + 5, (q + 1) % 4
                    pe.wait_ge(act_u, g + 1)
                    wait(pe, act_dr, 2 * g)
                    for lo, n, m in ((0, 0, P), (P, 1, 32)):
                        for j in range(NCH):
                            mm = nc.tensor.matmul(pro[1][0:m, GRP * n:GRP * n + GRP], w_x[:, j, lo:lo + m],
                                                  u[h if q == 3 else 1 - h][:, j, GRP * k:GRP * k + GRP],
                                                  start=(j == 0), stop=(j == NCH - 1))
                    mm.then_inc(pe_x, 1)

                def project_dt():
                    pe.wait_ge(act_dr, 2 * (s + 6))
                    for j in range(NCH):
                        mm = nc.tensor.matmul(pro[0][:, GRP * j:GRP * j + GRP], w_dt[:, P * j:P * j + P], drg[:],
                                              start=True, stop=True)
                    mm.then_inc(pe_z, 1)

                def project_qkv(j, i):
                    g = s - 4
                    if i == 0 and q == 0:
                        pe.wait_ge(act_y, 4 * (t - 1) + j + 1)
                    if j == 0:
                        wait(pe, (act_kv, act_q)[i], (6, 1)[i] * g)
                        if isinstance(t, int) and t == 1 and q == 0:
                            pe.wait_ge(s_qkvw, 16)
                    lo = D * (1 - i)
                    mm = nc.tensor.matmul(qk[i], x1[j][:, GRP * q:GRP * q + GRP], w_qkv[:, j, lo:lo + D],
                                          start=(j == 0), stop=(j == NCH - 1))
                    if i == 1:
                        mm.then_inc(pe_q, 1)
                    elif j == NCH - 1:
                        mm.then_inc(pe_kv, 1)

                for n in range(16):
                    if parts.first:
                        if n == 1:
                            project_u()
                        if n == 5:
                            project_x()
                        if n == 9:
                            project_dt()
                    if parts.third and 5 <= n < 5 + 2 * NCH:
                        project_qkv((n - 5) // 2, (n - 5) % 2)
                    if parts.scan:
                        c, e = n // 4, 16 * s + n
                        if q == 0 and n % 4 == 0:
                            wait(pe, act_y, 4 * (t - 1) + c + 1)
                            pe.wait_ge(dve_res, 4 * t + c + 1)
                            nc.tensor.matmul(y[c], ident[:], resid[c % 2][:], start=True, stop=False
                                             ).then_inc(pe_res, 1)
                        pe.wait_ge(pool_hc, e + 1)
                        nc.tensor.matmul(y[c], ident[:], hc[n % NBUF][:], start=False,
                                         stop=(q == 3 and n % 4 == 3)).then_inc(pe_hc, 1)

            quarters(pe, quarter)


def attention_block(nc, A, S):
    with ExitStack() as ctx:
        def sb(name, shape, dt=F32):
            return ctx.enter_context(nc.sbuf_tensor(name, shape, dt))

        def sem(name):
            return ctx.enter_context(nc.semaphore(name))

        psum = ctx.enter_context(nc.psum_tensor("attn_psum", [P, 8, 512], F32))
        q_bank = psum[:, 0, :]
        k_bank = [psum[:, 1 + i, 0:NKEY] for i in range(2)]
        score = [psum[:, 3 + i, 0:NKEY] for i in range(2)]
        p_bank = psum[0:KC, 5, 0:NKC * P]
        o_bank = psum[:, 6, :].rearrange("p (c t) -> p c t", c=4)
        a_bank = psum[:, 7, :]

        ident = sb("ident2", [P, P])
        ones = sb("ones", [P, P])
        w_o = sb("w_o", [P, 4, D])
        w_r = sb("w_r", [P, D])
        b_r = sb("b_r", [P, 1])
        q_scale = sb("q_scale", [P, 2, HD])
        one_qs = sb("one_qs", [P, 2, HD])
        cos = sb("cos2", [P, NG * HALF])
        sin = sb("sin2", [P, NG * HALF])
        dist = sb("dist", [P, NKEY])
        own = sb("own", [P, P])
        before = sb("before", [P, P])
        slot_no = sb("slot_no", [P, SEL * 2])

        ids = sb("ids", [P, NBLK])
        table_i = sb("table_i", [P, NBLK], I32)
        table = sb("table", [P, NBLK])
        len_i = sb("len2_i", [P, 1 + B], I32)
        len_f = sb("len_f", [P, 1 + B])
        sh_i = sb("sh_i", [P, 1 + B], I32)
        q_blk = sb("q_blk", [P, 1 + B])
        rest = sb("rest", [P, 1 + B])
        first = sb("first", [P, 1 + B])
        mask_at = sb("mask_at", [P, 1 + B])
        slots = sb("slots", [P, NSLOT])
        w_slots = sb("w_slots", [P, NWC])
        w_slot0 = sb("w_slot0", [P, NWC])
        junk = sb("junk", [P, NBLK])
        win = sb("win", [P, NSLOT])
        wid = sb("wid", [P, NWC])
        win_t = sb("win_t", [NSLOT, B])
        wid_t = sb("wid_t", [NWC, P])
        row_blk = sb("row_blk", [KC, NKC, B])
        all_blk = sb("all_blk", [P, NSLOT * B])
        all_wid = sb("all_wid", [P, NWC * P])
        later = sb("later", [P, NWC, NWC * P])
        beats = sb("beats", [P, NWC, NWC * P])
        off_in = sb("off_in", [P, 1])
        tau0 = sb("tau0", [P, NWC, BLOCK])
        tau = sb("tau", [P, NWC, BLOCK])
        cover = sb("cover", [P, NWC, BLOCK])
        alive = sb("alive", [P, NWC, BLOCK])
        tok0 = sb("tok0", [P, 1])
        token = sb("token", [P, NWC, BLOCK])
        placed = sb("placed", [P, NWC, SC, KC])
        match = sb("match", [P, NWC, NSLOT * B])
        far = sb("far", [KC, NKC * B])
        idx_old = sb("idx_old", [KC, NKC, B], I32)
        idx_new = sb("idx_new", [KC, NKC, B], I32)

        old_now = [sb(f"old_now{i}", [KC, NKC], I32) for i in range(4)]
        new_now = [sb(f"new_now{i}", [KC, NKC], I32) for i in range(4)]
        kv = [sb(f"kv{i}", [KC, NKC, KV]) for i in range(4)]
        q_in = [sb(f"q_in{i}", [P, H, HD]) for i in range(2)]
        q_sq = sb("q_sq", [P, H, HD])
        q_n = sb("q_n", [P, H, HD])
        q_rot = sb("q_rot", [P, H, HD])
        q_ss, q_ln, q_r0, q_r2, q_rs = (sb(n, [P, H]) for n in ("q_ss", "q_ln", "q_r0", "q_r2", "q_rs"))
        q_cos = sb("q_cos", [P, HD])
        q_sin = sb("q_sin", [P, HD])
        q_t = [sb(f"q_t{i}", [P, 2, 2, 2, T]) for i in range(2)]
        k_t = [sb(f"k_t{i}", [P, 2, NKEY]) for i in range(2)]
        far2 = sb("far2", [P, NKEY])
        mask = [sb(f"mask{i}", [P, NKEY]) for i in range(2)]
        sm = [sb(f"sm{i}", [P, NKEY]) for i in range(2)]
        prob = [sb(f"prob{i}", [P, NKEY]) for i in range(2)]
        p_t = [sb(f"p_t{i}", [KC, NKC, P]) for i in range(2)]
        top = [sb(f"top{i}", [P, 1]) for i in range(2)]
        ntop = [sb(f"ntop{i}", [P, 1]) for i in range(2)]
        total = [sb(f"total{i}", [P, 1]) for i in range(2)]
        share = [sb(f"share{i}", [P, 1]) for i in range(2)]
        o_t = [sb(f"o_t{i}", [P, 4, P]) for i in range(2)]
        a_sb = [sb(f"a_sb{i}", [P, D]) for i in range(2)]
        r_junk = sb("r_junk", [P, D])
        r_s = sb("r_s", [P, 1])
        r_diag = sb("r_diag", [P, P])
        r_own, r_gt, r_eq, r_rank = (sb(n, [P, 1]) for n in ("r_own", "r_gt", "r_eq", "r_rank"))
        keep = [sb(f"keep{i}", [P, 2 * SEL]) for i in range(2)]
        keep_t = [sb(f"keep_t{i}", [P, P]) for i in range(2)]
        xs = [sb(f"xs{i}", [P, NCH, 2 * SEL]) for i in range(2)]

        s_c = sem("a_const")
        c_dve, c_pe = sem("c2_dve"), sem("c2_pe")
        st_blk, ld_blk = sem("st_blk"), sem("ld_blk")
        idx_ok, now_ok, pool_mark = sem("idx_ok"), sem("now_ok"), sem("pool_mark2")
        sp_mark, dve_mark = sem("sp_mark2"), sem("dve_mark2")
        filled = sem("filled")
        ld_old = [sem(f"ld_old{i}") for i in range(4)]
        ld_kv = [sem(f"ld_kv{i}") for i in range(4)]
        ld_q = [sem(f"ld_q{i}") for i in range(2)]
        st_keep = [sem(f"st_keep{i}") for i in range(2)]
        st_xs = [sem(f"st_xs{i}") for i in range(2)]
        pe_q, pe_k, pe_sc, pe_pt, pe_pv = sem("pe2_q"), sem("pe_k"), sem("pe_sc"), sem("pe_pt"), sem("pe_pv")
        pe_a, pe_row, pe_xs = sem("pe_a"), sem("pe_row"), sem("pe_xs")
        act_sq, act_qr, act_qt, act_kt = sem("act_sq"), sem("act_qr"), sem("act_qt"), sem("act_kt")
        act_far, act_e, act_pt = sem("act_far"), sem("act_e"), sem("act_pt")
        act_o, act_a, act_xs = sem("act_o"), sem("act_a"), sem("act_xs")
        dve_qc, dve_ms, dve_q, dve_mask = sem("dve_qc"), sem("dve_qms"), sem("dve_q"), sem("dve_mask")
        dve_sm, dve_nt, dve_sh, dve_p = sem("dve_sm"), sem("dve_nt"), sem("dve_sh"), sem("dve_p")
        dve_rc, dve_diag, dve_keep = sem("dve_rc"), sem("dve_diag"), sem("dve_keep")

        NC = 23

        block = ctx.enter_context(nc.Block())

        def pairs(eng, pair):
            pair(0, 0, 0, False, True)
            pair(1, 0, 1, True, True)
            pair(2, 1, 0, True, True)
            pair(3, 1, 1, True, True)
            with eng.Fori(2, NG // 2 - 1) as i:
                pair(2 * i, i, 0, True, True)
                pair(2 * i + 1, i, 1, True, True)
            pair(NG - 2, NG // 2 - 1, 0, True, True)
            pair(NG - 1, NG // 2 - 1, 1, True, False)

        def unit(u):
            return u // 4, u // 2 % 2, u % 2

        @block.sync
        def _(sp):
            for dst, src in ((ident, A["ident"]), (ids, A["ids"]), (w_slot0, A["w_slot0"]), (tau0, A["tau0"]),
                             (tok0, A["tok0"]), (off_in, A["off_in"]), (later, A["later"]), (dist, A["dist"]),
                             (own, A["own"]), (before, A["before"]), (slot_no, A["slot_no"]), (w_o, A["w_o"]),
                             (cos, S["cos"]), (sin, S["sin"])):
                sp.dma_start(dst[:], src).then_inc(s_c, 16)
            for half in range(2):
                rows = slice(64 * half, 64 * half + 64)
                sp.dma_start(table_i[rows, :], A["table"]).then_inc(s_c, 16)
                sp.dma_start(len_i[rows, 0:1], A["lens"]).then_inc(s_c, 16)
            sp.dma_start(len_i[:, 1:1 + B], A["lens_row"].partition_broadcast(P)).then_inc(s_c, 16)
            sp.dma_start(w_r[:], A["w_r"].partition_broadcast(P)).then_inc(s_c, 16)
            sp.dma_start(b_r[:], A["b_r"].partition_broadcast(P)).then_inc(s_c, 16)
            for s in range(2):
                sp.dma_start(q_scale[:, s, :], A["q_scale2"][s].partition_broadcast(P)).then_inc(s_c, 16)
            sp.wait_ge(c_dve, C_TURNED)
            sp.dma_start(S["win"], win_t[:]).then_inc(st_blk, 16)
            sp.dma_start(S["wid"], wid_t[:]).then_inc(st_blk, 16)
            sp.wait_ge(st_blk, 32)
            by_slot = S["win"].rearrange("(c j) b -> j c b", j=SC)
            for j in range(SC):
                sp.dma_start(row_blk[BLOCK * j:BLOCK * j + BLOCK, :, :], by_slot[j].partition_broadcast(BLOCK)
                             ).then_inc(ld_blk, 16)
            sp.dma_start(all_blk[:], S["win"].rearrange("s b -> (s b)").partition_broadcast(P)).then_inc(ld_blk, 16)
            sp.dma_start(all_wid[:], S["wid"].rearrange("s b -> (s b)").partition_broadcast(P)).then_inc(ld_blk, 16)

            def load_q(m, h):
                wait(sp, dve_q, 6 * (m - 1), sp_mark)
                sp.dma_start(q_in[h][:].rearrange("p h d -> p (h d)"), S["q"][bass.ds(m * GRP, GRP), :]
                             ).then_inc(ld_q[h], 16)

            def pair(m, i, h, last, nxt):
                if nxt:
                    load_q(m + 1, 1 - h)
                if last:
                    store(m - 1, i if h else i - 1, 1 - h)

            def store(m, i, h):
                wait(sp, act_xs, 2 * (m + 1), sp_mark)
                sp.dma_start(S["keep"][bass.ds(2 * i + h, 1)].rearrange("o s t -> (o s) t"),
                             keep_t[h][64 * h:64 * h + 64, :]).then_inc(st_keep[h], 16)
                sp.dma_start(S["xsp"][:, :, bass.ds(m * 2 * SEL, 2 * SEL)], xs[h][:]).then_inc(st_xs[h], 16)

            load_q(0, 0)
            pairs(sp, pair)
            store(NG - 1, NG // 2 - 1, 1)
            for h in range(2):
                sp.wait_ge(st_keep[h], 16 * NG // 2)
                sp.wait_ge(st_xs[h], 16 * NG // 2)

        @block.gpsimd
        def _(pool):
            nc.gpsimd.memset(placed[:], 0.0).then_inc(filled, 1)
            nc.gpsimd.memset(ones[:], 1.0).then_inc(filled, 1)
            pool.wait_ge(idx_ok, 2)

            def gather_old(b, s):
                wait(pool, pe_pv, 4 * (b - 3), pool_mark)
                pool.tensor_copy(old_now[s][:], idx_old[:, :, bass.ds(b, 1)].rearrange("p c o -> p (c o)")
                                 ).then_inc(now_ok, 1)
                pool.tensor_copy(new_now[s][:], idx_new[:, :, bass.ds(b, 1)].rearrange("p c o -> p (c o)")
                                 ).then_inc(now_ok, 1)
                wait(pool, now_ok, 2 * (b + 1), pool_mark)
                for c in range(NKC):
                    pool.indirect_dma_start(kv[s][:, c, :], None, A["kv_rows"],
                                            bass.IndirectOffsetOnAxis(ap=old_now[s][:, c:c + 1], axis=0)
                                            ).then_inc(ld_old[s], 16)

            def gather_new(i, s):
                wait(pool, ld_old[s], 16 * NKC * (i + 1), pool_mark)
                for c in range(NKC):
                    pool.indirect_dma_start(kv[s][:, c, :], None, S["kv_new"],
                                            bass.IndirectOffsetOnAxis(ap=new_now[s][:, c:c + 1], axis=0),
                                            bounds_check=NTOK - 1, oob_is_err=False).then_inc(ld_kv[s], 16)

            gather_old(0, 0)
            for s in range(4):
                gather_old(s + 1, (s + 1) % 4)
                gather_new(0, s)
            with pool.Fori(1, B // 4 - 1) as i:
                for s in range(4):
                    gather_old(4 * i + s + 1, (s + 1) % 4)
                    gather_new(i, s)
            for s in range(4):
                if s < 3:
                    gather_old(B - 4 + s + 1, s + 1)
                gather_new(B // 4 - 1, s)

        @block.scalar
        def _(act):
            def query_squares(m, h):
                act.wait_ge(ld_q[h], 16 * (m // 2 + 1) if isinstance(m, int) else 16 * (half_of[0] + 1))
                wait(act, dve_q, 6 * m)
                nc.scalar.activation(q_sq[:], q_in[h][:], ACT.Square).then_inc(act_sq, 1)

            def query_rms(m):
                act.wait_ge(dve_ms, m + 1)
                nc.scalar.activation(q_ln[:], q_ss[:], ACT.Ln).then_inc(act_qr, 1)
                act.wait_ge(act_qr, 2 * m + 1)
                nc.scalar.activation(q_r0[:], q_ln[:], ACT.Exp, scale=-0.5).then_inc(act_qr, 1)

            def take_q(m, h):
                act.wait_ge(pe_q, m + 1)
                wait(act, pe_sc, 8 * (m - 1))
                for gp in range(2):
                    nc.scalar.copy(q_t[h][:, gp, :, :, :].rearrange("p b j t -> p j b t"),
                                   q_bank[:, 2 * P * gp:2 * P * gp + 2 * P].rearrange("p (j b t) -> p j b t", j=2, b=2)
                                   ).then_inc(act_qt, 1)

            def take_k(m, b):
                act.wait_ge(pe_k, 2 * m + b + 1)
                wait(act, pe_sc, 8 * m - 4 + 4 * b)
                for gp in range(2):
                    nc.scalar.copy(k_t[b][:, gp, :], k_bank[gp]).then_inc(act_kt, 1)

            def distance(m, b):
                wait(act, dve_mask, 2 * m + b)
                nc.scalar.activation(far2[:], dist[:], ACT.Square, bias=mask_at[:, bass.ds(2 * m + b + 1, 1)]
                                     ).then_inc(act_far, 1)

            def exps(m, u):
                act.wait_ge(dve_nt, 8 * m + u + 1)
                wait(act, pe_pt, 8 * m + u - 1)
                nc.scalar.activation(prob[u % 2][:], sm[u % 2][:], ACT.Exp, bias=ntop[u % 2][:], scale=SCALE,
                                     accum_out=total[u % 2][:]).then_inc(act_e, 1)

            def take_p(m, u):
                act.wait_ge(pe_pt, 8 * m + u + 1)
                wait(act, pe_pv, 8 * m + u - 1)
                nc.scalar.copy(p_t[u % 2][:].rearrange("p c t -> p (c t)"), p_bank).then_inc(act_pt, 1)

            def take_rows(m, h):
                act.wait_ge(pe_xs, m + 1)
                if not (isinstance(m, int) and m < 2):
                    act.wait_ge(st_keep[h], 16 * half_of[1])
                    act.wait_ge(st_xs[h], 16 * half_of[1])
                rows = slice(64 * h, 64 * h + 64)
                nc.scalar.copy(keep_t[h][rows, :], a_bank[rows, P:2 * P]).then_inc(act_xs, 1)
                nc.scalar.copy(xs[h][:].rearrange("p c s -> p (c s)"), a_bank[:, 2 * P:]).then_inc(act_xs, 1)

            half_of = [0, 0]

            def pair(m, i, h, last, nxt):
                half_of[0] = i if h == 0 else i + 1
                half_of[1] = i - 1 if h == 0 else i
                for u in range(8):
                    if u < 7:
                        exps(m, u + 1)
                    elif nxt:
                        exps(m + 1, 0)
                    if u == 0:
                        distance(m, 1)
                        if nxt:
                            query_squares(m + 1, 1 - h)
                    if u == 1 and nxt:
                        query_rms(m + 1)
                    if u == 2:
                        take_k(m, 1)
                    if u == 4 and nxt:
                        distance(m + 1, 0)
                        take_q(m + 1, 1 - h)
                    if u == 5 and last:
                        take_rows(m - 1, 1 - h)
                    if u == 6 and nxt:
                        take_k(m + 1, 0)
                    take_p(m, u)
                take_o(m, h)
                act.wait_ge(pe_a, m + 1)
                wait(act, pe_xs, m - 1)
                nc.scalar.copy(a_sb[h][:], a_bank).then_inc(act_a, 1)

            def take_o(m, h):
                act.wait_ge(pe_pv, 8 * m + 8)
                wait(act, pe_a, m - 1)
                nc.scalar.copy(o_t[h][:], o_bank).then_inc(act_o, 1)

            act.wait_ge(s_c, 16 * NC)
            query_squares(0, 0)
            query_rms(0)
            act.wait_ge(c_dve, C_MASK)
            distance(0, 0)
            take_q(0, 0)
            take_k(0, 0)
            exps(0, 0)
            pairs(act, pair)
            half_of[1] = NG // 2 - 1
            take_rows(NG - 1, 1)

        @block.vector
        def _(dve):
            done = [0]

            def mark(ins):
                done[0] += 1
                ins.then_inc(c_dve, 1)
                return ins

            def link(ins):
                mark(ins)
                dve.wait_ge(c_dve, done[0])

            dve.wait_ge(s_c, 16 * NC)
            v = nc.vector
            mark(v.tensor_scalar(one_qs[:, 0, :], q_scale[:, 0, :], 1.0, None, ALU.add))
            mark(v.tensor_scalar(one_qs[:, 1, 0:HALF], q_scale[:, 1, 0:HALF], -1.0, -1.0, ALU.mult, ALU.add))
            mark(v.tensor_scalar(one_qs[:, 1, HALF:HD], q_scale[:, 1, HALF:HD], 1.0, None, ALU.add))
            mark(v.tensor_copy(table[:], table_i[:]))
            mark(v.tensor_copy(len_f[:], len_i[:]))
            link(v.tensor_scalar(sh_i[:], len_i[:], 4, None, ALU.arith_shift_right))
            link(v.tensor_copy(q_blk[:], sh_i[:]))
            link(v.scalar_tensor_tensor(rest[:], q_blk[:], -float(BLOCK), len_f[:], ALU.mult, ALU.add))
            link(v.tensor_scalar(first[:], len_f[:], -float(WINDOW - 1), 0.0, ALU.add, ALU.max))
            link(v.tensor_copy(sh_i[:], first[:]))
            link(v.tensor_scalar(sh_i[:], sh_i[:], 4, None, ALU.arith_shift_right))
            link(v.tensor_copy(first[:], sh_i[:]))
            link(v.tensor_scalar(first[:], first[:], float(NBLK - NSLOT), None, ALU.min))
            link(v.scalar_tensor_tensor(mask_at[:], first[:], float(BLOCK), len_f[:], ALU.mult, ALU.subtract))
            link(v.tensor_scalar(mask_at[:], mask_at[:], WINDOW / 2 - 0.5, None, ALU.add))
            assert done[0] == C_MASK
            mark(v.tensor_scalar(slots[:], ids[:, 0:NSLOT], first[:, 0:1], None, ALU.add))
            link(v.tensor_scalar(w_slots[:], w_slot0[:], q_blk[:, 0:1], None, ALU.add))
            for n in range(NSLOT + NWC):
                at, to = (slots[:, n:n + 1], win[:, n:n + 1]) if n < NSLOT else \
                    (w_slots[:, n - NSLOT:n - NSLOT + 1], wid[:, n - NSLOT:n - NSLOT + 1])
                link(v.scalar_tensor_tensor(junk[:], ids[:], at, table[:], ALU.is_equal, ALU.mult, accum_out=to))
            assert done[0] == C_IDS
            link(v.tensor_scalar(tau[:], tau0[:], rest[:, 0:1], None, ALU.subtract))
            link(v.tensor_scalar(cover[:], tau[:], 0.0, None, ALU.is_ge))
            link(v.scalar_tensor_tensor(cover[:].rearrange("p c o -> p (c o)"), tau[:].rearrange("p c o -> p (c o)"),
                                        float(T), cover[:].rearrange("p c o -> p (c o)"), ALU.is_lt, ALU.mult))
            link(v.tensor_scalar(token[:], tau[:], tok0[:, 0:1], None, ALU.add))
            dve.wait_ge(c_pe, 1)
            mark(v.tensor_copy(win_t[:], q_bank[0:NSLOT, 0:B]))
            mark(v.tensor_copy(wid_t[:], q_bank[0:NWC, P:2 * P]))
            assert done[0] == C_TURNED
            dve.wait_ge(ld_blk, 16 * 9)
            for c in range(NWC):
                mark(v.scalar_tensor_tensor(beats[:, c, :], all_wid[:], wid[:, c:c + 1], later[:, c, :],
                                            ALU.is_equal, ALU.mult))
                mark(v.tensor_scalar(match[:, c, :], all_blk[:], wid[:, c:c + 1], None, ALU.is_equal))
            assert done[0] == C_BEATS
            v.tensor_scalar(idx_old[:], row_blk[:], float(BLOCK), off_in[0:KC, 0:1], ALU.mult, ALU.add
                            ).then_inc(idx_ok, 1)
            dve.wait_ge(c_pe, 2)
            link(v.scalar_tensor_tensor(alive[:].rearrange("p c o -> p (c o)"), q_bank[:, 0:NWC * BLOCK], 0.5,
                                        cover[:].rearrange("p c o -> p (c o)"), ALU.is_lt, ALU.mult))
            dve.wait_ge(filled, 2)
            for j in range(SC):
                mark(v.tensor_tensor(placed[:, :, j, BLOCK * j:BLOCK * j + BLOCK], alive[:], token[:], ALU.mult))
            assert done[0] == C_PLACED
            dve.wait_ge(c_pe, 3)
            winner = k_bank[0][0:KC, 0:NKC * B]
            link(v.tensor_scalar(far[:], winner, 0.5, FAR, ALU.is_lt, ALU.mult))
            v.scalar_tensor_tensor(idx_new[:].rearrange("p c b -> p (c b)"), winner, -1.0, far[:], ALU.add, ALU.add
                                   ).then_inc(idx_ok, 1)

            def query_squares(m):
                for out, table_, i in ((q_cos, cos, 0), (q_sin, sin, 1)):
                    v.tensor_tensor(out[:].rearrange("p (a f) -> p a f", a=2),
                                    table_[:, bass.ds(m * HALF, HALF)].unsqueeze(1).to_broadcast([P, 2, HALF]),
                                    one_qs[:, i, :].rearrange("p (a f) -> p a f", a=2), ALU.mult)
                dve.wait_ge(act_sq, m + 1)
                v.tensor_reduce(q_ss[:], q_sq[:], AX.X, ALU.add).then_inc(dve_qc, 1)
                dve.wait_ge(dve_qc, 3 * m + 1)
                v.tensor_scalar(q_ss[:], q_ss[:], 1.0 / HD, EPS, ALU.mult, ALU.add).then_inc(dve_ms, 1)

            def queries(m, h):
                dve.wait_ge(act_qr, 2 * m + 2)
                v.tensor_tensor(q_r2[:], q_r0[:], q_r0[:], ALU.mult).then_inc(dve_q, 1)
                dve.wait_ge(dve_q, 6 * m + 1)
                v.scalar_tensor_tensor(q_r2[:], q_r2[:], -0.5, q_ss[:], ALU.mult, ALU.mult).then_inc(dve_q, 1)
                dve.wait_ge(dve_q, 6 * m + 2)
                v.scalar_tensor_tensor(q_rs[:], q_r2[:], 1.5, q_r0[:], ALU.add, ALU.mult).then_inc(dve_q, 1)
                dve.wait_ge(dve_q, 6 * m + 3)
                v.tensor_tensor(q_n[:], q_in[h][:], q_rs[:].unsqueeze(2).to_broadcast([P, H, HD]), ALU.mult
                                ).then_inc(dve_q, 1)
                dve.wait_ge(dve_q, 6 * m + 4)
                wait(dve, pe_q, m)
                for half in range(2):
                    v.tensor_tensor(q_rot[:, :, HALF * half:HALF * half + HALF],
                                    q_n[:, :, HALF * (1 - half):HALF * (1 - half) + HALF],
                                    q_sin[:, HALF * half:HALF * half + HALF].unsqueeze(1)
                                    .to_broadcast([P, H, HALF]), ALU.mult).then_inc(dve_qc, 1)
                v.tensor_tensor(q_sq[:], q_n[:], q_cos[:].unsqueeze(1).to_broadcast([P, H, HD]), ALU.mult
                                ).then_inc(dve_q, 1)
                dve.wait_ge(dve_q, 6 * m + 5)
                dve.wait_ge(dve_qc, 3 * m + 3)
                v.tensor_tensor(q_rot[:], q_rot[:], q_sq[:], ALU.add).then_inc(dve_q, 1)

            def masks(m, b):
                dve.wait_ge(act_far, 2 * m + b + 1)
                v.tensor_scalar(mask[b][:], far2[:], float(WINDOW // 2) ** 2, NEG, ALU.is_gt, ALU.mult
                                ).then_inc(dve_mask, 1)

            def maxima(m, u):
                b = u // 4
                wait(dve, act_e, 8 * m + u - 1)
                dve.wait_ge(dve_mask, 2 * m + b + 1)
                wait(dve, pe_sc, 8 * m + u + 1, dve_mark)
                v.tensor_tensor_reduce(sm[u % 2][:], score[u % 2], mask[b][:], 1.0, NEG * 4, ALU.add, ALU.max,
                                       top[u % 2][:]).then_inc(dve_sm, 1)
                dve.wait_ge(dve_sm, 8 * m + u + 1)
                v.tensor_scalar(ntop[u % 2][:], top[u % 2][:], -SCALE, None, ALU.mult).then_inc(dve_nt, 1)

            def norms(m, u):
                dve.wait_ge(act_e, 8 * m + u + 1)
                v.reciprocal(share[u % 2][:], total[u % 2][:]).then_inc(dve_sh, 1)
                dve.wait_ge(dve_sh, 8 * m + u + 1)
                v.tensor_scalar(prob[u % 2][:], prob[u % 2][:], share[u % 2][:], None, ALU.mult).then_inc(dve_p, 1)

            def router_score(m, h):
                dve.wait_ge(act_a, m + 1)
                v.tensor_tensor_reduce(r_junk[:], a_sb[h][:], w_r[:], 1.0, 0.0, ALU.mult, ALU.add, r_s[:]
                                       ).then_inc(dve_rc, 1)
                dve.wait_ge(dve_rc, 6 * m + 1)
                v.tensor_tensor(r_s[:], r_s[:], b_r[:], ALU.add).then_inc(dve_rc, 1)
                dve.wait_ge(dve_rc, 6 * m + 2)
                v.tensor_scalar(r_diag[:], ident[:], r_s[:], None, ALU.mult).then_inc(dve_diag, 1)

            def router_keep(m, h):
                row = a_bank[:, 0:P]
                dve.wait_ge(pe_row, m + 1)
                v.tensor_tensor_reduce(r_junk[:, 0:P], row, ident[:], 1.0, 0.0, ALU.mult, ALU.add, r_own[:]
                                       ).then_inc(dve_rc, 1)
                dve.wait_ge(dve_rc, 6 * m + 3)
                v.scalar_tensor_tensor(r_junk[:, P:2 * P], row, r_own[:], own[:], ALU.is_gt, ALU.mult,
                                       accum_out=r_gt[:]).then_inc(dve_rc, 1)
                v.scalar_tensor_tensor(r_junk[:, 2 * P:3 * P], row, r_own[:], before[:], ALU.is_equal, ALU.mult,
                                       accum_out=r_eq[:]).then_inc(dve_rc, 1)
                dve.wait_ge(dve_rc, 6 * m + 5)
                v.tensor_tensor(r_rank[:], r_gt[:], r_eq[:], ALU.add).then_inc(dve_rc, 1)
                dve.wait_ge(dve_rc, 6 * m + 6)
                v.tensor_scalar(keep[h][:], slot_no[:], r_rank[:], None, ALU.is_equal).then_inc(dve_keep, 1)

            def pair(m, i, h, last, nxt):
                for u in range(8):
                    if u < 7:
                        maxima(m, u + 1)
                    elif nxt:
                        maxima(m + 1, 0)
                    norms(m, u)
                    if u == 0:
                        masks(m, 1)
                        if nxt:
                            query_squares(m + 1)
                    if u == 1 and last:
                        router_score(m - 1, 1 - h)
                    if u == 2 and nxt:
                        queries(m + 1, 1 - h)
                    if u == 3 and last:
                        router_keep(m - 1, 1 - h)
                    if u == 4 and nxt:
                        masks(m + 1, 0)

            query_squares(0)
            queries(0, 0)
            masks(0, 0)
            maxima(0, 0)
            pairs(dve, pair)
            router_score(NG - 1, 1)
            router_keep(NG - 1, 1)

        @block.tensor
        def _(pe):
            pe.wait_ge(s_c, 16 * NC)
            pe.wait_ge(c_dve, C_IDS)
            nc.tensor.matmul(q_bank[0:NSLOT, 0:B], win[0:B, :], ident[0:B, 0:B], start=True, stop=True)
            nc.tensor.matmul(q_bank[0:NWC, P:2 * P], wid[:], ident[:], start=True, stop=True).then_inc(c_pe, 1)
            pe.wait_ge(c_dve, C_BEATS)
            for c in range(NWC):
                for c2 in range(NWC):
                    mm = nc.tensor.matmul(q_bank[:, BLOCK * c:BLOCK * c + BLOCK], beats[:, c2, P * c:P * c + P],
                                          cover[:, c2, :], start=(c2 == 0), stop=(c2 == NWC - 1))
            mm.then_inc(c_pe, 1)
            pe.wait_ge(c_dve, C_PLACED)
            for n in range(SC * NWC):
                j, c = n // NWC, n % NWC
                mm = nc.tensor.matmul(k_bank[0][0:KC, 0:NKC * B], placed[:, c, j, :],
                                      match[:, c, :].rearrange("p (c j b) -> p j c b", c=NKC, j=SC)[:, j, :, :],
                                      start=(n == 0), stop=(n == SC * NWC - 1))
            mm.then_inc(c_pe, 1)

            def turn_q(m, h):
                pe.wait_ge(dve_q, 6 * (m + 1))
                wait(pe, act_qt, 2 * m)
                qv = q_rot[:].rearrange("p h d -> p (h d)")
                for c in range(4):
                    mm = nc.tensor.transpose(q_bank[:, P * c:P * c + P], qv[:, P * c:P * c + P], ident[:])
                mm.then_inc(pe_q, 1)

            def turn_k(m, i, h, b):
                s = 2 * h + b
                pe.wait_ge(ld_kv[s], 16 * NKC * (i + 1))
                wait(pe, act_kt, 2 * (2 * m + b))
                for gp in range(2):
                    for c in range(NKC):
                        mm = nc.tensor.transpose(k_bank[gp][:, KC * c:KC * c + KC],
                                                 kv[s][:, c, P * gp:P * gp + P], ident[0:KC, 0:KC])
                mm.then_inc(pe_k, 1)

            def scores(m, h, u):
                b, gp, gq = unit(u)
                rows = slice(64 * gq, 64 * gq + 64)
                if u == 0:
                    pe.wait_ge(act_qt, 2 * (m + 1))
                if u % 4 == 0:
                    pe.wait_ge(act_kt, 2 * (2 * m + b + 1))
                wait(pe, dve_sm, 8 * m + u - 1)
                nc.tensor.matmul(score[u % 2], q_t[h][rows, gp, b, :, :].rearrange("p j t -> p (j t)"),
                                 k_t[b][rows, gp, :], start=True, stop=True).then_inc(pe_sc, 1)

            def turn_p(m, u):
                pe.wait_ge(dve_p, 8 * m + u + 1)
                wait(pe, act_pt, 8 * m + u)
                for c in range(NKC):
                    mm = nc.tensor.transpose(p_bank[:, P * c:P * c + P], prob[u % 2][:, KC * c:KC * c + KC], ident[:])
                mm.then_inc(pe_pt, 1)

            def values(m, h, u):
                b, gp, gq = unit(u)
                g = 2 * gp + gq
                pe.wait_ge(act_pt, 8 * m + u + 1)
                if u == 0:
                    wait(pe, act_o, m)
                for c in range(NKC):
                    mm = nc.tensor.matmul(o_bank[64 * gq:64 * gq + 64, 2 * gp:2 * gp + 2, T * b:T * b + T],
                                          kv[2 * h + b][:, c, G * HD + HD * g:G * HD + HD * g + HD],
                                          p_t[u % 2][:, c, :].rearrange("p (j t) -> p j t", j=2),
                                          start=(c == 0), stop=(c == NKC - 1))
                mm.then_inc(pe_pv, 1)

            def project(m, h):
                pe.wait_ge(act_o, m + 1)
                wait(pe, act_xs, 2 * m)
                for c in range(4):
                    mm = nc.tensor.matmul(a_bank, o_t[h][:, c, :], w_o[:, c, :], start=(c == 0), stop=(c == 3))
                mm.then_inc(pe_a, 1)

            def router_row(m):
                pe.wait_ge(act_a, m + 1)
                pe.wait_ge(dve_diag, m + 1)
                nc.tensor.matmul(a_bank[:, 0:P], ones[:], r_diag[:], start=True, stop=True).then_inc(pe_row, 1)

            def router_take(m, h):
                pe.wait_ge(dve_keep, m + 1)
                nc.tensor.matmul(a_bank[64 * h:64 * h + 64, P:2 * P], keep[h][:], ident[:], start=True, stop=True)
                for c in range(NCH):
                    mm = nc.tensor.matmul(a_bank[:, 2 * P + 2 * SEL * c:2 * P + 2 * SEL * c + 2 * SEL],
                                          a_sb[h][:, P * c:P * c + P], keep[h][:], start=True, stop=True)
                mm.then_inc(pe_xs, 1)

            def pair(m, i, h, last, nxt):
                i1 = i if h == 0 else i + 1
                for u in range(8):
                    if u < 7:
                        scores(m, h, u + 1)
                    elif nxt:
                        scores(m + 1, 1 - h, 0)
                    if u == 1:
                        turn_k(m, i, h, 1)
                    if u == 2 and last:
                        router_row(m - 1)
                    if u == 3 and nxt:
                        turn_q(m + 1, 1 - h)
                    if u == 4 and last:
                        router_take(m - 1, 1 - h)
                    if u == 5 and nxt:
                        turn_k(m + 1, i1, 1 - h, 0)
                    if u > 0:
                        values(m, h, u - 1)
                    turn_p(m, u)
                values(m, h, 7)
                project(m, h)

            pe.wait_ge(filled, 2)
            pe.wait_ge(idx_ok, 2)
            turn_q(0, 0)
            turn_k(0, 0, 0, 0)
            scores(0, 0, 0)
            pairs(pe, pair)
            router_row(NG - 1)
            router_take(NG - 1, 1)


C_MASK = 15
C_IDS = C_MASK + 2 + NSLOT + NWC
C_TURNED = C_IDS + 4 + 2
C_BEATS = C_TURNED + 2 * NWC
C_PLACED = C_BEATS + 1 + SC


def ffn_block(nc, A, S, out):
    NS = NG * 2 * SEL // TILE
    NTT = TILE // P
    with ExitStack() as ctx:
        def sb(name, shape, dt=F32):
            return ctx.enter_context(nc.sbuf_tensor(name, shape, dt))

        def sem(name):
            return ctx.enter_context(nc.semaphore(name))

        psum = ctx.enter_context(nc.psum_tensor("ffn_psum", [P, 8, 512], F32))
        h_bank = [psum[:, i, :] for i in range(3)]
        y_bank = [psum[:, 3 + i, :] for i in range(2)]
        s_bank = [psum[:, 5 + i, :] for i in range(3)]

        w1 = sb("w1", [P, NCH, DF])
        w2 = sb("w2", [P, NF, D])
        b1 = sb("b1", [P, NF])
        b2 = sb("b2", [P, D])
        xs = sb("xs_in", [P, NCH, TILE])
        hid = sb("ffn_hid", [P, NF, TILE])
        y_sb = [sb(f"y_sb{i}", [P, D]) for i in range(2)]
        keep_t = [sb(f"keep_in{i}", [P, P]) for i in range(2)]
        x1 = [sb(f"x1_in{i}", [P, NCH, P]) for i in range(2)]
        res = [sb(f"res{i}", [P, NCH, P]) for i in range(2)]

        s_w = [sem(f"s_w{i}") for i in range(3)]
        ld_xs = sem("ld_xs")
        ld_keep = [sem(f"ld_keep{i}") for i in range(2)]
        ld_x1 = [sem(f"ld2_x1{i}") for i in range(2)]
        st_res = [sem(f"st_res{i}") for i in range(2)]
        pe_h, pe_y, pe_s = sem("pe_h"), sem("pe2_y"), sem("pe_s")
        act_h, dve_y, dve_r, sp_mark = sem("act_h"), sem("dve_y"), sem("dve_r"), sem("sp_mark3")

        block = ctx.enter_context(nc.Block())

        @block.sync
        def _(sp):
            sp.dma_start(w1[:], A["w1"]).then_inc(s_w[0], 16)
            sp.dma_start(b1[:], A["b1"]).then_inc(s_w[0], 16)
            sp.dma_start(xs[:], S["xsp"][:, :, 0:TILE]).then_inc(ld_xs, 16)
            sp.dma_start(w2[:], A["w2"]).then_inc(s_w[1], 16)
            sp.dma_start(b2[:], A["b2"].partition_broadcast(P)).then_inc(s_w[1], 16)

            def loads(n, p):
                wait(sp, pe_s, 2 * (n - 1), sp_mark)
                sp.dma_start(keep_t[p][:], S["keep"][bass.ds(2 * n, 2)].rearrange("j s t -> (j s) t")
                             ).then_inc(ld_keep[p], 16)

            def tile(s, tt, more):
                n, p = NTT * s + tt, tt % 2
                loads(n, p)
                if more and tt == 0:
                    wait(sp, pe_h, NF * (s + 1), sp_mark)
                    sp.dma_start(xs[:], S["xsp"][:, :, bass.ds((s + 1) * TILE, TILE)]).then_inc(ld_xs, 16)
                for j in range(2):
                    wait(sp, dve_r, 2 * n + j - 1, sp_mark)
                    sp.dma_start(x1[j][:], S["x1p"][:, :, bass.ds((2 * n + j) * GRP, GRP)]).then_inc(ld_x1[j], 16)
                for j in range(2):
                    wait(sp, dve_r, 2 * n + j + 1, sp_mark)
                    sp.dma_start(out.rearrange("c p t -> p c t")[:, :, bass.ds((2 * n + j) * GRP, GRP)],
                                 res[j][:]).then_inc(st_res[j], 16)

            for tt in range(NTT):
                tile(0, tt, True)
            with sp.Fori(1, NS - 1) as s:
                for tt in range(NTT):
                    tile(s, tt, True)
            for tt in range(NTT):
                tile(NS - 1, tt, False)
            for j in range(2):
                sp.wait_ge(st_res[j], 16 * NG // 2)

        @block.scalar
        def _(act):
            act.wait_ge(s_w[0], 32)

            def tile(s):
                for f in range(NF):
                    k = NF * s + f
                    act.wait_ge(pe_h, k + 1)
                    if f == 0:
                        wait(act, pe_y, NTT * s)
                    nc.scalar.activation(hid[:, f, :], h_bank[f % 2], ACT.Gelu_apprx_tanh, bias=b1[:, f:f + 1]
                                         ).then_inc(act_h, 1)

            tile(0)
            with act.Fori(1, NS) as s:
                tile(s)

        @block.vector
        def _(dve):
            dve.wait_ge(s_w[1], 32)

            def tile(s, tt):
                n, p = NTT * s + tt, tt % 2
                dve.wait_ge(pe_y, n + 1)
                wait(dve, pe_s, 2 * (n - 1))
                nc.vector.tensor_tensor(y_sb[p][:], y_bank[p], b2[:], ALU.add).then_inc(dve_y, 1)
                for j in range(2):
                    dve.wait_ge(pe_s, 2 * n + j + 1)
                    dve.wait_ge(ld_x1[j], 16 * (n + 1))
                    wait(dve, st_res[j], 16 * n)
                    nc.vector.tensor_tensor(res[j][:].rearrange("p c t -> p (c t)"), s_bank[j],
                                            x1[j][:].rearrange("p c t -> p (c t)"), ALU.add).then_inc(dve_r, 1)

            for tt in range(NTT):
                tile(0, tt)
            with dve.Fori(1, NS) as s:
                for tt in range(NTT):
                    tile(s, tt)

        @block.tensor
        def _(pe):
            pe.wait_ge(s_w[0], 32)

            def tile(s):
                pe.wait_ge(ld_xs, 16 * (s + 1))
                for f in range(NF):
                    k = NF * s + f
                    wait(pe, act_h, k - 1)
                    for c in range(NCH):
                        mm = nc.tensor.matmul(h_bank[f % 2], w1[:, c, P * f:P * f + P], xs[:, c, :],
                                              start=(c == 0), stop=(c == NCH - 1))
                    mm.then_inc(pe_h, 1)
                pe.wait_ge(s_w[1], 32)
                for tt in range(NTT + 1):
                    if tt < NTT:
                        n, p = NTT * s + tt, tt % 2
                        wait(pe, dve_y, n - 1)
                        for f in range(NF):
                            if tt == 0:
                                pe.wait_ge(act_h, NF * s + f + 1)
                            mm = nc.tensor.matmul(y_bank[p], hid[:, f, P * tt:P * tt + P], w2[:, f, :],
                                                  start=(f == 0), stop=(f == NF - 1))
                        mm.then_inc(pe_y, 1)
                    if tt > 0:
                        scatter(NTT * s + tt - 1, (tt - 1) % 2, 2 * s + (tt - 1) // 2)

            def scatter(n, p, uses):
                pe.wait_ge(dve_y, n + 1)
                pe.wait_ge(ld_keep[p], 16 * (uses + 1))
                for j in range(2):
                    rows = slice(64 * j, 64 * j + 64)
                    wait(pe, dve_r, 2 * n + j - 1)
                    for c in range(NCH):
                        mm = nc.tensor.matmul(s_bank[j][:, P * c:P * c + P], y_sb[p][rows, P * c:P * c + P],
                                              keep_t[p][rows, :], start=True, stop=True)
                    mm.then_inc(pe_s, 1)

            tile(0)
            with pe.Fori(1, NS) as s:
                tile(s)


def program(nc, A, out):
    S = {}
    S["x1"] = nc.dram_tensor("x1_scratch", [NCH, P, NTOK], F32).ap()
    S["x1p"] = S["x1"].rearrange("c p t -> p c t")
    S["bc"] = nc.dram_tensor("bc_scratch", [2 * NST, NTOK], F32).ap()
    S["q"] = nc.dram_tensor("q_scratch", [NTOK, H * HD], F32).ap()
    S["kv_new"] = nc.dram_tensor("kv_scratch", [NTOK, KV], F32).ap()
    S["cos"] = nc.dram_tensor("cos_scratch", [P, NG * HALF], F32).ap()
    S["sin"] = nc.dram_tensor("sin_scratch", [P, NG * HALF], F32).ap()
    S["win"] = nc.dram_tensor("win_scratch", [NSLOT, B], F32).ap()
    S["wid"] = nc.dram_tensor("wid_scratch", [NWC, P], F32).ap()
    S["keep"] = nc.dram_tensor("keep_scratch", [NG, 2 * SEL, P], F32).ap()
    S["xs"] = nc.dram_tensor("xs_scratch", [NCH, P, NG * 2 * SEL], F32).ap()
    S["xsp"] = S["xs"].rearrange("c p t -> p c t")
    scan_block(nc, A, S)
    attention_block(nc, A, S)
    ffn_block(nc, A, S, out)


def layouts(inp):
    f = np.ascontiguousarray
    a = {}
    x = inp["x"]
    a["x_pairs"] = f(x.reshape(NG, P, D))
    a["x_t"] = f(x.reshape(NTOK, NCH, P).transpose(1, 2, 0))
    a["w_cond"] = f(inp["L0_cond_weights"].reshape(-1, HD))
    a["cond"] = f(inp["itok_B_1_198"].reshape(NG, 2).T)
    a["lens_pair"] = f(inp["itok_B_37_3939"].reshape(NG, 2).T)
    a["a_log"] = f(inp["L0_attn_A_log"].reshape(NCH, P, NST).transpose(1, 0, 2).reshape(P, -1))
    a["skip_d"] = f(inp["L0_attn_D"].reshape(NCH, P).T)
    a["dt_bias"] = f(inp["L0_attn_dt_proj_b"].reshape(NCH, P).T)
    wx = inp["L0_attn_x_proj_w"]
    wx = np.concatenate([wx[:P], wx[P:].reshape(2, NST, D).transpose(1, 0, 2).reshape(2 * NST, D)])
    a["w_x"] = f(wx.T.reshape(NCH, P, 160).transpose(1, 0, 2))
    a["w_dt"] = f(inp["L0_attn_dt_proj_w"].T)
    wq = inp["L0_cond2_Wq"].reshape(2, 2, 2, HD, D).transpose(0, 2, 1, 3, 4).reshape(D, D)
    w = np.concatenate([wq, inp["L0_cond2_Wk"], inp["L0_cond2_Wv"]])
    a["w_qkv"] = f(w.T.reshape(NCH, P, 1024).transpose(1, 0, 2))
    ks = inp["L0_cond2_k_norm_scale"]
    a["k_scale2"] = f(np.stack([ks, np.concatenate([ks[HALF:], ks[:HALF]])]))
    a["ident"] = np.eye(P, dtype=np.float32)
    a["part"] = f(np.stack([np.arange(P) % T, np.zeros(P)], 1).astype(np.float32))
    qs = inp["L0_cond2_q_norm_scale"]
    a["q_scale2"] = f(np.stack([qs, np.concatenate([qs[HALF:], qs[:HALF]])]))
    wo = inp["L0_cond2_Wo"].T.reshape(2, 2, 2, HD, D).transpose(0, 2, 1, 3, 4).reshape(NCH, P, D)
    a["w_o"] = f(wo.transpose(1, 0, 2))
    kb = inp["L0_cond2_k_blocks"].transpose(0, 2, 1, 3).reshape(NROW, G * HD)
    vb = inp["L0_cond2_v_blocks"].transpose(0, 2, 1, 3).reshape(NROW, G * HD)
    a["kv_rows"] = f(np.concatenate([kb, vb], axis=1))
    a["table"] = f(inp["itok_Bx257_0_4111"])
    a["lens"] = f(inp["itok_B_37_3939"].reshape(B, 1))
    a["lens_row"] = f(inp["itok_B_37_3939"])
    a["w_r"] = f(inp["L0_ffn_w_r"])
    a["b_r"] = f(inp["L0_ffn_b_r"].reshape(1))
    a["w1"] = f(inp["L0_ffn_w1"].reshape(NCH, P, DF).transpose(1, 0, 2))
    a["w2"] = f(inp["L0_ffn_w2"].reshape(NF, P, D).transpose(1, 0, 2))
    a["b1"] = f(inp["L0_ffn_b1"].reshape(NF, P).T)
    a["b2"] = f(inp["L0_ffn_b2"])

    p = np.arange(P)
    half, seq = p // T, p % T
    slot = 2 * np.arange(NWC) + half[:, None]
    a["ids"] = f(np.broadcast_to(np.arange(NBLK, dtype=np.float32), (P, NBLK)))
    a["w_slot0"] = f(slot.astype(np.float32))
    a["tau0"] = f((BLOCK * slot[:, :, None] + np.arange(BLOCK)).astype(np.float32))
    a["tok0"] = f((T * seq + 1).astype(np.float32)[:, None])
    a["off_in"] = f((p % BLOCK).astype(np.float32)[:, None])
    order = seq[:, None] * 8 + slot
    a["later"] = f((order[:, :, None] > order.T.reshape(-1)).astype(np.float32))
    a["dist"] = f((np.arange(NKEY) - seq[:, None]).astype(np.float32))
    same = half[:, None] == half
    a["own"] = f(same.astype(np.float32))
    a["before"] = f((same & (p < p[:, None])).astype(np.float32))
    at = np.arange(2 * SEL)
    a["slot_no"] = f(np.where(at // SEL == half[:, None], at % SEL, -1).astype(np.float32))
    a["inv_freq"] = (1.0 / np.float32(10000.0) ** (np.arange(HALF, dtype=np.float32) / HALF)).astype(np.float32)
    return a


def kernel(**inputs):
    import concourse.bacc as _bacc
    from concourse.bass_utils import run_bass_kernel_spmd as _run

    nc = _bacc.Bacc("TRN2", target_bir_lowering=False, num_devices=1)
    arrays = layouts({k: np.asarray(v) for k, v in inputs.items()})
    aps = {n: nc.dram_tensor(f"in_{n}", v.shape, mybir.dt.from_np(v.dtype), kind="ExternalInput").ap()
           for n, v in arrays.items()}
    out = nc.dram_tensor("out_t", (NCH, P, NTOK), F32, kind="ExternalOutput").ap()
    program(nc, aps, out)
    r = _run(nc, [{f"in_{n}": v for n, v in arrays.items()}], core_ids=[0])
    return np.ascontiguousarray(r.results[0]["out_t"].transpose(2, 0, 1).reshape(B, T, D))
```

```python
from contextlib import ExitStack

import numpy as np

import concourse.bass as bass
from concourse import mybir

F32 = mybir.dt.float32
I32 = mybir.dt.int32
ALU = mybir.AluOpType
ACT = mybir.ActivationFunctionType
AX = mybir.AxisListType

P = 128
B, T, D = 64, 64, 512
NTOK = B * T
NCH = D // P
NST = 16
TILE = 512
NT = NTOK // TILE
GRP = 128
NG = NTOK // GRP
H, G, HD = 8, 4, 64
HALF = HD // 2
BLOCK, WINDOW, NBLK = 16, 256, 257
NROW = B // 4 * NBLK * BLOCK
QW = H * HD + H
KV = 2 * G * HD
SCALE = 256.0 ** -0.5
EPS = 1e-6
NBUF = 8
NCONST = 11
NIDX = 11
NSLOT = 21
SC = 7
KC = SC * BLOCK
NKC = NSLOT // SC
NKEY = NSLOT * BLOCK
NKV = 8
NWS = 6
NWC = NWS // 2
SEL = T // 2
DF = 4 * D
NF = DF // P
NEG = -1.0e30
FAR = 1.0e6
MAGIC = 12582912.0
TWO_PI = (6.28125, 1.9340515136718750e-03, 1.2556659146e-06)


def wait(eng, sem, value, mark=None):
    if isinstance(value, int) and value <= 0:
        return
    eng.wait_ge(sem, value)
    if mark and not isinstance(value, int):
        eng.sem_inc(mark, 1)


def half(t, k):
    return 2 * t + k // 2


def scan_block(nc, A, S, W):
    with ExitStack() as ctx:
        def sb(name, shape, dt=F32):
            return ctx.enter_context(nc.sbuf_tensor(name, shape, dt))

        def sem(name):
            return ctx.enter_context(nc.semaphore(name))

        psum = ctx.enter_context(nc.psum_tensor("scan_psum", [P, 8, 512], F32))
        y = [psum[:, c, :] for c in range(NCH)]
        pro = [psum[:, 4 + i, :] for i in range(2)]
        qk = [psum[:, 6 + i, :] for i in range(2)]

        ident = sb("ident", [P, P])
        neg_a = sb("neg_a", [P, NCH * NST])
        a_log = sb("a_log", [P, NCH * NST])
        skip_d = sb("skip_d", [P, NCH])
        dt_bias = sb("dt_bias", [P, NCH])
        w_x = sb("w_x", [P, NCH, 160])
        w_dt = sb("w_dt", [P, D])
        w_qkv = sb("w_qkv", [P, NCH, 1024])
        bc = [sb(f"bc{i}", [P, 4, 2, TILE]) for i in range(2)]
        u = [sb(f"u{i}", [P, NCH, TILE]) for i in range(2)]
        delta = [sb(f"delta{i}", [P, NCH, TILE]) for i in range(2)]
        du = [sb(f"du{c}", [P, TILE]) for c in range(NCH)]
        xt_in = [sb(f"xt_in{i}", [P, TILE]) for i in range(2)]
        resid = [sb(f"resid{i}", [P, TILE]) for i in range(2)]
        x1 = [sb(f"x1_{c}", [P, TILE]) for c in range(NCH)]
        decay = sb("decay", [P, NBUF, TILE])
        dbu = sb("dbu", [P, 4, TILE])
        hid = sb("hid", [P, NBUF, TILE])
        hc = sb("hc", [P, NBUF, TILE])

        x_pair = [sb(f"x_pair{i}", [P, D]) for i in range(2)]
        w_rows = [sb(f"w_rows{i}", [P, HD]) for i in range(2)]
        w_pair = [sb(f"w_pair{i}", [P, 2 * HD]) for i in range(2)]
        drg = sb("drg", [P, GRP])
        bcg = [sb(f"bcg{i}", [32, GRP]) for i in range(2)]
        zg = sb("zg", [P, NCH, GRP])
        sp_a = sb("sp_a", [P, NCH, GRP])
        sp_l = sb("sp_l", [P, NCH, GRP])

        qg = [sb(f"qg{i}", [P, QW]) for i in range(2)]
        kvg = [sb(f"kvg{i}", [P, KV]) for i in range(2)]
        k_raw = sb("k_raw", [P, G, HD])
        sq_junk = sb("sq_junk", [P, G + H, HD])
        k_n = sb("k_n", [P, G, HD])
        k_rot = sb("k_rot", [P, G, HD])
        k_par = sb("k_par", [P, G, HD])
        n_ss, n_ms, n_ln, n_r0, n_r2, n_r3 = (sb(n, [P, G + H]) for n in ("n_ss", "n_ms", "n_ln", "n_r0", "n_r2", "n_r3"))
        k_rs = sb("k_rs", [P, G])
        k_cos = sb("k_cos", [P, HD])
        k_sin = sb("k_sin", [P, HD])
        k_scale = sb("k_scale", [P, 2, HD])
        one_ks = sb("one_ks", [P, 2, HD])

        cond_i = sb("cond_i", [P, NG], I32)
        len_i = sb("len_i", [P, NG], I32)
        cond_f = sb("cond_f", [P, NG])
        pos_f = sb("pos_f", [P, NG])
        part = sb("part", [P, 2])
        inv = sb("inv", [P, HALF])
        w_idx = sb("w_idx", [P, NG], I32)
        w_now = [sb(f"w_now{i}", [P, 1], I32) for i in range(2)]
        ang, turns, rem = (hid[:, 2 * i:2 * i + 2, :].rearrange("p a b -> p (a b)") for i in range(3))
        cos = sb("cos", [P, NG * HALF])
        sin = sb("sin", [P, NG * HALF])

        def lay(buf, at, *shape):
            n = int(np.prod(shape))
            view = buf[:, at:at + n]
            if len(shape) == 3:
                view = view.rearrange("p (a b c) -> p a b c", b=shape[1], c=shape[2])
            elif len(shape) == 2:
                view = view.rearrange("p (a b) -> p a b", b=shape[1])
            return view

        flat = [decay[:].rearrange("p a b -> p (a b)"), bc[1][:].rearrange("p a b c -> p (a b c)"),
                hc[:].rearrange("p a b -> p (a b)")]
        nw = NWC * P
        placed = lay(flat[0], 0, NWC, SC, KC)
        all_blk = lay(flat[0], NWC * SC * KC, NSLOT * B)
        later = lay(flat[1], 0, NWC, nw)
        beats = lay(flat[1], NWC * nw, NWC, nw)
        all_wid = lay(flat[1], 2 * NWC * nw, nw)
        ids, table, junk = (lay(flat[1], (2 * NWC + 1) * nw + i * NBLK, NBLK) for i in range(3))
        match = lay(flat[2], 0, NWC, NSLOT * B)
        table_i = sb("table_i", [P, NBLK], I32)
        lens_i = sb("lens_i", [P, 1 + B], I32)
        sh_i = sb("sh_i", [P, 1 + B], I32)
        small = [t[:] for t in x1]
        lens_f, q_blk, rest, first = (lay(small[0], i * (1 + B), 1 + B) for i in range(4))
        slots, win = (lay(small[0], 4 * (1 + B) + i * NSLOT, NSLOT) for i in range(2))
        w_slots, w_slot0, wid = (lay(small[0], 4 * (1 + B) + 2 * NSLOT + i * NWC, NWC) for i in range(3))
        tau0, tau, cover, alive, token = (lay(small[1], i * NWC * BLOCK, NWC, BLOCK) for i in range(5))
        off_in, tok0 = (lay(small[1], 5 * NWC * BLOCK + i, 1) for i in range(2))
        win_t = lay(small[2], 0, B)[0:NSLOT]
        wid_t = lay(small[2], B, P)[0:NWC]
        row_blk = lay(small[2], B + P, NKC, B)[0:KC]
        far = lay(small[3], 0, NKC * B)[0:KC]
        mask_at, idx_old, idx_new = W["mask_at"], W["idx_old"], W["idx_new"]

        s_idx, c_idx, c_pe, filled = sem("s_idx"), sem("c_idx"), sem("c_pe"), sem("filled")
        st_blk, ld_blk, idx_ok = sem("st_blk"), sem("ld_blk"), sem("idx_ok")
        s_cond, s_const, s_qkvw = sem("s_cond"), sem("s_const"), sem("s_qkvw")
        c_a, c_neg, c_dve, c_sin = sem("c_a"), sem("c_neg"), sem("c_dve"), sem("c_sin")
        widx_ok, wnow_ok, wpair_ok = sem("widx_ok"), sem("wnow_ok"), sem("wpair_ok")
        rope_ok, zero_ok, zpair_ok = sem("rope_ok"), sem("zero_ok"), sem("zpair_ok")
        ld_xp = [sem(f"ld_xp{i}") for i in range(2)]
        ld_w = [sem(f"ld_w{i}") for i in range(2)]
        ld_xt = [sem(f"ld_xt{i}") for i in range(2)]
        ld_bc = [sem(f"ld_bc{i}") for i in range(2)]
        st_bc = [sem(f"st_bc{i}") for i in range(4)]
        st_x1 = [sem(f"st_x1{i}") for i in range(NCH)]
        st_q = [sem(f"st_q{i}") for i in range(2)]
        st_kv = [sem(f"st_kv{i}") for i in range(2)]
        st_rope = sem("st_rope")
        pe_u, pe_x, pe_z, pe_res = sem("pe_u"), sem("pe_x"), sem("pe_z"), sem("pe_res")
        pe_hc, pe_kv, pe_q = sem("pe_hc"), sem("pe_kv"), sem("pe_q")
        act_u, act_dr, act_sp = sem("act_u"), sem("act_dr"), sem("act_sp")
        act_exp, act_y, act_kv, act_q = sem("act_exp"), sem("act_y"), sem("act_kv"), sem("act_q")
        dve_du, dve_res, dve_dbu, dve_h = sem("dve_du"), sem("dve_res"), sem("dve_dbu"), sem("dve_h")
        dve_z, dve_dl, dve_ks, dve_kt = sem("dve_z"), sem("dve_dl"), sem("dve_ks"), sem("dve_kt")
        dve_ms, act_rs, act_qs, dve_qr = sem("dve_ms"), sem("act_rs"), sem("act_qs"), sem("dve_qr")
        pool_hc, pool_k = sem("pool_hc"), sem("pool_k")
        sp_mark, pool_mark = sem("sp_mark"), sem("pool_mark")

        C_MASK = 12
        C_IDS = C_MASK + 2 + NSLOT + NWC
        C_TURNED = C_IDS + 4 + 2
        C_BEATS = C_TURNED + 2 * NWC
        C_PLACED = C_BEATS + 1 + SC

        block = ctx.enter_context(nc.Block())

        class Parts:

            def __init__(self, t, q):
                s = 4 * t + q if isinstance(t, int) else None

                def within(lo, hi):
                    return s is None or lo <= s <= hi

                self.scan = within(0, 4 * NT - 1)
                self.next_scan = within(-1, 4 * NT - 2)
                self.gather = within(-6, NG - 7)
                self.first = within(-5, NG - 6)
                self.second = within(-4, NG - 5)
                self.third = within(4, NG + 3)
                self.fourth = within(5, NG + 4)

        def quarters(eng, quarter):
            def run(t, h, some=range(4)):
                for q in some:
                    quarter(t, h, q, Parts(t, q))

            run(-2, 0, [3])
            run(-1, 1)
            run(0, 0)
            run(1, 1)
            with eng.Fori(1, NT // 2 - 1) as i:
                run(2 * i, 0)
                run(2 * i + 1, 1)
            run(NT - 2, 0)
            run(NT - 1, 1)
            run(NT, 0)
            run(NT + 1, 1, [0])

        @block.sync
        def _(sp):
            def load_x(g, p):
                wait(sp, pe_u, g - 1, sp_mark)
                sp.dma_start(x_pair[p][:], A["x_pairs"][g]).then_inc(ld_xp[p], 16)

            for h in range(2):
                rows = slice(64 * h, 64 * h + 64)
                sp.dma_start(cond_i[rows, :], A["cond"][h].partition_broadcast(64)).then_inc(s_cond, 16)
            sp.dma_start(part[:], A["part"]).then_inc(s_cond, 16)
            load_x(0, 0)
            for dst, src in ((w_x, A["w_x"]), (w_dt, A["w_dt"]), (dt_bias, A["dt_bias"]), (a_log, A["a_log"]),
                             (skip_d, A["skip_d"]), (ident, A["ident"])):
                sp.dma_start(dst[:], src).then_inc(s_const, 16)
            sp.dma_start(inv[:], A["inv_freq"].partition_broadcast(P)).then_inc(s_const, 16)
            for h in range(2):
                rows = slice(64 * h, 64 * h + 64)
                sp.dma_start(len_i[rows, :], A["lens_pair"][h].partition_broadcast(64)).then_inc(s_const, 16)
            for i in range(2):
                sp.dma_start(k_scale[:, i, :], A["k_scale2"][i].partition_broadcast(P)).then_inc(s_const, 16)

            def spread_ids():
                sp.wait_ge(c_idx, C_TURNED)
                sp.dma_start(S["win"], win_t).then_inc(st_blk, 16)
                sp.dma_start(S["wid"], wid_t).then_inc(st_blk, 16)
                sp.wait_ge(st_blk, 32)
                by_slot = S["win"].rearrange("(c j) b -> j c b", j=SC)
                for j in range(SC):
                    sp.dma_start(row_blk[BLOCK * j:BLOCK * j + BLOCK, :, :], by_slot[j].partition_broadcast(BLOCK)
                                 ).then_inc(ld_blk, 16)
                sp.dma_start(all_blk, S["win"].rearrange("s b -> (s b)").partition_broadcast(P)).then_inc(ld_blk, 16)
                sp.dma_start(all_wid, S["wid"].rearrange("s b -> (s b)").partition_broadcast(P)).then_inc(ld_blk, 16)

            def load_bc(t, q):
                if q == 0:
                    for i in range(4):
                        wait(sp, st_bc[i], 16 * (t + 1), sp_mark)
                wait(sp, pool_hc, 16 * (4 * t + q - 1), sp_mark)
                sp.dma_start(bc[q % 2][:].rearrange("p a b c -> p (a b) c"),
                             S["bc"][8 * q:8 * q + 8, bass.ds(t * TILE, TILE)].partition_broadcast(P)
                             ).then_inc(ld_bc[q % 2], 16)

            def load_xt(t, c):
                wait(sp, dve_res, 4 * t + c - 1, sp_mark)
                sp.dma_start(xt_in[c % 2][:], A["x_t"][c][:, bass.ds(t * TILE, TILE)]).then_inc(ld_xt[c % 2], 16)

            def store_x1(t, c):
                wait(sp, act_y, 4 * t + c + 1, sp_mark)
                sp.dma_start(S["x1"][c][:, bass.ds(t * TILE, TILE)], x1[c][:]).then_inc(st_x1[c], 16)

            def quarter(t, h, q, parts):
                s = 4 * t + q
                if parts.gather:
                    load_x(s + 6, q % 2)
                if parts.next_scan:
                    if isinstance(t, int) and t == 0 and q == 0:
                        sp.wait_ge(idx_ok, 2)
                    load_bc(t if q < 3 else t + 1, (q + 1) % 4)
                if q == 3 and parts.next_scan:
                    load_xt(t + 1, 0)
                    load_xt(t + 1, 1)
                if q == 0 and parts.third:
                    store_x1(t - 1, 3)
                if q == 0 and parts.scan:
                    load_xt(t, 2)
                    load_xt(t, 3)
                if parts.fourth:
                    g, p = s - 5, (q + 1) % 2
                    wait(sp, act_q, g + 1, sp_mark)
                    wait(sp, dve_qr, g + 1, sp_mark)
                    sp.dma_start(S["q"][bass.ds(g * GRP, GRP), :], qg[p][:]).then_inc(st_q[p], 16)
                if parts.first:
                    g = s + 5
                    wait(sp, act_dr, 2 * (g + 1), sp_mark)
                    sp.dma_start(S["bc"][:, bass.ds(g * GRP, GRP)], bcg[(q + 1) % 2][:]
                                 ).then_inc(st_bc[(q + 1) % 4], 16)
                if isinstance(t, int) and t == -1 and q == 0:
                    sp.dma_start(w_qkv[:], A["w_qkv"]).then_inc(s_qkvw, 16)
                if parts.fourth:
                    wait(sp, pool_k, 5 * (g_kv(t, q) + 1), sp_mark)
                    sp.dma_start(S["kv_new"][bass.ds(g_kv(t, q) * GRP, GRP), :], kvg[(q + 1) % 2][:]
                                 ).then_inc(st_kv[(q + 1) % 2], 16)
                if q == 3 and parts.scan:
                    for c in range(3):
                        store_x1(t, c)
                if isinstance(t, int) and t == -2:
                    spread_ids()

            def g_kv(t, q):
                return 4 * t + q - 5

            quarters(sp, quarter)
            sp.wait_ge(rope_ok, 1)
            sp.dma_start(S["cos"], cos[:]).then_inc(st_rope, 16)
            sp.dma_start(S["sin"], sin[:]).then_inc(st_rope, 16)
            sp.wait_ge(st_rope, 32)
            for c in range(NCH):
                sp.wait_ge(st_x1[c], 16 * NT)
            for i in range(2):
                sp.wait_ge(st_q[i], 16 * NG // 2)
                sp.wait_ge(st_kv[i], 16 * NG // 2)

        @block.gpsimd
        def _(pool):
            def weights(g, p):
                wait(pool, wpair_ok, 2 * g - 2, pool_mark)
                pool.tensor_copy(w_now[p][:], w_idx[:, bass.ds(g, 1)]).then_inc(wnow_ok, 1)
                wait(pool, wnow_ok, g + 1, pool_mark)
                pool.indirect_dma_start(w_rows[p][:], None, A["w_cond"],
                                        bass.IndirectOffsetOnAxis(ap=w_now[p][:, :], axis=0)
                                        ).then_inc(ld_w[p], 16)

            def keys(g, p):
                k = 5 * g
                pool.wait_ge(dve_ks, g + 1)
                pool.tensor_tensor(k_n[:], k_raw[:], k_rs[:].unsqueeze(2).to_broadcast([P, G, HD]),
                                   ALU.mult).then_inc(pool_k, 1)
                pool.wait_ge(pool_k, k + 1)
                for i in range(2):
                    pool.tensor_tensor(k_rot[:, :, HALF * i:HALF * i + HALF],
                                       k_n[:, :, HALF * (1 - i):HALF * (1 - i) + HALF],
                                       k_sin[:, HALF * i:HALF * i + HALF].unsqueeze(1)
                                       .to_broadcast([P, G, HALF]), ALU.mult).then_inc(pool_k, 1)
                pool.tensor_tensor(k_par[:], k_n[:], k_cos[:].unsqueeze(1).to_broadcast([P, G, HD]),
                                   ALU.mult).then_inc(pool_k, 1)
                pool.wait_ge(pool_k, k + 4)
                pool.tensor_tensor(kvg[p][:, 0:G * HD].rearrange("p (g d) -> p g d", g=G), k_par[:], k_rot[:],
                                   ALU.add).then_inc(pool_k, 1)

            def quarter(t, h, q, parts):
                s = 4 * t + q
                if isinstance(t, int) and s == 0:
                    pool.wait_ge(idx_ok, 2)
                for n in range(16):
                    if parts.scan:
                        i, e = n % 4, 16 * s + n
                        if n == 0:
                            pool.wait_ge(ld_bc[q % 2], 16 * (half(t, q) + 1))
                        wait(pool, pe_hc, e + 1 - NBUF)
                        pool.wait_ge(dve_h, e + 1)
                        pool.tensor_tensor(hc[:, n % NBUF, :], hid[:, n % NBUF, :], bc[q % 2][:, i, 1, :],
                                           ALU.mult).then_inc(pool_hc, 1)
                    if n == 3 and parts.gather:
                        weights(s + 6, q % 2)
                    if n == 10 and parts.fourth:
                        keys(s - 5, (q + 1) % 2)

            for i in range(2):
                pool.memset(w_pair[i][:], 0.0).then_inc(zpair_ok, 1)
            pool.wait_ge(widx_ok, 1)
            weights(0, 0)
            pool.memset(placed, 0.0).then_inc(filled, 1)
            quarters(pool, quarter)
            for i in range(2):
                pool.wait_ge(ld_w[i], 16 * NG // 2)

        @block.scalar
        def _(act):
            def quarter(t, h, q, parts):
                s = 4 * t + q

                def weight_blocks():
                    g, p = s + 5, (q + 1) % 2
                    act.wait_ge(ld_w[p], 16 * (half(t, q + 5) + 1))
                    wait(act, pe_u, g - 1)
                    for b in range(2):
                        rows = slice(64 * b, 64 * b + 64)
                        nc.scalar.copy(w_pair[p][rows, HD * b:HD * b + HD], w_rows[p][rows, :]).then_inc(wpair_ok, 1)

                def sums(t, c):
                    act.wait_ge(pe_hc, 64 * t + 48 + 4 * c + 4)
                    wait(act, pe_q, 4 * (4 * t - 1) + c + 1)
                    wait(act, st_x1[c], 16 * t)
                    nc.scalar.copy(x1[c][:], y[c]).then_inc(act_y, 1)

                def take_u():
                    g = s + 5
                    act.wait_ge(pe_u, g + 1)
                    wait(act, dve_res, 4 * (t if q == 3 else t - 1) + 4)
                    k = (q + 1) % 4
                    nc.scalar.copy(u[h if q == 3 else 1 - h][:, :, GRP * k:GRP * k + GRP],
                                   pro[0].rearrange("p (c t) -> p c t", c=NCH)).then_inc(act_u, 1)

                def take_x():
                    g, p = s + 5, (q + 1) % 2
                    act.wait_ge(pe_x, g + 1)
                    wait(act, st_bc[(q + 3) % 4], 16 * (t + (q + 3) // 4))
                    nc.scalar.copy(drg[:], pro[1][:, 0:GRP]).then_inc(act_dr, 1)
                    nc.scalar.copy(bcg[p][:], pro[1][0:32, GRP:2 * GRP]).then_inc(act_dr, 1)

                def softplus_exp():
                    g = s + 4
                    act.wait_ge(dve_z, g + 1)
                    wait(act, act_sp, 3 * g)
                    nc.scalar.activation(sp_a[:], zg[:], ACT.Abs).then_inc(act_sp, 1)
                    act.wait_ge(act_sp, 3 * g + 1)
                    nc.scalar.activation(sp_a[:], sp_a[:], ACT.Exp, scale=-1.0).then_inc(act_sp, 1)

                def softplus_ln():
                    g = s + 4
                    act.wait_ge(act_sp, 3 * g + 2)
                    wait(act, dve_dl, g)
                    nc.scalar.activation(sp_l[:], sp_a[:], ACT.Ln, bias=1.0).then_inc(act_sp, 1)

                def take_kv():
                    g, p = s - 5, (q + 1) % 2
                    act.wait_ge(pe_kv, g + 1)
                    wait(act, st_kv[p], 16 * half(t, q - 5))
                    nc.scalar.copy(kvg[p][:, G * HD:KV], qk[0][:, G * HD:KV]).then_inc(act_kv, 1)
                    wait(act, pool_k, 5 * g)
                    nc.scalar.copy(k_raw[:].rearrange("p g d -> p (g d)"), qk[0][:, 0:G * HD]).then_inc(act_kv, 1)
                    wait(act, dve_ms, g)
                    for j in range(G):
                        nc.scalar.activation(sq_junk[:, j, :], qk[0][:, HD * j:HD * j + HD], ACT.Square,
                                             accum_out=n_ss[:, j:j + 1]).then_inc(act_kv, 1)

                def key_rms():
                    g = s - 5
                    act.wait_ge(dve_ms, g + 1)
                    wait(act, dve_ks, g)
                    nc.scalar.activation(n_ln[:], n_ms[:], ACT.Ln).then_inc(act_rs, 1)
                    act.wait_ge(act_rs, 2 * g + 1)
                    nc.scalar.activation(n_r0[:], n_ln[:], ACT.Exp, scale=-0.5).then_inc(act_rs, 1)

                def take_q():
                    g, p = s - 5, (q + 1) % 2
                    act.wait_ge(pe_q, 4 * (g + 1))
                    wait(act, st_q[p], 16 * half(t, q - 5))
                    nc.scalar.copy(qg[p][:, 0:D], qk[1]).then_inc(act_q, 1)
                    for j in range(H):
                        nc.scalar.activation(sq_junk[:, G + j, :], qk[1][:, HD * j:HD * j + HD], ACT.Square,
                                             accum_out=n_ss[:, G + j:G + j + 1]).then_inc(act_qs, 1)

                if parts.scan and q == 0:
                    act.wait_ge(dve_dl, 4 * (t + 1))
                for n in range(16):
                    if parts.scan:
                        c, i, e = n // 4, n % 4, 16 * s + n
                        wait(act, dve_h, e + 1 - NBUF)
                        nc.scalar.activation(
                            decay[:, n % NBUF, :].rearrange("p (b t) -> p b t", t=T)[:, :, 1:T],
                            delta[h][:, c, :].rearrange("p (b t) -> p b t", t=T)[:, :, 1:T],
                            ACT.Exp, scale=neg_a[:, NST * c + 4 * q + i:NST * c + 4 * q + i + 1]).then_inc(act_exp, 1)
                    if n == 0 and parts.first:
                        weight_blocks()
                    if n == 1 and parts.fourth:
                        take_kv()
                    if n == 2 and parts.fourth:
                        take_q()
                    if n == 3 and parts.second:
                        softplus_exp()
                    if n == 4 and q == 0 and parts.third:
                        sums(t - 1, 3)
                    if n == 6 and parts.first:
                        take_u()
                    if n == 7:
                        if parts.second:
                            softplus_ln()
                        if parts.fourth:
                            key_rms()
                    if n == 10 and parts.first:
                        take_x()
                    if n in (11, 13, 15) and q == 3 and parts.scan:
                        sums(t, (n - 11) // 2)

                if isinstance(t, int) and t == -1:
                    if q == 0:
                        act.wait_ge(s_const, 16 * NCONST)
                        nc.scalar.activation(neg_a[:], a_log[:], ACT.Exp).then_inc(c_neg, 1)
                    if q == 1:
                        act.wait_ge(c_sin, 1)
                        nc.scalar.activation(sin[:], rem, ACT.Sin).then_inc(c_a, 1)
                    if q == 2:
                        act.wait_ge(c_sin, 2)
                        nc.scalar.activation(cos[:], rem, ACT.Sin).then_inc(c_a, 1)
                    if q == 3:
                        act.wait_ge(zero_ok, 2)

            for dst, src in ((ids, A["ids"]), (w_slot0, A["w_slot0"]), (tau0, A["tau0"]),
                             (tok0, A["tok0"]), (off_in, A["off_in"]), (later, A["later"])):
                act.dma_start(dst, src).then_inc(s_idx, 16)
            for h in range(2):
                rows = slice(64 * h, 64 * h + 64)
                act.dma_start(table_i[rows, :], A["table"]).then_inc(s_idx, 16)
                act.dma_start(lens_i[rows, 0:1], A["lens"]).then_inc(s_idx, 16)
            act.dma_start(lens_i[:, 1:1 + B], A["lens_row"].partition_broadcast(P)).then_inc(s_idx, 16)
            act.wait_ge(zpair_ok, 2)
            quarters(act, quarter)

        @block.vector
        def _(dve):
            done = [0]

            def link(ins):
                done[0] += 1
                ins.then_inc(c_dve, 1)
                dve.wait_ge(c_dve, done[0])

            dve.wait_ge(s_cond, 16 * 3)
            link(nc.vector.tensor_copy(cond_f[:], cond_i[:]))
            link(nc.vector.tensor_scalar(cond_f[:], cond_f[:], 64.0, part[:, 0:1], ALU.mult, ALU.add))
            nc.vector.tensor_copy(w_idx[:], cond_f[:]).then_inc(widx_ok, 1)

            v = nc.vector
            count = [0]

            def mark(ins):
                count[0] += 1
                ins.then_inc(c_idx, 1)

            def chained(ins):
                mark(ins)
                dve.wait_ge(c_idx, count[0])

            dve.wait_ge(s_idx, 16 * NIDX)
            mark(v.tensor_copy(table, table_i[:]))
            mark(v.tensor_copy(lens_f, lens_i[:]))
            chained(v.tensor_scalar(sh_i[:], lens_i[:], 4, None, ALU.arith_shift_right))
            chained(v.tensor_copy(q_blk, sh_i[:]))
            chained(v.scalar_tensor_tensor(rest, q_blk, -float(BLOCK), lens_f, ALU.mult, ALU.add))
            chained(v.tensor_scalar(first, lens_f, -float(WINDOW - 1), 0.0, ALU.add, ALU.max))
            chained(v.tensor_copy(sh_i[:], first))
            chained(v.tensor_scalar(sh_i[:], sh_i[:], 4, None, ALU.arith_shift_right))
            chained(v.tensor_copy(first, sh_i[:]))
            chained(v.tensor_scalar(first, first, float(NBLK - NSLOT), None, ALU.min))
            chained(v.scalar_tensor_tensor(mask_at[:], first, float(BLOCK), lens_f, ALU.mult, ALU.subtract))
            chained(v.tensor_scalar(mask_at[:], mask_at[:], WINDOW / 2 - 0.5, None, ALU.add))
            assert count[0] == C_MASK
            mark(v.tensor_scalar(slots, ids[:, 0:NSLOT], first[:, 0:1], None, ALU.add))
            chained(v.tensor_scalar(w_slots, w_slot0, q_blk[:, 0:1], None, ALU.add))
            for n in range(NSLOT + NWC):
                at, to = (slots[:, n:n + 1], win[:, n:n + 1]) if n < NSLOT else \
                    (w_slots[:, n - NSLOT:n - NSLOT + 1], wid[:, n - NSLOT:n - NSLOT + 1])
                chained(v.scalar_tensor_tensor(junk, ids, at, table, ALU.is_equal, ALU.mult, accum_out=to))
            assert count[0] == C_IDS

            def turned_ids():
                chained(v.tensor_scalar(tau, tau0, rest[:, 0:1], None, ALU.subtract))
                chained(v.tensor_scalar(cover, tau, 0.0, None, ALU.is_ge))
                chained(v.scalar_tensor_tensor(cover.rearrange("p c o -> p (c o)"), tau.rearrange("p c o -> p (c o)"),
                                            float(T), cover.rearrange("p c o -> p (c o)"), ALU.is_lt, ALU.mult))
                chained(v.tensor_scalar(token, tau, tok0[:, 0:1], None, ALU.add))
                dve.wait_ge(c_pe, 1)
                mark(v.tensor_copy(win_t, y[0][0:NSLOT, 0:B]))
                mark(v.tensor_copy(wid_t, y[0][0:NWC, P:2 * P]))
                assert count[0] == C_TURNED

            def compare_ids():
                dve.wait_ge(ld_blk, 16 * 9)
                for c in range(NWC):
                    mark(v.scalar_tensor_tensor(beats[:, c, :], all_wid, wid[:, c:c + 1], later[:, c, :],
                                                ALU.is_equal, ALU.mult))
                    mark(v.tensor_scalar(match[:, c, :], all_blk, wid[:, c:c + 1], None, ALU.is_equal))
                assert count[0] == C_BEATS
                v.tensor_scalar(idx_old[:], row_blk, float(BLOCK), off_in[0:KC, 0:1], ALU.mult, ALU.add
                                ).then_inc(idx_ok, 1)

            def place_tokens():
                dve.wait_ge(c_pe, 2)
                chained(v.scalar_tensor_tensor(alive.rearrange("p c o -> p (c o)"), y[0][:, 0:NWC * BLOCK], 0.5,
                                            cover.rearrange("p c o -> p (c o)"), ALU.is_lt, ALU.mult))
                dve.wait_ge(filled, 1)
                for j in range(SC):
                    mark(v.tensor_tensor(placed[:, :, j, BLOCK * j:BLOCK * j + BLOCK], alive, token, ALU.mult))
                assert count[0] == C_PLACED

            def last_writers():
                dve.wait_ge(c_pe, 3)
                winner = y[1][0:KC, 0:NKC * B]
                chained(v.tensor_scalar(far, winner, 0.5, FAR, ALU.is_lt, ALU.mult))
                v.scalar_tensor_tensor(idx_new[:].rearrange("p c b -> p (c b)"), winner, -1.0, far, ALU.add, ALU.add
                                       ).then_inc(idx_ok, 1)
                v.memset(decay[:].rearrange("p i (b t) -> p (i b) t", t=T)[:, :, 0:1], 0.0).then_inc(zero_ok, 1)

            dve.wait_ge(s_const, 16 * NCONST)

            def tables(which):
                if which == 0:
                    link(nc.vector.tensor_copy(pos_f[:], len_i[:]))
                    link(nc.vector.tensor_scalar(pos_f[:], pos_f[:], part[:, 0:1], None, ALU.add))
                    link(nc.vector.tensor_tensor(ang.rearrange("p (g f) -> p g f", f=HALF),
                                                 pos_f[:].unsqueeze(2).to_broadcast([P, NG, HALF]),
                                                 inv[:].unsqueeze(1).to_broadcast([P, NG, HALF]), ALU.mult))
                quart, shift = ((0.0, 0.0), (0.25, float(np.float32(np.pi / 2))))[which]
                link(nc.vector.tensor_scalar(turns, ang, float(1 / (2 * np.pi)), quart, ALU.mult, ALU.add))
                link(nc.vector.tensor_scalar(turns, turns, MAGIC, None, ALU.add))
                link(nc.vector.tensor_scalar(turns, turns, MAGIC, None, ALU.subtract))
                if which:
                    dve.wait_ge(c_a, 1)
                link(nc.vector.scalar_tensor_tensor(rem, turns, -TWO_PI[0], ang, ALU.mult, ALU.add))
                link(nc.vector.scalar_tensor_tensor(rem, turns, -TWO_PI[1], rem, ALU.mult, ALU.add))
                link(nc.vector.scalar_tensor_tensor(rem, turns, -TWO_PI[2], rem, ALU.mult, ALU.add))
                link(nc.vector.tensor_scalar(rem, rem, shift, 3.1415925, ALU.add, ALU.min))
                nc.vector.tensor_scalar(rem, rem, -3.1415925, None, ALU.max).then_inc(c_sin, 1)

            def scales():
                nc.vector.tensor_scalar(one_ks[:, 0, :], k_scale[:, 0, :], 1.0, None, ALU.add)
                nc.vector.tensor_scalar(one_ks[:, 1, 0:HALF], k_scale[:, 1, 0:HALF], -1.0, -1.0, ALU.mult, ALU.add)
                link(nc.vector.tensor_scalar(one_ks[:, 1, HALF:HD], k_scale[:, 1, HALF:HD], 1.0, None, ALU.add))
                dve.wait_ge(c_neg, 1)
                nc.vector.tensor_scalar(neg_a[:], neg_a[:], -1.0, None, ALU.mult).then_inc(zero_ok, 1)
                dve.wait_ge(c_a, 2)
                nc.vector.memset(n_ms[:], 0.0).then_inc(rope_ok, 1)

            def quarter(t, h, q, parts):
                s = 4 * t + q

                def times_b(n):
                    if n == 0:
                        dve.wait_ge(ld_bc[q % 2], 16 * (half(t, q) + 1))
                    if n % 4 == 0 and q == 0:
                        dve.wait_ge(dve_du, 4 * t + n // 4 + 1)
                    wait(dve, dve_h, 16 * s + n + 1 - 4)
                    nc.vector.tensor_tensor(dbu[:, n % 4, :], du[n // 4][:], bc[q % 2][:, n % 4, 0, :], ALU.mult
                                            ).then_inc(dve_dbu, 1)

                def prepare(t, c, h):
                    dve.wait_ge(dve_dl, 4 * (t + 1))
                    wait(dve, dve_dbu, 64 * t - 16 + 4 * c + 4)
                    nc.vector.tensor_tensor(du[c][:], delta[h][:, c, :], u[h][:, c, :], ALU.mult).then_inc(dve_du, 1)
                    dve.wait_ge(ld_xt[c % 2], 16 * (2 * t + c // 2 + 1))
                    wait(dve, pe_res, 4 * t + c - 1)
                    nc.vector.scalar_tensor_tensor(resid[c % 2][:], u[h][:, c, :], skip_d[:, c:c + 1], xt_in[c % 2][:],
                                                   ALU.mult, ALU.add).then_inc(dve_res, 1)

                def add_bias():
                    g = s + 5
                    dve.wait_ge(pe_z, g + 1)
                    wait(dve, act_sp, 3 * g)
                    wait(dve, dve_dl, g)
                    nc.vector.tensor_tensor(zg[:], pro[0].rearrange("p (c t) -> p c t", c=NCH),
                                            dt_bias[:].unsqueeze(2).to_broadcast([P, NCH, GRP]),
                                            ALU.add).then_inc(dve_z, 1)

                def softplus():
                    g = s + 4
                    dve.wait_ge(act_sp, 3 * (g + 1))
                    wait(dve, act_exp, 64 * t)
                    nc.vector.scalar_tensor_tensor(delta[1 - h][:, :, GRP * q:GRP * q + GRP], zg[:], 0.0, sp_l[:],
                                                   ALU.max, ALU.add).then_inc(dve_dl, 1)

                def key_squares():
                    g = s - 5
                    wait(dve, pool_k, 5 * g)
                    for out, table, i in ((k_cos, cos, 0), (k_sin, sin, 1)):
                        nc.vector.tensor_tensor(
                            out[:].rearrange("p (a f) -> p a f", a=2),
                            table[:, bass.ds(g * HALF, HALF)].unsqueeze(1).to_broadcast([P, 2, HALF]),
                            one_ks[:, i, :].rearrange("p (a f) -> p a f", a=2), ALU.mult)
                    dve.wait_ge(act_kv, 6 * (g + 1))
                    dve.wait_ge(act_qs, H * (g + 1))
                    wait(dve, dve_ks, g)
                    nc.vector.tensor_scalar(n_ms[:], n_ss[:], 1.0 / HD, EPS, ALU.mult, ALU.add).then_inc(dve_ms, 1)

                def key_rms():
                    g, p = s - 5, (q + 1) % 2
                    wait(dve, dve_qr, g)
                    dve.wait_ge(act_rs, 2 * g + 2)
                    nc.vector.tensor_tensor(n_r2[:], n_r0[:], n_r0[:], ALU.mult).then_inc(dve_kt, 1)
                    dve.wait_ge(dve_kt, 2 * g + 1)
                    nc.vector.scalar_tensor_tensor(n_r3[:], n_r2[:], -0.5, n_ms[:], ALU.mult, ALU.mult
                                                   ).then_inc(dve_kt, 1)
                    dve.wait_ge(dve_kt, 2 * g + 2)
                    nc.vector.scalar_tensor_tensor(k_rs[:], n_r3[:, 0:G], 1.5, n_r0[:, 0:G], ALU.add, ALU.mult
                                                   ).then_inc(dve_ks, 1)
                    wait(dve, st_q[p], 16 * half(t, q - 5))
                    nc.vector.scalar_tensor_tensor(qg[p][:, D:QW], n_r3[:, G:G + H], 1.5, n_r0[:, G:G + H],
                                                   ALU.add, ALU.mult).then_inc(dve_qr, 1)

                if parts.scan:
                    times_b(0)
                for n in range(16):
                    if n == 3 and parts.fourth:
                        key_squares()
                    if n == 9:
                        if parts.second:
                            softplus()
                        if parts.fourth:
                            key_rms()
                    if n == 13 and parts.first:
                        add_bias()
                    if n in (2, 6, 10) and q == 0 and parts.scan:
                        prepare(t, n // 4 + 1, h)
                    if n == 14 and q == 3 and parts.next_scan:
                        prepare(t + 1, 0, 1 - h)
                    if parts.scan:
                        e = 16 * s + n
                        if n < 15:
                            times_b(n + 1)
                        dve.wait_ge(act_exp, e + 1)
                        dve.wait_ge(dve_dbu, e + 1)
                        wait(dve, pool_hc, e + 1 - NBUF)
                        nc.vector.tensor_tensor_scan(hid[:, n % NBUF, :], decay[:, n % NBUF, :], dbu[:, n % 4, :], 0.0,
                                                     ALU.mult, ALU.add).then_inc(dve_h, 1)
                if isinstance(t, int) and t == -2:
                    turned_ids()
                if isinstance(t, int) and t == -1:
                    if q == 0:
                        tables(0)
                        compare_ids()
                    if q == 1:
                        tables(1)
                        place_tokens()
                    if q == 2:
                        scales()
                        last_writers()

            quarters(dve, quarter)

        @block.tensor
        def _(pe):
            pe.wait_ge(s_const, 16 * NCONST)

            def turn_ids():
                pe.wait_ge(c_idx, C_IDS)
                nc.tensor.matmul(y[0][0:NSLOT, 0:B], win[0:B, :], ident[0:B, 0:B], start=True, stop=True)
                nc.tensor.matmul(y[0][0:NWC, P:2 * P], wid, ident[:], start=True, stop=True).then_inc(c_pe, 1)

            def count_later():
                pe.wait_ge(c_idx, C_BEATS)
                for c in range(NWC):
                    for c2 in range(NWC):
                        mm = nc.tensor.matmul(y[0][:, BLOCK * c:BLOCK * c + BLOCK], beats[:, c2, P * c:P * c + P],
                                              cover[:, c2, :], start=(c2 == 0), stop=(c2 == NWC - 1))
                mm.then_inc(c_pe, 1)

            def take_last():
                pe.wait_ge(c_idx, C_PLACED)
                for n in range(SC * NWC):
                    j, c = n // NWC, n % NWC
                    mm = nc.tensor.matmul(y[1][0:KC, 0:NKC * B], placed[:, c, j, :],
                                          match[:, c, :].rearrange("p (c j b) -> p j c b", c=NKC, j=SC)[:, j, :, :],
                                          start=(n == 0), stop=(n == SC * NWC - 1))
                mm.then_inc(c_pe, 1)

            def quarter(t, h, q, parts):
                s = 4 * t + q

                def project_u():
                    g, p = s + 5, (q + 1) % 2
                    pe.wait_ge(ld_xp[p], 16 * (half(t, q + 5) + 1))
                    pe.wait_ge(wpair_ok, 2 * (g + 1))
                    wait(pe, dve_z, g)
                    for j in range(NCH):
                        mm = nc.tensor.matmul(pro[0][:, GRP * j:GRP * j + GRP], x_pair[p][:, P * j:P * j + P],
                                              w_pair[p][:], start=True, stop=True)
                    mm.then_inc(pe_u, 1)

                def project_x():
                    g, k = s + 5, (q + 1) % 4
                    pe.wait_ge(act_u, g + 1)
                    wait(pe, act_dr, 2 * g)
                    for lo, n, m in ((0, 0, P), (P, 1, 32)):
                        for j in range(NCH):
                            mm = nc.tensor.matmul(pro[1][0:m, GRP * n:GRP * n + GRP], w_x[:, j, lo:lo + m],
                                                  u[h if q == 3 else 1 - h][:, j, GRP * k:GRP * k + GRP],
                                                  start=(j == 0), stop=(j == NCH - 1))
                    mm.then_inc(pe_x, 1)

                def project_dt():
                    pe.wait_ge(act_dr, 2 * (s + 6))
                    for j in range(NCH):
                        mm = nc.tensor.matmul(pro[0][:, GRP * j:GRP * j + GRP], w_dt[:, P * j:P * j + P], drg[:],
                                              start=True, stop=True)
                    mm.then_inc(pe_z, 1)

                def project_qkv(j, i):
                    g = s - 4
                    if i == 0 and q == 0:
                        pe.wait_ge(act_y, 4 * (t - 1) + j + 1)
                    if j == 0:
                        wait(pe, (act_kv, act_qs)[i], (6, H)[i] * g)
                        if isinstance(t, int) and t == 1 and q == 0:
                            pe.wait_ge(s_qkvw, 16)
                    lo = D * (1 - i)
                    mm = nc.tensor.matmul(qk[i], x1[j][:, GRP * q:GRP * q + GRP], w_qkv[:, j, lo:lo + D],
                                          start=(j == 0), stop=(j == NCH - 1))
                    if i == 1:
                        mm.then_inc(pe_q, 1)
                    elif j == NCH - 1:
                        mm.then_inc(pe_kv, 1)

                for n in range(16):
                    if parts.first:
                        if n == 0:
                            project_u()
                        if n == 4:
                            project_x()
                        if n == 8:
                            project_dt()
                    if parts.third and 5 <= n < 5 + 2 * NCH:
                        project_qkv((n - 5) // 2, (n - 5) % 2)
                    if parts.scan:
                        c, e = n // 4, 16 * s + n
                        if q == 0 and n % 4 == 0:
                            wait(pe, act_y, 4 * (t - 1) + c + 1)
                            pe.wait_ge(dve_res, 4 * t + c + 1)
                            nc.tensor.matmul(y[c], ident[:], resid[c % 2][:], start=True, stop=False
                                             ).then_inc(pe_res, 1)
                        pe.wait_ge(pool_hc, e + 1)
                        nc.tensor.matmul(y[c], ident[:], hc[:, n % NBUF, :], start=False,
                                         stop=(q == 3 and n % 4 == 3)).then_inc(pe_hc, 1)

                if isinstance(t, int) and t < 0:
                    if t == -2:
                        turn_ids()
                    if t == -1 and q == 1:
                        count_later()
                    if t == -1 and q == 2:
                        take_last()

            quarters(pe, quarter)


def attention_block(nc, A, S, W):
    with ExitStack() as ctx:
        def sb(name, shape, dt=F32):
            return ctx.enter_context(nc.sbuf_tensor(name, shape, dt))

        def sem(name):
            return ctx.enter_context(nc.semaphore(name))

        psum = ctx.enter_context(nc.psum_tensor("attn_psum", [P, 8, 512], F32))
        k_bank = [psum[:, i, 0:NKEY] for i in range(2)]
        q_bank = psum[:, 0, :]
        score = [psum[:, 2 + i, 0:NKEY] for i in range(2)]
        p_bank = [psum[0:KC, 4 + i, 0:NKC * P] for i in range(2)]
        o_bank = psum[:, 6, :].rearrange("p (c t) -> p c t", c=4)
        a_bank = psum[:, 7, :]

        ident = sb("ident2", [P, P])
        ones = sb("ones", [P, P])
        w_o = sb("w_o", [P, 4, D])
        w_r = sb("w_r", [P, D])
        b_r = sb("b_r", [P, 1])
        q_scale = sb("q_scale", [P, 2, HD])
        one_qs = sb("one_qs", [P, 2, HD])
        cos = sb("cos2", [P, NG * HALF])
        sin = sb("sin2", [P, NG * HALF])
        dist = sb("dist", [P, NKEY])
        own = sb("own", [P, P])
        before = sb("before", [P, P])
        slot_no = sb("slot_no", [P, SEL * 2])

        mask_at, idx_old, idx_new = W["mask_at"], W["idx_old"], W["idx_new"]
        old_now = [sb(f"old_now{i}", [KC, NKC], I32) for i in range(NKV)]
        new_now = [sb(f"new_now{i}", [KC, NKC], I32) for i in range(NKV)]
        kv = [sb(f"kv{i}", [KC, NKC, KV]) for i in range(NKV)]
        q_in = [sb(f"q_in{i}", [P, QW]) for i in range(2)]
        q_par = sb("q_par", [P, H, HD])
        q_n = sb("q_n", [P, H, HD])
        q_rot = sb("q_rot", [P, H, HD])
        q_cos = sb("q_cos", [P, HD])
        q_sin = sb("q_sin", [P, HD])
        q_t = [sb(f"q_t{i}", [P, 2, 2, 2, T]) for i in range(2)]
        k_t = [sb(f"k_t{i}", [P, 2, NKEY]) for i in range(2)]
        far2 = sb("far2", [P, NKEY])
        mask = [sb(f"mask{i}", [P, NKEY]) for i in range(2)]
        sm = [sb(f"sm{i}", [P, NKEY]) for i in range(4)]
        prob = [sb(f"prob{i}", [P, NKEY]) for i in range(4)]
        p_t = [sb(f"p_t{i}", [KC, NKC, P]) for i in range(2)]
        top = [sb(f"top{i}", [P, 1]) for i in range(4)]
        ntop = [sb(f"ntop{i}", [P, 1]) for i in range(4)]
        total = [sb(f"total{i}", [P, 1]) for i in range(4)]
        share = [sb(f"share{i}", [P, 1]) for i in range(4)]
        o_t = [sb(f"o_t{i}", [P, 4, P]) for i in range(2)]
        a_sb = [sb(f"a_sb{i}", [P, D]) for i in range(2)]
        r_junk = sb("r_junk", [P, D])
        r_s = sb("r_s", [P, 1])
        r_diag = sb("r_diag", [P, P])
        r_own, r_gt, r_eq, r_rank = (sb(n, [P, 1]) for n in ("r_own", "r_gt", "r_eq", "r_rank"))
        keep = [sb(f"keep{i}", [P, 2 * SEL]) for i in range(2)]
        keep_t = [sb(f"keep_t{i}", [P, P]) for i in range(2)]
        xs = [sb(f"xs{i}", [P, NCH, 2 * SEL]) for i in range(2)]

        s_c, s_late = sem("a_const"), sem("a_late")
        s_w = sem("s_w_ffn")
        scale_ok, now_ok, pool_mark = sem("scale_ok"), sem("now_ok"), sem("pool_mark2")
        sp_mark, dve_mark = sem("sp_mark2"), sem("dve_mark2")
        filled = sem("filled")
        ld_old = [sem(f"ld_old{i}") for i in range(NKV)]
        ld_kv = [sem(f"ld_kv{i}") for i in range(NKV)]
        ld_q = [sem(f"ld_q{i}") for i in range(2)]
        st_keep = [sem(f"st_keep{i}") for i in range(2)]
        st_xs = [sem(f"st_xs{i}") for i in range(2)]
        pe_q, pe_k, pe_sc, pe_pt, pe_pv = sem("pe2_q"), sem("pe_k"), sem("pe_sc"), sem("pe_pt"), sem("pe_pv")
        pe_a, pe_row, pe_xs = sem("pe_a"), sem("pe_row"), sem("pe_xs")
        act_qt, act_kt = sem("act_qt"), sem("act_kt")
        act_far, act_e, act_pt = sem("act_far"), sem("act_e"), sem("act_pt")
        act_o, act_a, act_xs = sem("act_o"), sem("act_a"), sem("act_xs")
        dve_qc, dve_qt, dve_q, dve_mask = sem("dve_qc"), sem("dve_qt"), sem("dve_q"), sem("dve_mask")
        dve_sm, dve_nt, dve_sh, dve_p = sem("dve_sm"), sem("dve_nt"), sem("dve_sh"), sem("dve_p")
        dve_rc, dve_diag, dve_keep = sem("dve_rc"), sem("dve_diag"), sem("dve_keep")

        NC, NLATE = 6, 6

        block = ctx.enter_context(nc.Block())

        class Parts:

            def __init__(self, m):
                last = NG - 1
                self.own = m is None or m <= last
                self.nxt = m is None or m < last
                self.load = m is None or m + 2 <= last
                self.prev = m is None or 1 <= m <= last + 1
                self.prev2 = m is None or 2 <= m

        def pairs(eng, pair):
            for m in range(4):
                pair(m, 0, m, m // 2, Parts(m))
            with eng.Fori(1, NG // 4 - 1) as i:
                for j in range(4):
                    pair(4 * i + j, i, j, 2 * i + j // 2, Parts(None))
            for m in range(NG - 4, NG + 2):
                pair(m, m // 4, m % 4, m // 2, Parts(m))

        def unit(u):
            return u // 4, u // 2 % 2, u % 2

        @block.sync
        def _(sp):
            for s in range(2):
                sp.dma_start(q_scale[:, s, :], A["q_scale2"][s].partition_broadcast(P)).then_inc(s_c, 16)
            for dst, src in ((cos, S["cos"]), (sin, S["sin"]), (dist, A["dist"]), (ident, A["ident"])):
                sp.dma_start(dst[:], src).then_inc(s_c, 16)

            def load_q(m, h):
                wait(sp, dve_q, 3 * (m - 2) + 1, sp_mark)
                sp.dma_start(q_in[h][:], S["q"][bass.ds(m * GRP, GRP), :]).then_inc(ld_q[h], 16)

            def pair(m, i, j, r, parts):
                h = j % 2
                if parts.load:
                    load_q(m + 2, h)
                if isinstance(m, int) and m < NCH:
                    n = NF // NCH
                    sp.wait_ge(pe_sc, 8 * m + 2)
                    sp.dma_start(W["w1"][:, m, :], A["w1"][:, m, :]).then_inc(s_w, 16)
                    sp.dma_start(W["w2"][:, n * m:n * m + n, :], A["w2"][:, n * m:n * m + n, :]).then_inc(s_w, 16)
                if parts.prev2:
                    store(m - 2, r - 1, h)

            def store(m, i, h):
                wait(sp, act_xs, 2 * (m + 1), sp_mark)
                sp.dma_start(S["keep"][bass.ds(2 * i + h, 1)].rearrange("o s t -> (o s) t"),
                             keep_t[h][64 * h:64 * h + 64, :]).then_inc(st_keep[h], 16)
                sp.dma_start(S["xsp"][:, :, bass.ds(m * 2 * SEL, 2 * SEL)], xs[h][:]).then_inc(st_xs[h], 16)

            load_q(0, 0)
            for dst, src in ((own, A["own"]), (before, A["before"]), (slot_no, A["slot_no"]), (w_o, A["w_o"])):
                sp.dma_start(dst[:], src).then_inc(s_late, 16)
            sp.dma_start(w_r[:], A["w_r"].partition_broadcast(P)).then_inc(s_late, 16)
            sp.dma_start(b_r[:], A["b_r"].partition_broadcast(P)).then_inc(s_late, 16)
            load_q(1, 1)
            pairs(sp, pair)
            sp.wait_ge(s_w, 32 * NCH)
            for h in range(2):
                sp.wait_ge(st_keep[h], 16 * NG // 2)
                sp.wait_ge(st_xs[h], 16 * NG // 2)

        @block.gpsimd
        def _(pool):
            nc.gpsimd.memset(ones[:], 1.0).then_inc(filled, 1)

            def gather_old(b, s):
                wait(pool, pe_pv, 4 * (b + 1 - NKV), pool_mark)
                pool.tensor_copy(old_now[s][:], idx_old[:, :, bass.ds(b, 1)].rearrange("p c o -> p (c o)")
                                 ).then_inc(now_ok, 1)
                pool.tensor_copy(new_now[s][:], idx_new[:, :, bass.ds(b, 1)].rearrange("p c o -> p (c o)")
                                 ).then_inc(now_ok, 1)
                wait(pool, now_ok, 2 * (b + 1), pool_mark)
                for c in range(NKC):
                    pool.indirect_dma_start(kv[s][:, c, :], None, A["kv_rows"],
                                            bass.IndirectOffsetOnAxis(ap=old_now[s][:, c:c + 1], axis=0)
                                            ).then_inc(ld_old[s], 16)

            def gather_new(i, s):
                wait(pool, ld_old[s], 16 * NKC * (i + 1), pool_mark)
                for c in range(NKC):
                    pool.indirect_dma_start(kv[s][:, c, :], None, S["kv_new"],
                                            bass.IndirectOffsetOnAxis(ap=new_now[s][:, c:c + 1], axis=0),
                                            bounds_check=NTOK - 1, oob_is_err=False).then_inc(ld_kv[s], 16)

            def gather(i, s):
                gather_old(NKV * i + s, s)
                if s:
                    gather_new(i, s - 1)
                elif not isinstance(i, int):
                    gather_new(i - 1, NKV - 1)

            for s in range(NKV):
                gather(0, s)
            with pool.Fori(1, B // NKV) as i:
                for s in range(NKV):
                    gather(i, s)
            gather_new(B // NKV - 1, NKV - 1)

        @block.scalar
        def _(act):
            def take_q(m, h):
                act.wait_ge(pe_q, m + 1)
                wait(act, pe_sc, 8 * (m - 1))
                for gp in range(2):
                    nc.scalar.copy(q_t[h][:, gp, :, :, :].rearrange("p b j t -> p j b t"),
                                   q_bank[:, 2 * P * gp:2 * P * gp + 2 * P].rearrange("p (j b t) -> p j b t", j=2, b=2)
                                   ).then_inc(act_qt, 1)

            def take_k(m, b):
                act.wait_ge(pe_k, 2 * m + b + 1)
                wait(act, pe_sc, 8 * m - 4 + 4 * b)
                for gp in range(2):
                    nc.scalar.copy(k_t[b][:, gp, :], k_bank[gp]).then_inc(act_kt, 1)

            def distance(m, b):
                wait(act, dve_mask, 2 * m + b)
                nc.scalar.activation(far2[:], dist[:], ACT.Square, bias=mask_at[:, bass.ds(2 * m + b + 1, 1)]
                                     ).then_inc(act_far, 1)

            def exps(m, u):
                act.wait_ge(dve_nt, 8 * m + u + 1)
                wait(act, pe_pt, 8 * m + u - 3)
                nc.scalar.activation(prob[u % 4][:], sm[u % 4][:], ACT.Exp, bias=ntop[u % 4][:], scale=SCALE,
                                     accum_out=total[u % 4][:]).then_inc(act_e, 1)

            def take_p(m, u):
                act.wait_ge(pe_pt, 8 * m + u + 1)
                wait(act, pe_pv, 8 * m + u - 1)
                nc.scalar.copy(p_t[u % 2][:].rearrange("p c t -> p (c t)"), p_bank[u % 2]).then_inc(act_pt, 1)

            def take_rows(m, i, h):
                act.wait_ge(pe_xs, m + 1)
                wait(act, st_keep[h], 16 * i)
                wait(act, st_xs[h], 16 * i)
                rows = slice(64 * h, 64 * h + 64)
                nc.scalar.copy(keep_t[h][rows, :], a_bank[rows, P:2 * P]).then_inc(act_xs, 1)
                nc.scalar.copy(xs[h][:].rearrange("p c s -> p (c s)"), a_bank[:, 2 * P:]).then_inc(act_xs, 1)

            def take_o(m, h):
                act.wait_ge(pe_pv, 8 * m + 8)
                wait(act, pe_a, m - 1)
                nc.scalar.copy(o_t[h][:], o_bank).then_inc(act_o, 1)

            def take_a(m, h):
                act.wait_ge(pe_a, m + 1)
                wait(act, pe_xs, m - 1)
                nc.scalar.copy(a_sb[h][:], a_bank).then_inc(act_a, 1)

            def pair(m, i, j, r, parts):
                h = j % 2
                for k in range(8):
                    if k < 6 and parts.own:
                        exps(m, k + 2)
                    if k >= 6 and parts.nxt:
                        exps(m + 1, k - 6)
                    if parts.nxt:
                        if k == 3:
                            take_k(m + 1, 0)
                        if k == 5:
                            take_q(m + 1, 1 - h)
                        if k == 7:
                            take_k(m + 1, 1)
                    if parts.own:
                        take_p(m, k)
                    if k == 0 and parts.prev:
                        take_o(m - 1, 1 - h)
                    if k == 3 and parts.prev2:
                        take_rows(m - 2, r - 1, h)
                    if k == 6 and parts.prev:
                        take_a(m - 1, 1 - h)
                    if k in (3, 6) and parts.nxt:
                        distance(m + 1, k // 6)

            act.wait_ge(s_c, 16 * NC)
            distance(0, 0)
            distance(0, 1)
            take_k(0, 0)
            take_q(0, 0)
            take_k(0, 1)
            exps(0, 0)
            exps(0, 1)
            pairs(act, pair)

        @block.vector
        def _(dve):
            dve.wait_ge(s_c, 16 * NC)
            v = nc.vector
            v.tensor_scalar(one_qs[:, 0, :], q_scale[:, 0, :], 1.0, None, ALU.add).then_inc(scale_ok, 1)
            v.tensor_scalar(one_qs[:, 1, 0:HALF], q_scale[:, 1, 0:HALF], -1.0, -1.0, ALU.mult, ALU.add
                            ).then_inc(scale_ok, 1)
            v.tensor_scalar(one_qs[:, 1, HALF:HD], q_scale[:, 1, HALF:HD], 1.0, None, ALU.add).then_inc(scale_ok, 1)
            dve.wait_ge(scale_ok, 3)

            def scale_queries(m, i, h):
                wait(dve, dve_q, 3 * m)
                for out, table_, j in ((q_cos, cos, 0), (q_sin, sin, 1)):
                    v.tensor_tensor(out[:].rearrange("p (a f) -> p a f", a=2),
                                    table_[:, bass.ds(m * HALF, HALF)].unsqueeze(1).to_broadcast([P, 2, HALF]),
                                    one_qs[:, j, :].rearrange("p (a f) -> p a f", a=2), ALU.mult).then_inc(dve_qt, 1)
                dve.wait_ge(ld_q[h], 16 * (i + 1))
                v.tensor_tensor(q_n[:], q_in[h][:, 0:D].rearrange("p (h d) -> p h d", h=H),
                                q_in[h][:, D:QW].unsqueeze(2).to_broadcast([P, H, HD]), ALU.mult).then_inc(dve_q, 1)

            def cross_queries(m):
                dve.wait_ge(dve_q, 3 * m + 1)
                dve.wait_ge(dve_qt, 2 * m + 2)
                wait(dve, pe_q, m)
                for j in range(2):
                    v.tensor_tensor(q_rot[:, :, HALF * j:HALF * j + HALF],
                                    q_n[:, :, HALF * (1 - j):HALF * (1 - j) + HALF],
                                    q_sin[:, HALF * j:HALF * j + HALF].unsqueeze(1)
                                    .to_broadcast([P, H, HALF]), ALU.mult).then_inc(dve_qc, 1)

            def straight_queries(m):
                v.tensor_tensor(q_par[:], q_n[:], q_cos[:].unsqueeze(1).to_broadcast([P, H, HD]), ALU.mult
                                ).then_inc(dve_q, 1)

            def add_queries(m):
                dve.wait_ge(dve_q, 3 * m + 2)
                dve.wait_ge(dve_qc, 2 * m + 2)
                v.tensor_tensor(q_rot[:], q_rot[:], q_par[:], ALU.add).then_inc(dve_q, 1)

            def masks(m, b):
                dve.wait_ge(act_far, 2 * m + b + 1)
                v.tensor_scalar(mask[b][:], far2[:], float(WINDOW // 2) ** 2, NEG, ALU.is_gt, ALU.mult
                                ).then_inc(dve_mask, 1)

            def maxima(m, u):
                b = u // 4
                wait(dve, act_e, 8 * m + u - 3)
                dve.wait_ge(dve_mask, 2 * m + b + 1)
                wait(dve, pe_sc, 8 * m + u + 1, dve_mark)
                v.tensor_tensor_reduce(sm[u % 4][:], score[u % 2], mask[b][:], 1.0, NEG * 4, ALU.add, ALU.max,
                                       top[u % 4][:]).then_inc(dve_sm, 1)
                dve.wait_ge(dve_sm, 8 * m + u + 1)
                v.tensor_scalar(ntop[u % 4][:], top[u % 4][:], -SCALE, None, ALU.mult).then_inc(dve_nt, 1)

            def norms(m, u):
                dve.wait_ge(act_e, 8 * m + u + 1)
                v.reciprocal(share[u % 4][:], total[u % 4][:]).then_inc(dve_sh, 1)
                dve.wait_ge(dve_sh, 8 * m + u + 1)
                v.tensor_scalar(prob[u % 4][:], prob[u % 4][:], share[u % 4][:], None, ALU.mult).then_inc(dve_p, 1)

            def router_score(m, h):
                if isinstance(m, int) and m == 0:
                    dve.wait_ge(s_late, 16 * NLATE)
                dve.wait_ge(act_a, m + 1)
                v.tensor_tensor_reduce(r_junk[:], a_sb[h][:], w_r[:], 1.0, 0.0, ALU.mult, ALU.add, r_s[:]
                                       ).then_inc(dve_rc, 1)
                dve.wait_ge(dve_rc, 6 * m + 1)
                v.tensor_tensor(r_s[:], r_s[:], b_r[:], ALU.add).then_inc(dve_rc, 1)
                dve.wait_ge(dve_rc, 6 * m + 2)
                v.tensor_scalar(r_diag[:], ident[:], r_s[:], None, ALU.mult).then_inc(dve_diag, 1)

            def router_keep(m, h):
                row = a_bank[:, 0:P]
                dve.wait_ge(pe_row, m + 1)
                v.tensor_tensor_reduce(r_junk[:, 0:P], row, ident[:], 1.0, 0.0, ALU.mult, ALU.add, r_own[:]
                                       ).then_inc(dve_rc, 1)
                dve.wait_ge(dve_rc, 6 * m + 3)
                v.scalar_tensor_tensor(r_junk[:, P:2 * P], row, r_own[:], own[:], ALU.is_gt, ALU.mult,
                                       accum_out=r_gt[:]).then_inc(dve_rc, 1)
                v.scalar_tensor_tensor(r_junk[:, 2 * P:3 * P], row, r_own[:], before[:], ALU.is_equal, ALU.mult,
                                       accum_out=r_eq[:]).then_inc(dve_rc, 1)
                dve.wait_ge(dve_rc, 6 * m + 5)
                v.tensor_tensor(r_rank[:], r_gt[:], r_eq[:], ALU.add).then_inc(dve_rc, 1)
                dve.wait_ge(dve_rc, 6 * m + 6)
                v.tensor_scalar(keep[h][:], slot_no[:], r_rank[:], None, ALU.is_equal).then_inc(dve_keep, 1)

            def pair(m, i, j, r, parts):
                h = j % 2
                for k in range(8):
                    if k < 6 and parts.own:
                        maxima(m, k + 2)
                    if k >= 6 and parts.nxt:
                        maxima(m + 1, k - 6)
                    if k < 7 and parts.own:
                        norms(m, k + 1)
                    if k == 7 and parts.nxt:
                        norms(m + 1, 0)
                    if k == 1 and parts.prev2:
                        router_keep(m - 2, h)
                    if parts.nxt:
                        if k == 0:
                            scale_queries(m + 1, r + h, 1 - h)
                        if k == 1:
                            cross_queries(m + 1)
                        if k == 2:
                            straight_queries(m + 1)
                        if k == 3:
                            add_queries(m + 1)
                        if k in (4, 7):
                            masks(m + 1, k // 7)
                    if k == 7 and parts.prev:
                        router_score(m - 1, 1 - h)

            scale_queries(0, 0, 0)
            cross_queries(0)
            straight_queries(0)
            add_queries(0)
            masks(0, 0)
            masks(0, 1)
            maxima(0, 0)
            maxima(0, 1)
            norms(0, 0)
            pairs(dve, pair)

        @block.tensor
        def _(pe):
            pe.wait_ge(s_c, 16 * NC)
            def turn_q(m, h):
                pe.wait_ge(dve_q, 3 * (m + 1))
                wait(pe, act_kt, 2 * (2 * m + 1))
                qv = q_rot[:].rearrange("p h d -> p (h d)")
                for c in range(4):
                    mm = nc.tensor.transpose(q_bank[:, P * c:P * c + P], qv[:, P * c:P * c + P], ident[:])
                mm.then_inc(pe_q, 1)

            def turn_k(m, i, j, b):
                s = 2 * j + b
                pe.wait_ge(ld_kv[s], 16 * NKC * (i + 1))
                wait(pe, act_kt, 2 * (2 * m + b))
                if b == 1:
                    pe.wait_ge(act_qt, 2 * (m + 1))
                for gp in range(2):
                    for c in range(NKC):
                        mm = nc.tensor.transpose(k_bank[gp][:, KC * c:KC * c + KC],
                                                 kv[s][:, c, P * gp:P * gp + P], ident[0:KC, 0:KC])
                mm.then_inc(pe_k, 1)

            def scores(m, h, u):
                b, gp, gq = unit(u)
                rows = slice(64 * gq, 64 * gq + 64)
                if u == 0:
                    pe.wait_ge(act_qt, 2 * (m + 1))
                if u % 4 == 0:
                    pe.wait_ge(act_kt, 2 * (2 * m + b + 1))
                wait(pe, dve_sm, 8 * m + u - 1)
                nc.tensor.matmul(score[u % 2], q_t[h][rows, gp, b, :, :].rearrange("p j t -> p (j t)"),
                                 k_t[b][rows, gp, :], start=True, stop=True).then_inc(pe_sc, 1)

            def turn_p(m, u):
                pe.wait_ge(dve_p, 8 * m + u + 1)
                wait(pe, act_pt, 8 * m + u - 1)
                for c in range(NKC):
                    mm = nc.tensor.transpose(p_bank[u % 2][:, P * c:P * c + P], prob[u % 4][:, KC * c:KC * c + KC], ident[:])
                mm.then_inc(pe_pt, 1)

            def values(m, j, u):
                b, gp, gq = unit(u)
                g = 2 * gp + gq
                pe.wait_ge(act_pt, 8 * m + u + 1)
                if u == 0:
                    wait(pe, act_o, m)
                for c in range(NKC):
                    mm = nc.tensor.matmul(o_bank[64 * gq:64 * gq + 64, 2 * gp:2 * gp + 2, T * b:T * b + T],
                                          kv[2 * j + b][:, c, G * HD + HD * g:G * HD + HD * g + HD],
                                          p_t[u % 2][:, c, :].rearrange("p (j t) -> p j t", j=2),
                                          start=(c == 0), stop=(c == NKC - 1))
                mm.then_inc(pe_pv, 1)

            def project(m, h, part):
                if isinstance(m, int) and m == 0:
                    pe.wait_ge(s_late, 16 * NLATE)
                if part == 0:
                    pe.wait_ge(act_o, m + 1)
                    wait(pe, act_xs, 2 * m)
                for c in (2 * part, 2 * part + 1):
                    mm = nc.tensor.matmul(a_bank, o_t[h][:, c, :], w_o[:, c, :], start=(c == 0), stop=(c == 3))
                if part:
                    mm.then_inc(pe_a, 1)

            def router_row(m):
                pe.wait_ge(act_a, m + 1)
                pe.wait_ge(dve_diag, m + 1)
                nc.tensor.matmul(a_bank[:, 0:P], ones[:], r_diag[:], start=True, stop=True).then_inc(pe_row, 1)

            def router_take(m, h):
                pe.wait_ge(dve_keep, m + 1)
                nc.tensor.matmul(a_bank[64 * h:64 * h + 64, P:2 * P], keep[h][:], ident[:], start=True, stop=True)
                for c in range(NCH):
                    mm = nc.tensor.matmul(a_bank[:, 2 * P + 2 * SEL * c:2 * P + 2 * SEL * c + 2 * SEL],
                                          a_sb[h][:, P * c:P * c + P], keep[h][:], start=True, stop=True)
                mm.then_inc(pe_xs, 1)

            def pair(m, i, j, r, parts):
                h = j % 2
                i1, j1 = (i, j + 1) if j < 3 else (i + 1, 0)
                for k in range(8):
                    if k < 6 and parts.own:
                        scores(m, h, k + 2)
                    if k >= 6 and parts.nxt:
                        scores(m + 1, 1 - h, k - 6)
                    if parts.nxt:
                        if k == 2:
                            turn_k(m + 1, i1, j1, 0)
                        if k == 4:
                            turn_q(m + 1, 1 - h)
                        if k == 6:
                            turn_k(m + 1, i1, j1, 1)
                    if parts.own:
                        turn_p(m, k)
                    if k > 0 and parts.own:
                        values(m, j, k - 1)
                    if k == 0 and parts.prev:
                        values(m - 1, (j - 1) % 4, 7)
                    if k in (4, 5) and parts.prev:
                        project(m - 1, 1 - h, k - 4)
                    if k == 0 and parts.prev2:
                        router_row(m - 2)
                    if k == 2 and parts.prev2:
                        router_take(m - 2, h)

            pe.wait_ge(filled, 1)
            turn_k(0, 0, 0, 0)
            turn_q(0, 0)
            turn_k(0, 0, 0, 1)
            scores(0, 0, 0)
            scores(0, 0, 1)
            pairs(pe, pair)


def ffn_block(nc, A, S, W, out):
    NS = NG * 2 * SEL // TILE
    NTT = TILE // P
    with ExitStack() as ctx:
        def sb(name, shape, dt=F32):
            return ctx.enter_context(nc.sbuf_tensor(name, shape, dt))

        def sem(name):
            return ctx.enter_context(nc.semaphore(name))

        psum = ctx.enter_context(nc.psum_tensor("ffn_psum", [P, 8, 512], F32))
        h_bank = [psum[:, i, :] for i in range(3)]
        y_bank = [psum[:, 3 + i, :] for i in range(2)]
        s_bank = [psum[:, 5 + i, :] for i in range(3)]

        w1, w2 = W["w1"], W["w2"]
        b1 = sb("b1", [P, NF])
        b2 = sb("b2", [P, D])
        xs = sb("xs_in", [P, NCH, TILE])
        hid = sb("ffn_hid", [P, NF, TILE])
        y_sb = [sb(f"y_sb{i}", [P, D]) for i in range(2)]
        keep_t = [sb(f"keep_in{i}", [P, P]) for i in range(2)]
        x1 = [sb(f"x1_in{i}", [P, NCH, P]) for i in range(2)]
        res = [sb(f"res{i}", [P, NCH, P]) for i in range(2)]

        ld_b1, ld_b2, ld_xs = sem("ld_b1"), sem("ld_b2"), sem("ld_xs")
        ld_keep = [sem(f"ld_keep{i}") for i in range(2)]
        ld_x1 = [sem(f"ld2_x1{i}") for i in range(2)]
        st_res = [sem(f"st_res{i}") for i in range(2)]
        pe_h, pe_y, pe_s = sem("pe_h"), sem("pe2_y"), sem("pe_s")
        act_h, dve_y, dve_r, sp_mark = sem("act_h"), sem("dve_y"), sem("dve_r"), sem("sp_mark3")

        block = ctx.enter_context(nc.Block())

        @block.sync
        def _(sp):
            sp.dma_start(xs[:], S["xsp"][:, :, 0:TILE]).then_inc(ld_xs, 16)
            sp.dma_start(b1[:], A["b1"]).then_inc(ld_b1, 16)
            sp.dma_start(b2[:], A["b2"].partition_broadcast(P)).then_inc(ld_b2, 16)

            def loads(n, p):
                wait(sp, pe_s, 2 * (n - 1), sp_mark)
                sp.dma_start(keep_t[p][:], S["keep"][bass.ds(2 * n, 2)].rearrange("j s t -> (j s) t")
                             ).then_inc(ld_keep[p], 16)

            def tile(s, tt, more):
                n, p = NTT * s + tt, tt % 2
                loads(n, p)
                if more and tt == 0:
                    wait(sp, pe_h, NF * (s + 1), sp_mark)
                    sp.dma_start(xs[:], S["xsp"][:, :, bass.ds((s + 1) * TILE, TILE)]).then_inc(ld_xs, 16)
                for j in range(2):
                    wait(sp, dve_r, 2 * n + j - 1, sp_mark)
                    sp.dma_start(x1[j][:], S["x1p"][:, :, bass.ds((2 * n + j) * GRP, GRP)]).then_inc(ld_x1[j], 16)
                for j in range(2):
                    wait(sp, dve_r, 2 * n + j + 1, sp_mark)
                    sp.dma_start(out.rearrange("c p t -> p c t")[:, :, bass.ds((2 * n + j) * GRP, GRP)],
                                 res[j][:]).then_inc(st_res[j], 16)

            for tt in range(NTT):
                tile(0, tt, True)
            with sp.Fori(1, NS - 1) as s:
                for tt in range(NTT):
                    tile(s, tt, True)
            for tt in range(NTT):
                tile(NS - 1, tt, False)
            for j in range(2):
                sp.wait_ge(st_res[j], 16 * NG // 2)

        @block.scalar
        def _(act):
            act.wait_ge(ld_b1, 16)

            def tile(s):
                for f in range(NF):
                    k = NF * s + f
                    act.wait_ge(pe_h, k + 1)
                    if f == 0:
                        wait(act, pe_y, NTT * s)
                    nc.scalar.activation(hid[:, f, :], h_bank[f % 2], ACT.Gelu_apprx_tanh, bias=b1[:, f:f + 1]
                                         ).then_inc(act_h, 1)

            tile(0)
            with act.Fori(1, NS) as s:
                tile(s)

        @block.vector
        def _(dve):
            dve.wait_ge(ld_b2, 16)

            def tile(s, tt):
                n, p = NTT * s + tt, tt % 2
                dve.wait_ge(pe_y, n + 1)
                wait(dve, pe_s, 2 * (n - 1))
                nc.vector.tensor_tensor(y_sb[p][:], y_bank[p], b2[:], ALU.add).then_inc(dve_y, 1)
                for j in range(2):
                    dve.wait_ge(pe_s, 2 * n + j + 1)
                    dve.wait_ge(ld_x1[j], 16 * (n + 1))
                    wait(dve, st_res[j], 16 * n)
                    nc.vector.tensor_tensor(res[j][:].rearrange("p c t -> p (c t)"), s_bank[j],
                                            x1[j][:].rearrange("p c t -> p (c t)"), ALU.add).then_inc(dve_r, 1)

            for tt in range(NTT):
                tile(0, tt)
            with dve.Fori(1, NS) as s:
                for tt in range(NTT):
                    tile(s, tt)

        @block.tensor
        def _(pe):
            def tile(s):
                pe.wait_ge(ld_xs, 16 * (s + 1))
                for f in range(NF):
                    k = NF * s + f
                    wait(pe, act_h, k - 1)
                    for c in range(NCH):
                        mm = nc.tensor.matmul(h_bank[f % 2], w1[:, c, P * f:P * f + P], xs[:, c, :],
                                              start=(c == 0), stop=(c == NCH - 1))
                    mm.then_inc(pe_h, 1)
                for tt in range(NTT + 1):
                    if tt < NTT:
                        n, p = NTT * s + tt, tt % 2
                        wait(pe, dve_y, n - 1)
                        for f in range(NF):
                            if tt == 0:
                                pe.wait_ge(act_h, NF * s + f + 1)
                            mm = nc.tensor.matmul(y_bank[p], hid[:, f, P * tt:P * tt + P], w2[:, f, :],
                                                  start=(f == 0), stop=(f == NF - 1))
                        mm.then_inc(pe_y, 1)
                    if tt > 0:
                        scatter(NTT * s + tt - 1, (tt - 1) % 2, 2 * s + (tt - 1) // 2)

            def scatter(n, p, uses):
                pe.wait_ge(dve_y, n + 1)
                pe.wait_ge(ld_keep[p], 16 * (uses + 1))
                for j in range(2):
                    rows = slice(64 * j, 64 * j + 64)
                    wait(pe, dve_r, 2 * n + j - 1)
                    for c in range(NCH):
                        mm = nc.tensor.matmul(s_bank[j][:, P * c:P * c + P], y_sb[p][rows, P * c:P * c + P],
                                              keep_t[p][rows, :], start=True, stop=True)
                    mm.then_inc(pe_s, 1)

            tile(0)
            with pe.Fori(1, NS) as s:
                tile(s)


def program(nc, A, out):
    S = {}
    S["x1"] = nc.dram_tensor("x1_scratch", [NCH, P, NTOK], F32).ap()
    S["x1p"] = S["x1"].rearrange("c p t -> p c t")
    S["bc"] = nc.dram_tensor("bc_scratch", [2 * NST, NTOK], F32).ap()
    S["q"] = nc.dram_tensor("q_scratch", [NTOK, QW], F32).ap()
    S["kv_new"] = nc.dram_tensor("kv_scratch", [NTOK, KV], F32).ap()
    S["cos"] = nc.dram_tensor("cos_scratch", [P, NG * HALF], F32).ap()
    S["sin"] = nc.dram_tensor("sin_scratch", [P, NG * HALF], F32).ap()
    S["win"] = nc.dram_tensor("win_scratch", [NSLOT, B], F32).ap()
    S["wid"] = nc.dram_tensor("wid_scratch", [NWC, P], F32).ap()
    S["keep"] = nc.dram_tensor("keep_scratch", [NG, 2 * SEL, P], F32).ap()
    S["xs"] = nc.dram_tensor("xs_scratch", [NCH, P, NG * 2 * SEL], F32).ap()
    S["xsp"] = S["xs"].rearrange("c p t -> p c t")
    with ExitStack() as ctx:
        W = {"mask_at": ctx.enter_context(nc.sbuf_tensor("mask_at", [P, 1 + B], F32)),
             "idx_old": ctx.enter_context(nc.sbuf_tensor("idx_old", [KC, NKC, B], I32)),
             "idx_new": ctx.enter_context(nc.sbuf_tensor("idx_new", [KC, NKC, B], I32))}
        scan_block(nc, A, S, W)
        W["w1"] = ctx.enter_context(nc.sbuf_tensor("w1", [P, NCH, DF], F32))
        W["w2"] = ctx.enter_context(nc.sbuf_tensor("w2", [P, NF, D], F32))
        attention_block(nc, A, S, W)
        ffn_block(nc, A, S, W, out)


def layouts(inp):
    f = np.ascontiguousarray
    a = {}
    x = inp["x"]
    a["x_pairs"] = f(x.reshape(NG, P, D))
    a["x_t"] = f(x.reshape(NTOK, NCH, P).transpose(1, 2, 0))
    a["w_cond"] = f(inp["L0_cond_weights"].reshape(-1, HD))
    a["cond"] = f(inp["itok_B_1_198"].reshape(NG, 2).T)
    a["lens_pair"] = f(inp["itok_B_37_3939"].reshape(NG, 2).T)
    a["a_log"] = f(inp["L0_attn_A_log"].reshape(NCH, P, NST).transpose(1, 0, 2).reshape(P, -1))
    a["skip_d"] = f(inp["L0_attn_D"].reshape(NCH, P).T)
    a["dt_bias"] = f(inp["L0_attn_dt_proj_b"].reshape(NCH, P).T)
    wx = inp["L0_attn_x_proj_w"]
    wx = np.concatenate([wx[:P], wx[P:].reshape(2, NST, D).transpose(1, 0, 2).reshape(2 * NST, D)])
    a["w_x"] = f(wx.T.reshape(NCH, P, 160).transpose(1, 0, 2))
    a["w_dt"] = f(inp["L0_attn_dt_proj_w"].T)
    wq = inp["L0_cond2_Wq"].reshape(2, 2, 2, HD, D).transpose(0, 2, 1, 3, 4).reshape(D, D)
    w = np.concatenate([wq, inp["L0_cond2_Wk"], inp["L0_cond2_Wv"]])
    a["w_qkv"] = f(w.T.reshape(NCH, P, 1024).transpose(1, 0, 2))
    ks = inp["L0_cond2_k_norm_scale"]
    a["k_scale2"] = f(np.stack([ks, np.concatenate([ks[HALF:], ks[:HALF]])]))
    a["ident"] = np.eye(P, dtype=np.float32)
    a["part"] = f(np.stack([np.arange(P) % T, np.zeros(P)], 1).astype(np.float32))
    qs = inp["L0_cond2_q_norm_scale"]
    a["q_scale2"] = f(np.stack([qs, np.concatenate([qs[HALF:], qs[:HALF]])]))
    wo = inp["L0_cond2_Wo"].T.reshape(2, 2, 2, HD, D).transpose(0, 2, 1, 3, 4).reshape(NCH, P, D)
    a["w_o"] = f(wo.transpose(1, 0, 2))
    kb = inp["L0_cond2_k_blocks"].transpose(0, 2, 1, 3).reshape(NROW, G * HD)
    vb = inp["L0_cond2_v_blocks"].transpose(0, 2, 1, 3).reshape(NROW, G * HD)
    a["kv_rows"] = f(np.concatenate([kb, vb], axis=1))
    a["table"] = f(inp["itok_Bx257_0_4111"])
    a["lens"] = f(inp["itok_B_37_3939"].reshape(B, 1))
    a["lens_row"] = f(inp["itok_B_37_3939"])
    a["w_r"] = f(inp["L0_ffn_w_r"])
    a["b_r"] = f(inp["L0_ffn_b_r"].reshape(1))
    a["w1"] = f(inp["L0_ffn_w1"].reshape(NCH, P, DF).transpose(1, 0, 2))
    a["w2"] = f(inp["L0_ffn_w2"].reshape(NF, P, D).transpose(1, 0, 2))
    a["b1"] = f(inp["L0_ffn_b1"].reshape(NF, P).T)
    a["b2"] = f(inp["L0_ffn_b2"])

    p = np.arange(P)
    half, seq = p // T, p % T
    slot = 2 * np.arange(NWC) + half[:, None]
    a["ids"] = f(np.broadcast_to(np.arange(NBLK, dtype=np.float32), (P, NBLK)))
    a["w_slot0"] = f(slot.astype(np.float32))
    a["tau0"] = f((BLOCK * slot[:, :, None] + np.arange(BLOCK)).astype(np.float32))
    a["tok0"] = f((T * seq + 1).astype(np.float32)[:, None])
    a["off_in"] = f((p % BLOCK).astype(np.float32)[:, None])
    order = seq[:, None] * 8 + slot
    a["later"] = f((order[:, :, None] > order.T.reshape(-1)).astype(np.float32))
    a["dist"] = f((np.arange(NKEY) - seq[:, None]).astype(np.float32))
    same = half[:, None] == half
    a["own"] = f(same.astype(np.float32))
    a["before"] = f((same & (p < p[:, None])).astype(np.float32))
    at = np.arange(2 * SEL)
    a["slot_no"] = f(np.where(at // SEL == half[:, None], at % SEL, -1).astype(np.float32))
    a["inv_freq"] = (1.0 / np.float32(10000.0) ** (np.arange(HALF, dtype=np.float32) / HALF)).astype(np.float32)
    return a


def kernel(**inputs):
    import concourse.bacc as _bacc
    from concourse.bass_utils import run_bass_kernel_spmd as _run

    nc = _bacc.Bacc("TRN2", target_bir_lowering=False, num_devices=1)
    arrays = layouts({k: np.asarray(v) for k, v in inputs.items()})
    aps = {n: nc.dram_tensor(f"in_{n}", v.shape, mybir.dt.from_np(v.dtype), kind="ExternalInput").ap()
           for n, v in arrays.items()}
    out = nc.dram_tensor("out_t", (NCH, P, NTOK), F32, kind="ExternalOutput").ap()
    program(nc, aps, out)
    r = _run(nc, [{f"in_{n}": v for n, v in arrays.items()}], core_ids=[0])
    return np.ascontiguousarray(r.results[0]["out_t"].transpose(2, 0, 1).reshape(B, T, D))
```
